# Optimizing a Trainium2 kernel written in Bass

```python
import numpy as np
import jax
import jax.numpy as jnp

def _softmax(x, axis=-1):
    return jax.nn.softmax(x, axis=axis)

def _gelu(x):
    return jax.nn.gelu(x, approximate=True)

def _silu(x):
    return jax.nn.silu(x)

def _sigmoid(x):
    return jax.nn.sigmoid(x)

def _layernorm(x, axis=-1, eps=1e-05):
    m = jnp.mean(x, axis=axis, keepdims=True)
    v = jnp.var(x, axis=axis, keepdims=True)
    return (x - m) / jnp.sqrt(v + eps)

def _scatter_add(tgt, idx, src, axis=0):
    return tgt.at[idx].add(src)

def _segment_sum(src, seg, n):
    return jax.ops.segment_sum(src, seg, n)
kernel_name = 'mk_xattn_ffn_d2_seqx_r4_4ac187'

def setup_inputs(seed: int=0):
    np.random.seed(seed)
    _w = jnp.asarray

    def _rec_inputs():
        import jax
        import jax.numpy as jnp
        _rk = jax.random.key(seed)
        x = -0.0001033 + 0.9999 * jax.random.normal(jax.random.fold_in(_rk, 1), (4, 1024, 256), jnp.float32)
        _lenS = 1024 - jax.random.randint(jax.random.fold_in(_rk, 7), (4,), 0, max(1, 1024 // 4) + 1, jnp.int32)
        _lenS2 = 64 - jax.random.randint(jax.random.fold_in(_rk, 8), (4,), 0, max(1, 64 // 4) + 1, jnp.int32)
        _ctx_1024P = jax.random.normal(jax.random.fold_in(_rk, 11), (4, 16, 256), jnp.float32)
        _ctx_1024c = jax.random.dirichlet(jax.random.fold_in(_rk, 511), 0.3 * jnp.ones((16,), jnp.float32), (4, 64))
        _ctx_1024t = jnp.einsum('bsk,bkd->bsd', _ctx_1024c, _ctx_1024P)
        _ctx_1024t = _ctx_1024t * jax.lax.rsqrt(jnp.mean(jnp.square(_ctx_1024t)) + 1e-12) * 0.953939
        ctx_1024 = -0.000292821 + 1.00034 * (_ctx_1024t + 0.3 * jax.random.normal(jax.random.fold_in(_rk, 611), (4, 64, 256), jnp.float32))
        return (x, ctx_1024)
    x, ctx_1024 = _rec_inputs()

    def _L0_xattn_setup():
        import jax, jax.numpy as jnp
        import numpy as np
        from jax import lax
        B, T, F = (32, 128, 256)
        CONV_UNITS = 512
        SHORT_UNITS = 512
        RATE = 4
        key = jax.random.key(seed)
        k1, k2, k3 = jax.random.split(key, 3)
        inputs = jax.random.normal(k1, (B, T, F), dtype=jnp.float32)
        memory = jax.random.normal(k2, (B, CONV_UNITS + SHORT_UNITS, F), dtype=jnp.float32)
        conv_w = jax.random.normal(k3, (RATE, F, F), dtype=jnp.float32) * 0.02
        conv_b = jnp.zeros((F,), dtype=jnp.float32)
        return {'inputs': inputs, 'memory': memory, 'conv_w': conv_w, 'conv_b': conv_b, 'conv_units': CONV_UNITS, 'short_units': SHORT_UNITS, 'rate': RATE}
    _L0_xattn_all = _L0_xattn_setup()
    _L0_xattn_in = {k: v for k, v in _L0_xattn_all.items() if k in ('conv_w', 'conv_b')}
    del _L0_xattn_all

    def _L0_ffn_setup():
        import jax, jax.numpy as jnp
        import numpy as np
        E = 8
        K = 2
        key = jax.random.key(seed)
        ks = jax.random.split(key, 8)
        B, T, d = (4, 512, 256)
        h = 4 * d // E
        s = 0.02
        X = jax.random.normal(ks[0], (B, T, d), jnp.float32)
        routing_W = jax.random.normal(ks[1], (E, d), jnp.float32) * s
        expert_bias = jnp.zeros((E,), jnp.float32)
        sW1 = jax.random.normal(ks[2], (d, h), jnp.float32) * s
        sb1 = jnp.zeros((h,), jnp.float32)
        sW2 = jax.random.normal(ks[3], (h, d), jnp.float32) * s
        sb2 = jnp.zeros((d,), jnp.float32)
        rW1 = jax.random.normal(ks[4], (E, d, h), jnp.float32) * s
        rb1 = jnp.zeros((E, h), jnp.float32)
        rW2 = jax.random.normal(ks[5], (E, h, d), jnp.float32) * s
        rb2 = jnp.zeros((E, d), jnp.float32)
        return dict(X=X, routing_W=routing_W, expert_bias=expert_bias, sW1=sW1, sb1=sb1, sW2=sW2, sb2=sb2, rW1=rW1, rb1=rb1, rW2=rW2, rb2=rb2)
    _L0_ffn_all = _L0_ffn_setup()
    _L0_ffn_in = {k: v for k, v in _L0_ffn_all.items() if k in ('routing_W', 'expert_bias', 'sW1', 'sb1', 'sW2', 'sb2', 'rW1', 'rb1', 'rW2', 'rb2')}
    del _L0_ffn_all

    def _L1_xattn_setup():
        import jax, jax.numpy as jnp
        import numpy as np
        NUM_HEADS = 16
        KEY_SIZE = 64
        VALUE_SIZE = 64
        MODEL_SIZE = 256
        B, S, D = (2, 512, 256)

        def _vs_init(key, shape):
            fan_in = shape[0]
            stddev = np.sqrt(1.0 / fan_in) / 0.8796256610342398
            return stddev * jax.random.truncated_normal(key, -2.0, 2.0, shape, dtype=jnp.float32)
        key = jax.random.key(seed)
        ks = jax.random.split(key, 7)
        query = jax.random.normal(ks[0], (B, S, D), dtype=jnp.float32)
        k_in = jax.random.normal(ks[1], (B, S, D), dtype=jnp.float32)
        v_in = jax.random.normal(ks[2], (B, S, D), dtype=jnp.float32)
        Wq = _vs_init(ks[3], (D, NUM_HEADS * KEY_SIZE))
        Wk = _vs_init(ks[4], (D, NUM_HEADS * KEY_SIZE))
        Wv = _vs_init(ks[5], (D, NUM_HEADS * VALUE_SIZE))
        Wo = _vs_init(ks[6], (NUM_HEADS * VALUE_SIZE, MODEL_SIZE))
        bq = jnp.zeros((NUM_HEADS * KEY_SIZE,), jnp.float32)
        bk = jnp.zeros((NUM_HEADS * KEY_SIZE,), jnp.float32)
        bv = jnp.zeros((NUM_HEADS * VALUE_SIZE,), jnp.float32)
        bo = jnp.zeros((MODEL_SIZE,), jnp.float32)
        return {'query': query, 'key': k_in, 'value': v_in, 'Wq': Wq, 'bq': bq, 'Wk': Wk, 'bk': bk, 'Wv': Wv, 'bv': bv, 'Wo': Wo, 'bo': bo}
    _L1_xattn_all = _L1_xattn_setup()
    _L1_xattn_in = {k: v for k, v in _L1_xattn_all.items() if k in ('Wq', 'bq', 'Wk', 'bk', 'Wv', 'bv', 'Wo', 'bo')}
    del _L1_xattn_all

    def _L1_ffn_setup():
        import jax, jax.numpy as jnp
        import numpy as np
        DIM = 256
        NUM_EXPERTS = 8
        TOP_K = 2
        HIDDEN = int(DIM * 1.5)
        key = jax.random.key(seed)
        k_x, k_r, k_w1, k_w2, k_w3 = jax.random.split(key, 5)
        B, T = (2, 1024)
        s_in = 1.0 / np.sqrt(DIM)
        s_h = 1.0 / np.sqrt(HIDDEN)
        return {'x': jax.random.normal(k_x, (B, T, DIM), dtype=jnp.float32), 'Wr': jax.random.uniform(k_r, (DIM, NUM_EXPERTS), minval=-s_in, maxval=s_in, dtype=jnp.float32), 'W1': jax.random.uniform(k_w1, (NUM_EXPERTS, DIM, HIDDEN), minval=-s_in, maxval=s_in, dtype=jnp.float32), 'W2': jax.random.uniform(k_w2, (NUM_EXPERTS, HIDDEN, DIM), minval=-s_h, maxval=s_h, dtype=jnp.float32), 'W3': jax.random.uniform(k_w3, (NUM_EXPERTS, DIM, HIDDEN), minval=-s_in, maxval=s_in, dtype=jnp.float32)}
    _L1_ffn_all = _L1_ffn_setup()
    _L1_ffn_in = {k: v for k, v in _L1_ffn_all.items() if k in ('Wr', 'W1', 'W2', 'W3')}
    del _L1_ffn_all
    return {'x': x, 'ctx_1024': ctx_1024, 'L0_xattn_conv_w': _L0_xattn_in['conv_w'], 'L0_xattn_conv_b': _L0_xattn_in['conv_b'], 'L0_ffn_routing_W': _L0_ffn_in['routing_W'], 'L0_ffn_expert_bias': _L0_ffn_in['expert_bias'], 'L0_ffn_sW1': _L0_ffn_in['sW1'], 'L0_ffn_sb1': _L0_ffn_in['sb1'], 'L0_ffn_sW2': _L0_ffn_in['sW2'], 'L0_ffn_sb2': _L0_ffn_in['sb2'], 'L0_ffn_rW1': _L0_ffn_in['rW1'], 'L0_ffn_rb1': _L0_ffn_in['rb1'], 'L0_ffn_rW2': _L0_ffn_in['rW2'], 'L0_ffn_rb2': _L0_ffn_in['rb2'], 'L1_xattn_Wq': _L1_xattn_in['Wq'], 'L1_xattn_bq': _L1_xattn_in['bq'], 'L1_xattn_Wk': _L1_xattn_in['Wk'], 'L1_xattn_bk': _L1_xattn_in['bk'], 'L1_xattn_Wv': _L1_xattn_in['Wv'], 'L1_xattn_bv': _L1_xattn_in['bv'], 'L1_xattn_Wo': _L1_xattn_in['Wo'], 'L1_xattn_bo': _L1_xattn_in['bo'], 'L1_ffn_Wr': _L1_ffn_in['Wr'], 'L1_ffn_W1': _L1_ffn_in['W1'], 'L1_ffn_W2': _L1_ffn_in['W2'], 'L1_ffn_W3': _L1_ffn_in['W3']}

def reference(x, ctx_1024, L0_xattn_conv_w, L0_xattn_conv_b, L0_ffn_routing_W, L0_ffn_expert_bias, L0_ffn_sW1, L0_ffn_sb1, L0_ffn_sW2, L0_ffn_sb2, L0_ffn_rW1, L0_ffn_rb1, L0_ffn_rW2, L0_ffn_rb2, L1_xattn_Wq, L1_xattn_bq, L1_xattn_Wk, L1_xattn_bk, L1_xattn_Wv, L1_xattn_bv, L1_xattn_Wo, L1_xattn_bo, L1_ffn_Wr, L1_ffn_W1, L1_ffn_W2, L1_ffn_W3):
    import jax
    import jax.numpy as jnp

    def _L0_xattn_ref(inputs, memory, conv_w, conv_b, conv_units, short_units, rate):
        import jax, jax.numpy as jnp
        import numpy as np
        from jax import lax
        B, T, F = (32, 128, 256)
        CONV_UNITS = 512
        SHORT_UNITS = 512
        RATE = 4
        b, t, f = inputs.shape
        conv_mem = memory[:, :conv_units]
        short_mem = memory[:, -short_units:]
        old_memory = short_mem[:, :t]
        compression = lax.conv_general_dilated(old_memory, conv_w, window_strides=(rate,), padding='VALID', dimension_numbers=('NWC', 'WIO', 'NWC')) + conv_b
        tc = compression.shape[1]
        new_short = jnp.concatenate([short_mem[:, t:], inputs], axis=1)
        new_conv = jnp.concatenate([conv_mem[:, tc:], compression], axis=1)
        return jnp.concatenate([new_conv, new_short], axis=1)

    def _L0_ffn_ref(X, routing_W, expert_bias, sW1, sb1, sW2, sb2, rW1, rb1, rW2, rb2):
        import jax, jax.numpy as jnp
        import numpy as np
        E = 8
        K = 2
        B, T, d = X.shape
        shared = jax.nn.silu(X @ sW1 + sb1) @ sW2 + sb2
        logits = jnp.einsum('btd,ed->bte', X, routing_W) + expert_bias
        activation = jnp.sqrt(jax.nn.softplus(logits))
        top_vals, top_idx = jax.lax.top_k(activation, K)
        combine = jnp.sum(jax.nn.one_hot(top_idx, E, dtype=X.dtype) * top_vals[..., None], axis=-2)
        Xf = X.reshape(-1, d)
        cf = combine.reshape(-1, E)
        hdn = jax.nn.silu(jnp.einsum('nd,edh->enh', Xf, rW1) + rb1[:, None, :])
        y = jnp.einsum('enh,ehd->end', hdn, rW2) + rb2[:, None, :]
        routed = jnp.einsum('ne,end->nd', cf, y).reshape(B, T, d)
        return shared + routed

    def _L1_xattn_ref(query, key, value, Wq, bq, Wk, bk, Wv, bv, Wo, bo):
        import jax, jax.numpy as jnp
        import numpy as np
        NUM_HEADS = 16
        KEY_SIZE = 64
        VALUE_SIZE = 64
        MODEL_SIZE = 256
        B, S, D = (2, 512, 256)

        def _vs_init(key, shape):
            fan_in = shape[0]
            stddev = np.sqrt(1.0 / fan_in) / 0.8796256610342398
            return stddev * jax.random.truncated_normal(key, -2.0, 2.0, shape, dtype=jnp.float32)
        b, s, _ = query.shape
        q = (query @ Wq + bq).reshape(b, s, NUM_HEADS, KEY_SIZE)
        k = (key @ Wk + bk).reshape(b, key.shape[1], NUM_HEADS, KEY_SIZE)
        v = (value @ Wv + bv).reshape(b, value.shape[1], NUM_HEADS, VALUE_SIZE)
        logits = jnp.einsum('bshd,bShd->bhsS', q, k) / np.sqrt(KEY_SIZE).astype(np.float32)
        weights = jax.nn.softmax(logits, axis=-1)
        attn = jnp.einsum('bhsS,bShd->bshd', weights, v).reshape(b, s, NUM_HEADS * VALUE_SIZE)
        return attn @ Wo + bo

    def _L1_ffn_ref(x, Wr, W1, W2, W3):
        import jax, jax.numpy as jnp
        import numpy as np
        DIM = 256
        NUM_EXPERTS = 8
        TOP_K = 2
        HIDDEN = int(DIM * 1.5)
        B, T, C = x.shape
        xf = x.reshape(-1, C)
        gate_logits = xf @ Wr
        w, idx = jax.lax.top_k(gate_logits, TOP_K)
        w = jax.nn.softmax(w, axis=-1)
        comb = jnp.sum(w[:, :, None] * jax.nn.one_hot(idx, NUM_EXPERTS, dtype=w.dtype), axis=1)
        h = jnp.einsum('nc,ech->neh', xf, W1)
        g = jnp.einsum('nc,ech->neh', xf, W3)
        y = jnp.einsum('neh,ehc->nec', jax.nn.silu(h) * g, W2)
        out = jnp.einsum('nec,ne->nc', y, comb)
        return out.reshape(B, T, C)
    x = x + _L0_xattn_ref(ctx_1024, _layernorm(x, axis=-1), L0_xattn_conv_w, L0_xattn_conv_b, 512, 512, 4)
    x = x + _L0_ffn_ref(_layernorm(x, axis=-1), L0_ffn_routing_W, L0_ffn_expert_bias, L0_ffn_sW1, L0_ffn_sb1, L0_ffn_sW2, L0_ffn_sb2, L0_ffn_rW1, L0_ffn_rb1, L0_ffn_rW2, L0_ffn_rb2)
    x = x + _L1_xattn_ref(_layernorm(x, axis=-1), ctx_1024, ctx_1024, L1_xattn_Wq, L1_xattn_bq, L1_xattn_Wk, L1_xattn_bk, L1_xattn_Wv, L1_xattn_bv, L1_xattn_Wo, L1_xattn_bo)
    x = x + _L1_ffn_ref(_layernorm(x, axis=-1), L1_ffn_Wr, L1_ffn_W1, L1_ffn_W2, L1_ffn_W3)
    return x

_drawn_inputs = setup_inputs


def setup_inputs(seed=0):
    import zlib

    import numpy as np

    out = dict(_drawn_inputs(seed))
    spreads = {'L0_xattn_conv_b': (0.0, 0.8),
     'L0_ffn_expert_bias': (0.0, 0.1),
     'L0_ffn_sb1': (0.0, 0.8),
     'L0_ffn_sb2': (0.0, 0.1),
     'L0_ffn_rb1': (0.0, 0.685),
     'L0_ffn_rb2': (0.0, 0.1),
     'L1_xattn_bq': (0.0, 0.462),
     'L1_xattn_bk': (0.0, 0.8),
     'L1_xattn_bv': (0.0, 0.1),
     'L1_xattn_bo': (0.0, 0.1)}
    factors = {}
    for name, (base, spread) in spreads.items():
        noise = np.random.default_rng([zlib.crc32(name.encode()), seed]).standard_normal(out[name].shape)
        drawn = base * np.exp(spread * noise) if base else spread * noise
        out[name] = jnp.asarray(drawn.astype(out[name].dtype))
    for name, factor in factors.items():
        out[name] = (out[name] * factor).astype(out[name].dtype)
    return out
```

```python
from contextlib import ExitStack

import numpy as np
import concourse.bass as bass
from concourse import mybir

F32 = mybir.dt.float32
F32R = mybir.dt.float32r
BF16 = mybir.dt.bfloat16
I32 = mybir.dt.int32
ALU = mybir.AluOpType
ACT = mybir.ActivationFunctionType
AX = mybir.AxisListType

P = 128
NB, T, D = 4, 1024, 256
DC = D // P
S = 64
TILES = NB * T // P
GROUPS = 2
GT = TILES // GROUPS
BT = T // P
E = 8
E9 = E + 1
H0, H1 = 128, 384
QT = 4
QN = QT * P
QUADS = TILES // QT
UNITS = QUADS * E9
HC1 = H1 // P
XW = 260
SLOT_TILES = 2 * GT + E
NHEAD, DH = 16, 64
PAIRS = NHEAD // 2
HK = NHEAD * S
CONV = 512
RATE = 4
EPS = 1e-5
SMALL = 13
MAGIC = 1597463007.0


def build(nc, x, ctx_in, conv_w, conv_b, rout_w, rout_b, sw1, sb1, sw2, sb2, rw1, rb1, rw2, rb2,
          wq, bq, wk, bk, wv, bv, wo, bo, wr, w1, w2, w3, out):
    st = ExitStack()
    with st:
        st.enter_context(nc.allow_non_contiguous_dma(reason="bias columns and router weights, small"))

        def sb(name, shape, dt=F32, stack=st):
            return stack.enter_context(nc.sbuf_tensor(name, shape, dt))

        def sem(name):
            return st.enter_context(nc.semaphore(name))

        X = sb("X", [P, TILES, D])
        crow = sb("crow", [65, HK])
        zero4 = sb("zero4", [P, XW])
        def carve(mem, at, n, pattern=None, **k):
            v = mem[:, at:at + n]
            return v.rearrange(pattern, **k) if pattern else v

        ident = sb("ident", [P, P])
        ones = sb("ones", [P, P])
        upper = sb("upper", [P, P], BF16)
        ones_b = sb("ones_b", [P, P], BF16)
        bcols = sb("bcols", [P, 3, PAIRS])
        rows = crow[64:65, 0:2 * D]
        segones = crow[64:65, 2 * D:2 * D + P]
        roT = [sb(f"roT{l}", [P, DC, E]) for l in range(2)]
        rb_bc = sb("rb_bc", [P, 4 * E])
        prio = sb("prio", [P, E])
        stats = sb("stats", [P, TILES, 6])
        mean = sb("mean", [P, TILES])
        rstd = sb("rstd", [P, TILES])
        ta, tb, tc_ = (sb(n, [P, TILES * E]) for n in ("ta", "tb", "tc"))
        L = sb("L", [P, TILES, E])
        oh1, oh2, wk1, wk2 = (sb(n, [P, TILES, E]) for n in ("oh1", "oh2", "wk1", "wk2"))
        m1, m2, hot = (sb(n, [P, TILES]) for n in ("m1", "m2", "hot"))
        M = sb("M", [P, E, GT], BF16)
        segm = sb("segm", [P, E * GT])
        thr = sb("thr", [P, GT])
        slotno = sb("slotno", [P, SLOT_TILES])
        te, ti, ones8 = (sb(n, [P, E]) for n in ("te", "ti", "ones8"))
        wt = [sb(f"wt{k}", [P, GROUPS, GT]) for k in range(2)]
        slot = [sb(f"slot{k}", [P, GROUPS, GT], I32) for k in range(2)]
        eid_f = sb("eid_f", [P, SLOT_TILES])
        eid = sb("eid", [P, GROUPS, SLOT_TILES], I32)
        mx = sb("mx", [P, NHEAD])
        sm = sb("sm", [P, NHEAD])
        b1c = sb("b1c", [P, E9])

        s1 = ExitStack()
        N0 = sb("N0", [P, TILES, D], stack=s1)
        C = sb("C", [S, D], stack=s1)[:, :]
        wq_sb, wk_sb, wv_sb = (sb(n, [P, DC, NHEAD * DH], stack=s1)[:, :, :] for n in ("wq_sb", "wk_sb", "wv_sb"))
        wo_sb = sb("wo_sb", [P, PAIRS, D], stack=s1)[:, :, :]
        wqT = sb("wqT", [P, PAIRS, D], stack=s1)[:, :, :]
        kbd, vbd, ast, vst = ([sb(f"{n}{k}", [P, NB * P], stack=s1)[:, :] for k in range(2)]
                              for n in ("kbd", "vbd", "ast", "vst"))
        convw_sb = sb("convw_sb", [P, RATE, DC, D], stack=s1)[:, :, :, :]
        ctxT = sb("ctxT", [P, DC, NB * S], stack=s1)[:, :, :]
        CT = sb("CT", [P, 2, D], stack=s1)[:, :, :]
        U = sb("U", [P, 2, D], stack=s1)[:, :, :]
        UT = sb("UT", [P, DC, NB * S], stack=s1)[:, :, :]
        s1.close()

        s2 = ExitStack()
        stage = sb("stage", [P, DC * E9 * H0 + E9 * D], stack=s2)
        w1_raw = stage[:, 0:DC * E9 * H0].rearrange("p (c e h) -> p c e h", c=DC, e=E9)
        w2_raw = stage[:, DC * E9 * H0:].rearrange("p (e n) -> p e n", e=E9)
        cfT = stage[0:2 * E9, 0:TILES * P].rearrange("p (q n) -> p q n", q=QUADS)
        b2_raw = sb("b2_raw", [2 * E9, D], stack=s2)
        w1h, w1l = (sb(n, [P, DC, E9, H0], F32R, s2) for n in ("w1h", "w1l"))
        w2h, w2l = (sb(n, [P, E9, D], F32R, s2) for n in ("w2h", "w2l"))
        b2h, b2l = (sb(n, [2 * E9, D], F32R, s2) for n in ("b2h", "b2l"))
        roh, rol = (sb(n, [P, DC, E], F32R, s2) for n in ("roh", "rol"))
        sel = sb("sel", [2 * E9, E9, P], F32R, s2)
        cf = sb("cf", [P, TILES, 2 * E9], F32R, s2)
        cfq = [sb(f"cfq{k}", [2 * E9, QN], F32R, s2) for k in range(2)]
        xh, xl = (sb(n, [P, QUADS, DC, QN], F32R, s2) for n in ("xh", "xl"))
        xnq = [sb(f"xnq{k}", [P, QT, D], stack=s2) for k in range(2)]
        hsl = [sb(f"hsl{k}", [P, QN], stack=s2) for k in range(2)]
        hg = [sb(f"hg{k}", [P, QN], stack=s2) for k in range(2)]
        hh = [sb(f"hh{k}", [P, QN], F32R, s2) for k in range(2)]
        hl = [sb(f"hl{k}", [P, QN], F32R, s2) for k in range(2)]
        s2.close()

        N = sb("N", [P, TILES, XW])
        w13_sb = sb("w13_sb", [P, DC, E, 2 * H1])
        w2_sb = sb("w2_sb", [P, HC1, E, D])
        A_sb = [sb(f"A{k}", [P, DC, HK])[:, :, :] for k in range(2)]
        VW_sb = [sb(f"VW{k}", [P, PAIRS, D])[:, :, :] for k in range(2)]
        B = sb("B", [P, 4608])
        pr = [carve(B, 1024 * k, 1024) for k in range(2)]
        prT = carve(B, 2048, 1024)
        xn_a = [carve(B, 3072 + 256 * k, 256) for k in range(2)]
        xnT_a = [carve(B, 3584 + 256 * k, 256, "p (c n) -> p c n", c=DC) for k in range(2)]
        xs = [carve(B, XW * k, XW) for k in range(4)]
        xT = [carve(B, 1040 + 256 * k, 256, "p (c n) -> p c n", c=DC) for k in range(2)]
        hs = [carve(B, 1552 + H1 * k, H1) for k in range(2)]
        hT = [carve(B, 2320 + H1 * k, H1, "p (c n) -> p c n", c=HC1) for k in range(2)]
        ys = [carve(B, 3088 + 256 * k, 256) for k in range(2)]
        wcol = carve(B, 3600, 4)
        xn4 = carve(B, 0, 1024, "p (t n) -> p t n", t=4)
        xnT4 = carve(B, 1024, 1024, "p (c n) -> p c n", c=DC)
        cmp = carve(B, 2048, SLOT_TILES * E, "p (j e) -> p j e", e=E)
        tot = carve(B, 1024, E * GT)
        inc = carve(B, 1152, E * GT)

        psum = st.enter_context(nc.psum_tensor("psum", [P, 8, 512], F32))
        bank = [psum[:, k, :] for k in range(8)]

        XS = [nc.dram_tensor(f"xs_dram{g}", [SLOT_TILES * P, XW], F32).ap() for g in range(GROUPS)]
        YS = [nc.dram_tensor(f"ys_dram{g}", [SLOT_TILES * P, D], F32).ap() for g in range(GROUPS)]
        AD = nc.dram_tensor("a_dram", [NB, P, DC, HK], F32).ap()
        VD = nc.dram_tensor("vw_dram", [NB, P, PAIRS, D], F32).ap()
        CD = nc.dram_tensor("c_dram", [NB, HK], F32).ap()

        names = """consts ctx_in u_in x_in0 x_in1 s_in0 s_in1 qk_in vo_in small_in l0_in l1_in zeroed
            u_norm ut_p ut_sb c_p c_sb s_norm c_put
            pre_t pre_ts wqt_p wqt_sb k_p k_sb v_p v_sb a_p a_sb a_out0 a_out1 c2_p c2_sb c2_out0 c2_out1 vw_p vw_sb vw_out0 vw_out1
            l_ro l_sel l_w l_b2h l_b2 l_xn l_tp l_xh l_xl l_lg l_cf l_cft l_cfa l_cfd
            l_cfq l_bc l_h l_hs l_hg l_hh l_hl l_y l_yq l_xu
            xn4_r n_cp t_p xt_a xt_d ro_p ro_sb
            spa spd r_m r_pt rout sc1 sc2
            xs_in0 xs_in1 xs_in2 xs_in3 e_tp e_xt e_h e_g e_hs e_hg e_htp e_ht e_y e_ys e_st0 e_st1
            av_in0 av_in1 a_xn a_tp a_xt a_lg a_sub a_ex a_pn a_ptp a_pta a_ptd a_o a_xu
            gat1 gat2 stored bar_pe bar_act bar_dve bar_sp""".split()
        s = {n: sem(n) for n in names}

        class Marks:
            def __init__(self, eng, own):
                self.eng, self.own, self.n = eng, own, 0

            def meet(self):
                self.n += 1
                self.eng.drain()
                self.eng.sem_inc(s[self.own], 1)
                for other in ("bar_pe", "bar_act", "bar_dve", "bar_sp"):
                    if other != self.own:
                        self.eng.wait_ge(s[other], self.n)

        block = st.enter_context(nc.Block())

        @block.sync
        def _(sp):
            meet = Marks(sp, "bar_sp").meet
            sp.dma_start(CT, ctx_in.rearrange("(q b) s d -> (b s) q d", q=2)).then_inc(s["ctx_in"], 16)
            for b in range(NB):
                sp.dma_start(U[S * (b % 2):S * (b % 2) + S, b // 2, :],
                             x[b, CONV:CONV + S, :]).then_inc(s["u_in"], 16)
            for g in range(GROUPS):
                for b in (2 * g, 2 * g + 1):
                    t0 = b * BT
                    sp.dma_start(X[:, t0:t0 + BT, :], x[b].rearrange("(t p) d -> p t d", p=P)).then_inc(s[f"x_in{g}"], 16)
                    k = S // RATE
                    sp.dma_start(N0[:, t0:t0 + 4, :],
                                 x[b, k:k + CONV, :].rearrange("(t p) d -> p t d", p=P)).then_inc(s[f"s_in{g}"], 16)
                    sp.dma_start(N0[:, t0 + 4:t0 + 7, :],
                                 x[b, CONV + S:T - S, :].rearrange("(t p) d -> p t d", p=P)).then_inc(s[f"s_in{g}"], 16)
                    sp.dma_start(N0[0:S, t0 + 7, :], x[b, T - S:T, :]).then_inc(s[f"s_in{g}"], 16)
                    sp.dma_start(N0[S:P, t0 + 7, :], ctx_in[b]).then_inc(s[f"s_in{g}"], 16)
            for j in range(PAIRS):
                sp.wait_ge(s["c2_sb"], j + 1)
                sp.dma_start(CD[:, P * j:P * j + P].rearrange("(a b) n -> a b n", a=1),
                             crow[0:1, 512 * (j % 2):512 * (j % 2) + 512].rearrange("a (b n) -> a b n", b=NB)).then_inc(s[f"c2_out{j % 2}"], 16)
                for c in range(DC):
                    sp.wait_ge(s["a_sb"], DC * j + c + 1)
                    sp.dma_start(AD[:, :, c, P * j:P * j + P].rearrange("b p n -> p b n"),
                                 ast[c].rearrange("p (b n) -> p b n", b=NB)).then_inc(s[f"a_out{c}"], 16)
                for h in range(2):
                    sp.wait_ge(s["vw_sb"], 2 * j + h + 1)
                    sp.dma_start(VD[2 * h:2 * h + 2, :, j, :].rearrange("b p n -> p b n"),
                                 vst[h].rearrange("p (b n) -> p b n", b=2)).then_inc(s[f"vw_out{h}"], 16)
            for k in range(2):
                sp.wait_ge(s[f"c2_out{k}"], 16 * PAIRS // 2)
                sp.wait_ge(s[f"a_out{k}"], 16 * PAIRS)
                sp.wait_ge(s[f"vw_out{k}"], 16 * PAIRS)
            meet()
            for c in range(DC):
                sp.dma_start(w1_raw[:, c, 0:E, :], rw1[:, c * P:c * P + P, :].rearrange("e p h -> p e h")).then_inc(s["l0_in"], 16)
                sp.dma_start(w1_raw[:, c, E, :], sw1[c * P:c * P + P, :]).then_inc(s["l0_in"], 16)
            sp.dma_start(w2_raw[:, 0:E, :], rw2.rearrange("e p n -> p e n")).then_inc(s["l0_in"], 16)
            sp.dma_start(w2_raw[:, E, :], sw2).then_inc(s["l0_in"], 16)
            for k in (0, E9):
                sp.dma_start(b2_raw[k:k + E, :], rb2).then_inc(s["l0_in"], 16)
                sp.dma_start(b2_raw[k + E:k + E9, :], sb2.rearrange("(a n) -> a n", a=1)).then_inc(s["l0_in"], 16)
            for g in range(GROUPS):
                sp.dma_start(XS[g].rearrange("(p r) d -> p r d", p=P),
                             zero4[:, :].rearrange("p (a d) -> p a d", a=1).to_broadcast([P, SLOT_TILES, XW])).then_inc(s["zeroed"], 16)
            meet()

            def experts(g):
                sp.wait_ge(s["sc1"], 16 * GT * (g + 1))
                sp.wait_ge(s["sc2"], 16 * GT * (g + 1))
                base = g * SLOT_TILES

                def load(j, b, early=False):
                    if not early:
                        sp.wait_ge(s["e_xt"], base + j - 3)
                    sp.dma_start(xs[b], XS[g][bass.ds(j * P, P), :]).then_inc(s[f"xs_in{b}"], 16)

                def store(j, b):
                    sp.wait_ge(s["e_ys"], base + j + 1)
                    sp.dma_start(YS[g][bass.ds(j * P, P), :], ys[b]).then_inc(s[f"e_st{b}"], 16)

                for j in range(4):
                    load(j, j, True)
                load(4, 0)
                load(5, 1)
                loops = (SLOT_TILES - 6) // 4
                with sp.Fori(0, loops) as h_:
                    i = h_ * 4
                    for r in range(4):
                        load(i + (r + 6), (r + 2) % 4)
                        store(i + r, r % 2)
                for j in range(4 * loops, SLOT_TILES):
                    if j + 6 < SLOT_TILES:
                        load(j + 6, (j + 6) % 4)
                    store(j, j % 2)
                for b in range(2):
                    sp.wait_ge(s[f"e_st{b}"], 8 * SLOT_TILES * (g + 1))

            for c in range(DC):
                sp.dma_start(w13_sb[:, c, :, 0:H1], w1[:, c * P:c * P + P, :].rearrange("e p h -> p e h")).then_inc(s["l1_in"], 16)
                sp.dma_start(w13_sb[:, c, :, H1:], w3[:, c * P:c * P + P, :].rearrange("e p h -> p e h")).then_inc(s["l1_in"], 16)
            for c in range(HC1):
                sp.dma_start(w2_sb[:, c, :, :], w2[:, c * P:c * P + P, :].rearrange("e p n -> p e n")).then_inc(s["l1_in"], 16)
            for g in range(GROUPS):
                for k in range(2):
                    b = 2 * g + k
                    if b >= 2:
                        sp.wait_ge(s["a_o"], BT * (b - 1))
                    sp.dma_start(A_sb[k], AD[b]).then_inc(s[f"av_in{k}"], 16)
                    sp.dma_start(VW_sb[k], VD[b]).then_inc(s[f"av_in{k}"], 16)
                    sp.dma_start(crow[32 * k:32 * k + 1, :], CD[b:b + 1, :]).then_inc(s[f"av_in{k}"], 16)
            meet()
            meet()
            experts(0)
            meet()
            experts(1)
            meet()
            for g in range(GROUPS):
                sp.wait_ge(s["gat2"], 16 * GT * (g + 1))
                for b in (2 * g, 2 * g + 1):
                    sp.dma_start(out[b].rearrange("(t p) d -> p t d", p=P), X[:, b * BT:b * BT + BT, :]).then_inc(s["stored"], 16)
            sp.wait_ge(s["stored"], 16 * NB)

        @block.gpsimd
        def _(po):
            po.memset(ident[:, :], 0.0)
            po.memset(upper[:, :], 0.0)
            po.memset(ones_b[:, :], 1.0)
            po.memset(ones8[:, :], 1.0)
            po.memset(ones[:, :], 1.0)
            po.memset(segm[:, :], 1.0)
            po.iota(prio[:, :], pattern=[[-1, E]], base=E, channel_multiplier=0,
                    allow_small_or_imprecise_dtypes=True)
            po.iota(thr[:, :], pattern=[[P, GT]], base=0, channel_multiplier=0,
                    allow_small_or_imprecise_dtypes=True)
            po.iota(slotno[:, :], pattern=[[1, SLOT_TILES]], base=0, channel_multiplier=0,
                    allow_small_or_imprecise_dtypes=True)
            po.memset(zero4[:, :], 0.0)
            po.drain()
            po.memset(segm[:, :].rearrange("p (e t) -> p e t", e=E)[:, :, 0:1], 0.0)
            po.affine_select(out=ident[:, :], in_=ident[:, :], compare_op=ALU.not_equal, fill=1.0,
                             base=0, pattern=[[-1, P]], channel_multiplier=1)
            po.affine_select(out=upper[:, :], in_=upper[:, :], compare_op=ALU.is_ge, fill=1.0,
                             base=0, pattern=[[-1, P]], channel_multiplier=1)
            po.drain()
            po.memset(segones, 0.0)
            po.drain()
            for k in range(2):
                po.memset(kbd[k], 0.0)
                po.memset(vbd[k], 0.0)
            po.drain()
            po.memset(segones[:, 0:S], 1.0)
            po.drain()
            po.sem_inc(s["consts"], 2)
            po.wait_ge(s["c_sb"], 1)
            k = S // RATE
            for g in range(GROUPS):
                po.wait_ge(s["s_norm"], g + 1)
                for b in (2 * g, 2 * g + 1):
                    po.dma_start(N0[P - k:P, b * BT + 3, :], C[k * b:k * b + k, :]).then_inc(s["c_put"], 16)

            def after(n):
                for other in ("bar_pe", "bar_act", "bar_dve", "bar_sp"):
                    po.wait_ge(s[other], n)

            after(1)
            po.wait_ge(s["l0_in"], 16 * 10)
            for raw, high, low in ((w1_raw, w1h[:, :, :, :], w1l[:, :, :, :]), (w2_raw, w2h[:, :, :], w2l[:, :, :])):
                po.tensor_copy(high, raw)
                po.drain()
                last = po.tensor_tensor(low, raw, high.bitcast(F32), ALU.subtract)
                last.then_inc(s["l_w"], 1)
            after(2)
            po.memset(N[:, :, D:XW], 0.0)
            po.drain()
            po.sem_inc(s["consts"], 1)

            def scatter(g):
                if g == 0:
                    po.wait_ge(s["zeroed"], 16 * GROUPS)
                po.wait_ge(s["rout"], g + 1)
                for k in range(2):
                    if k == 1:
                        po.tensor_copy(N[:, g * GT:g * GT + GT, D:D + 1], wt[1][:, g, :].rearrange("p (t a) -> p t a", a=1))
                        po.drain()
                    for t in range(GT):
                        po.indirect_dma_start(
                            XS[g], bass.IndirectOffsetOnAxis(ap=slot[k][:, g, t:t + 1], axis=0),
                            N[:, g * GT + t, :], None).then_inc(s[f"sc{k + 1}"], 16)
                    po.wait_ge(s[f"sc{k + 1}"], 16 * GT * (g + 1))

            def gather(g):
                for b in range(2):
                    po.wait_ge(s[f"e_st{b}"], 16 * (SLOT_TILES // 2) * (g + 1))
                for k in range(2):
                    for t in range(GT):
                        po.indirect_dma_start(
                            X[:, g * GT + t, :], None, YS[g],
                            bass.IndirectOffsetOnAxis(ap=slot[k][:, g, t:t + 1], axis=0),
                            compute_op=ALU.add).then_inc(s[f"gat{k + 1}"], 16)
                    po.wait_ge(s[f"gat{k + 1}"], 16 * GT * (g + 1))

            scatter(0)
            scatter(1)
            gather(0)
            gather(1)

        @block.tensor
        def _(pe):
            meet = Marks(pe, "bar_pe").meet

            def mm(o, l, r, start, stop):
                return nc.tensor.matmul(o, l, r, start=start, stop=stop)

            pe.wait_ge(s["consts"], 2)
            pe.wait_ge(s["ctx_in"], 16)
            for q in range(2):
                for c in range(DC):
                    last = nc.tensor.transpose(bank[0][:, 256 * c + P * q:256 * c + P * q + P],
                                               CT[:, q, c * P:c * P + P], ident[:, :])
            last.then_inc(s["pre_t"], 1)
            pe.wait_ge(s["qk_in"], 32)
            for m in range(4):
                if m >= 2:
                    pe.wait_ge(s["wqt_sb"], m - 1)
                for h in range(2):
                    for c in range(DC):
                        last = nc.tensor.transpose(bank[1 + m % 2][:, 256 * h + P * c:256 * h + P * c + P],
                                                   wq_sb[:, c, (2 * m + h) * P:(2 * m + h + 1) * P], ident[:, :])
                last.then_inc(s["wqt_p"], 1)
            pe.wait_ge(s["u_norm"], 1)
            for q in range(2):
                for c in range(DC):
                    last = nc.tensor.transpose(bank[3][:, 256 * c + P * q:256 * c + P * q + P],
                                               U[:, q, c * P:c * P + P], ident[:, :])
            last.then_inc(s["ut_p"], 1)
            pe.wait_ge(s["ut_sb"], 1)
            pe.wait_ge(s["small_in"], 16 * SMALL)
            for k in range(RATE):
                for c in range(DC):
                    mm(bank[4][0:S, 0:D], UT[:, c, k::RATE], convw_sb[:, k, c, :], k == 0 and c == 0, False)
            mm(bank[4][0:S, 0:D], ones[64:65, 0:S], rows[:, 0:D], False, True).then_inc(s["c_p"], 1)

            pe.wait_ge(s["pre_ts"], 1)
            pe.wait_ge(s["wqt_sb"], 4)
            pe.wait_ge(s["vo_in"], 32)
            for j in range(PAIRS):
                if j >= 1:
                    pe.wait_ge(s["k_sb"], j)
                for c in range(DC):
                    last = mm(bank[0][:, 0:256], wk_sb[:, c, j * P:j * P + P], ctxT[:, c, :], c == 0, c == DC - 1)
                last.then_inc(s["k_p"], 1)
                if j >= 1:
                    pe.wait_ge(s["v_sb"], j)
                if j == 0:
                    pe.wait_ge(s["ut_sb"], 1)
                for c in range(DC):
                    last = mm(bank[1][:, 0:256], wv_sb[:, c, j * P:j * P + P], ctxT[:, c, :], c == 0, c == DC - 1)
                last.then_inc(s["v_p"], 1)
                pe.wait_ge(s["k_sb"], j + 1)
                for c in range(DC):
                    if j >= 1:
                        pe.wait_ge(s["a_sb"], DC * (j - 1) + c + 1)
                    mm(bank[2 + c], wqT[:, j, c * P:c * P + P], kbd[j % 2], True, True).then_inc(s["a_p"], 1)
                if j == 0:
                    pe.wait_ge(s["c_sb"], 1)
                if j >= 1:
                    pe.wait_ge(s["c2_sb"], j)
                mm(bank[4][0:1, :], bcols[:, 0, j:j + 1], kbd[j % 2], True, True).then_inc(s["c2_p"], 1)
                pe.wait_ge(s["v_sb"], j + 1)
                for h in range(2):
                    if j >= 1:
                        pe.wait_ge(s["vw_sb"], 2 * (j - 1) + h + 1)
                    for b in (2 * h, 2 * h + 1):
                        o = bank[5 + h][:, 256 * (b % 2):256 * (b % 2) + 256]
                        last = mm(o, vbd[j % 2][:, b * P:b * P + P], wo_sb[:, j, :], True, j > 0)
                        if j == 0:
                            last = mm(o, segones, rows[:, D:2 * D], False, True)
                    last.then_inc(s["vw_p"], 1)
            meet()

            def layer0():
                for q in range(QUADS):
                    pe.wait_ge(s["l_xn"], q + 1)
                    if q >= 2:
                        pe.wait_ge(s["l_xl"], q - 1)
                    for c in range(DC):
                        for t in range(QT):
                            last = nc.tensor.transpose(bank[2 * (q % 2) + c][:, t * P:t * P + P],
                                                       xnq[q % 2][:, t, c * P:c * P + P], ident[:, :])
                    last.then_inc(s["l_tp"], 1)
                    if q == 0:
                        pe.wait_ge(s["l_ro"], 1)
                    pe.wait_ge(s["l_xl"], q + 1)
                    for t in range(QT):
                        o = bank[5][:, (QT * q + t) * E:(QT * q + t) * E + E]
                        for c in range(DC):
                            for a, w in ((xh, roh), (xl, roh), (xh, rol)):
                                last = nc.tensor.matmul(o, a[:, q, c, t * P:t * P + P], w[:, c, :],
                                                        start=q == t == c == 0 and a is xh and w is roh, stop=False,
                                                        skip_group_check=True)
                    last.then_inc(s["l_lg"], 1)
                pe.wait_ge(s["l_cf"], 1)
                for q in range(QUADS):
                    for t in range(QT):
                        last = nc.tensor.transpose(bank[q][0:2 * E9, t * P:t * P + P],
                                                   cf[:, QT * q + t, :].bitcast(F32), ident[:, :])
                    last.then_inc(s["l_cft"], 1)
                pe.wait_ge(s["l_cfa"], 1)
                pe.wait_ge(s["l_cfd"], 1)
                pe.wait_ge(s["l_w"], 2)
                pe.wait_ge(s["l_b2"], 1)
                pe.wait_ge(s["l_sel"], 1)

                def up(n, u, q, v, e, early):
                    if e == 0:
                        pe.wait_ge(s["l_cfq"], q + 1)
                    if not early:
                        pe.wait_ge(s["l_hg"], n - 1)
                        pe.wait_ge(s["l_hs"], n - 1)
                    nc.tensor.matmul(bank[u % 2], sel[:, e, :], cfq[v][:, :], start=True, stop=True).then_inc(s["l_bc"], 1)
                    for i, (w, a) in enumerate(((w1h, xh), (w1h, xl), (w1l, xh))):
                        for c in range(DC):
                            last = nc.tensor.matmul(bank[3 + u % 2], w[:, c, e, :],
                                                    a[:, bass.ds(q, 1), c, :].rearrange("p a n -> p (a n)"),
                                                    start=i == c == 0, stop=i == 2 and c == DC - 1)
                    last.then_inc(s["l_h"], 1)

                def down(n, u, q, v, e, early):
                    pe.wait_ge(s["l_hl"], n + 1)
                    if e == 0 and not early:
                        pe.wait_ge(s["l_xu"], q - 1)
                    for t in range(QT):
                        o = bank[(6, 7, 2, 5)[2 * v + t // 2]][:, D * (t % 2):D * (t % 2) + D]
                        if e == 0:
                            for w in (b2h, b2l):
                                nc.tensor.matmul(o, cfq[v][:, t * P:t * P + P], w[:, :],
                                                 start=t % 2 == 0 and w is b2h, stop=False, skip_group_check=True)
                        for a, w in ((hh, w2h), (hl, w2h), (hh, w2l)):
                            last = nc.tensor.matmul(o, a[u % 2][:, t * P:t * P + P], w[:, e, :],
                                                    start=False, stop=False, skip_group_check=True)
                    last.then_inc(s["l_y"], 1)

                def pair(h, first):
                    for u in range(2 * E9):
                        up(h * (2 * E9) + u, u, h * 2 + u // E9, u // E9, u % E9, first and u < 2)
                        w = u - 2
                        if w >= 0:
                            down(h * (2 * E9) + w, w, h * 2 + w // E9, w // E9, w % E9, first)
                        elif not first:
                            down(h * (2 * E9) + w, w + 2 * E9, h * 2 - 1, 1, w + E9, False)

                pair(0, True)
                with pe.Fori(1, QUADS // 2) as h_:
                    pair(h_, False)
                for w in (2, 1):
                    down(UNITS - w, 2 * E9 - w, QUADS - 1, 1, E9 - w, False)

            def router(g):
                for q in range(4):
                    k = 4 * g + q
                    pe.wait_ge(s["xn4_r"], k + 1)
                    if k:
                        pe.wait_ge(s["xt_a"], k)
                        pe.wait_ge(s["xt_d"], k)
                    for c in range(DC):
                        for t in range(4):
                            last = nc.tensor.transpose(bank[c][:, t * P:t * P + P], xn4[:, t, c * P:c * P + P], ident[:, :])
                    last.then_inc(s["t_p"], 1)
                    pe.wait_ge(s["xt_a"], k + 1)
                    pe.wait_ge(s["xt_d"], k + 1)
                    if k:
                        pe.wait_ge(s["ro_sb"], k)
                    for t in range(4):
                        for c in range(DC):
                            last = mm(bank[5][:, t * E:t * E + E], xnT4[:, c, t * P:t * P + P], roT[1][:, c, :],
                                      c == 0, c == DC - 1)
                    last.then_inc(s["ro_p"], 1)
                pe.wait_ge(s["r_m"], g + 1)
                mflat = M[:, :, :].rearrange("p e t -> p (e t)")
                mm(bank[6][:, 0:E * GT], upper[:, :], mflat, True, True)
                mm(bank[7][:, 0:E * GT], ones_b[:, :], mflat, True, True).then_inc(s["r_pt"], 1)

            def experts(g):
                base = g * SLOT_TILES

                def xpose(j, b, b4, early=False):
                    pe.wait_ge(s[f"xs_in{b4}"], (j - b4) * 4 + 16 * (g * SLOT_TILES // 4 + 1))
                    if not early:
                        pe.wait_ge(s["e_xt"], base + j)
                    for c in range(DC):
                        last = nc.tensor.transpose(bank[0][:, c * P:c * P + P], xs[b4][:, c * P:c * P + P], ident[:, :])
                    last.then_inc(s["e_tp"], 1)

                def up(j, b, early=False):
                    ex = pe.value_load(eid[0:1, g, bass.ds(j, 1)], min_val=0, max_val=E - 1)
                    pe.wait_ge(s["e_xt"], base + j + 1)
                    if not early:
                        pe.wait_ge(s["e_hg"], base + j - 1)
                    for half, sm_name in enumerate(("e_h", "e_g")):
                        for c in range(DC):
                            last = mm(bank[2 + 2 * half + b][:, 0:H1], xT[b][:, c, :],
                                      w13_sb[:, c, bass.ds(ex, 1), half * H1:half * H1 + H1].rearrange("p a n -> p (a n)"),
                                      c == 0, c == DC - 1)
                        last.then_inc(s[sm_name], 1)

                def hpose(j, b, early=False):
                    pe.wait_ge(s["e_hg"], base + j + 1)
                    if not early:
                        pe.wait_ge(s["e_ht"], base + j - 1)
                    for c in range(HC1):
                        last = nc.tensor.transpose(bank[6 + b][:, c * P:c * P + P], hs[b][:, c * P:c * P + P], ident[:, :])
                    last.then_inc(s["e_htp"], 1)

                def down(j, b, early=False):
                    ex = pe.value_load(eid[0:1, g, bass.ds(j, 1)], min_val=0, max_val=E - 1)
                    pe.wait_ge(s["e_ht"], base + j + 1)
                    if not early:
                        pe.wait_ge(s["e_ys"], base + j)
                    for c in range(HC1):
                        last = mm(bank[1][:, 0:D], hT[b][:, c, :], w2_sb[:, c, bass.ds(ex, 1), :].rearrange("p a n -> p (a n)"),
                                  c == 0, c == HC1 - 1)
                    last.then_inc(s["e_y"], 1)

                if g == 0:
                    pe.wait_ge(s["l1_in"], 16 * 7)
                xpose(0, 0, 0, True)
                up(0, 0, True)
                xpose(1, 1, 1)
                up(1, 1, True)
                hpose(0, 0, True)
                xpose(2, 0, 2)
                up(2, 0)
                hpose(1, 1, True)
                xpose(3, 1, 3)
                down(0, 0, True)
                with pe.Fori(0, (SLOT_TILES - 4) // 4) as h_:
                    i = h_ * 4
                    for r in range(4):
                        j, b = i + (r + 3), (r + 3) % 2
                        up(j, b)
                        hpose(i + (r + 2), 1 - b)
                        xpose(i + (r + 4), 1 - b, r)
                        down(i + (r + 1), b)
                z = SLOT_TILES - 1
                up(z, 1)
                hpose(z - 1, 0)
                down(z - 2, 1)
                hpose(z, 1)
                down(z - 1, 0)
                down(z, 1)

            def attention(g):
                for k in range(2):
                    b_ = 2 * g + k
                    base = b_ * BT
                    pe.wait_ge(s[f"av_in{k}"], 48 * (g + 1))

                    def xpose(j, b, first):
                        pe.wait_ge(s["a_xn"], base + j + 1)
                        if not first:
                            pe.wait_ge(s["a_xt"], base + j)
                        for c in range(DC):
                            last = nc.tensor.transpose(bank[6][:, c * P:c * P + P], xn_a[b][:, c * P:c * P + P], ident[:, :])
                        last.then_inc(s["a_tp"], 1)

                    def logits(j, b, first):
                        pe.wait_ge(s["a_xt"], base + j + 1)
                        if not first:
                            pe.wait_ge(s["a_sub"], base + j - 1)
                        for h in range(2):
                            for c in range(DC):
                                mm(bank[2 * b + h], xnT_a[b][:, c, :], A_sb[k][:, c, 512 * h:512 * h + 512], c == 0, False)
                            last = mm(bank[2 * b + h], ones[32 * k:32 * k + 1, :], crow[32 * k:32 * k + 1, 512 * h:512 * h + 512], False, True)
                        last.then_inc(s["a_lg"], 1)

                    def ppose(j, b, first):
                        pe.wait_ge(s["a_pn"], base + j + 1)
                        if not first:
                            pe.wait_ge(s["a_pta"], base + j)
                            pe.wait_ge(s["a_ptd"], base + j)
                        for c in range(PAIRS):
                            last = nc.tensor.transpose(bank[4 + c // 4][:, (c % 4) * P:(c % 4) * P + P], pr[b][:, c * P:c * P + P], ident[:, :])
                        last.then_inc(s["a_ptp"], 1)

                    def values(j, b, first):
                        pe.wait_ge(s["a_pta"], base + j + 1)
                        pe.wait_ge(s["a_ptd"], base + j + 1)
                        if not first:
                            pe.wait_ge(s["a_xu"], base + j)
                        for c in range(PAIRS):
                            last = mm(bank[7][:, 0:D], prT[:, c * P:c * P + P], VW_sb[k][:, c, :], c == 0, c == PAIRS - 1)
                        last.then_inc(s["a_o"], 1)

                    f0 = b_ == 0
                    xpose(0, 0, f0)
                    logits(0, 0, f0)
                    xpose(1, 1, False)
                    logits(1, 1, f0)
                    ppose(0, 0, f0)
                    xpose(2, 0, False)
                    values(0, 0, f0)
                    with pe.Fori(1, (BT - 2) // 2) as h_:
                        i = h_ * 2
                        for b in range(2):
                            logits(i + b, b, False)
                            ppose(i + b - 1, 1 - b, False)
                            xpose(i + b + 1, 1 - b, False)
                            values(i + b - 1, 1 - b, False)
                    z = BT - 2
                    logits(z, 0, False)
                    ppose(z - 1, 1, False)
                    xpose(z + 1, 1, False)
                    values(z - 1, 1, False)
                    logits(z + 1, 1, False)
                    ppose(z, 0, False)
                    values(z, 0, False)
                    ppose(z + 1, 1, False)
                    values(z + 1, 1, False)

            layer0()
            meet()
            for g in range(GROUPS):
                attention(g)
                router(g)
                meet()
            experts(0)
            meet()
            experts(1)
            meet()

        @block.scalar
        def _(ac):
            meet = Marks(ac, "bar_act").meet
            act = nc.scalar.activation

            for dst, src in ((wk_sb, wk), (wq_sb, wq)):
                ac.dma_start(dst, src.rearrange("(c p) n -> p c n", p=P)).then_inc(s["qk_in"], 16)
            small = [(bcols[:, k, :], v.rearrange("(j p) -> p j", p=P)) for k, v in enumerate((bq, bk, bv))]
            small += [(rows[:, k * D:k * D + D], v.rearrange("(a n) -> a n", a=1)) for k, v in enumerate((conv_b, bo))]
            small += [(convw_sb[:, :, c, :], conv_w[:, c * P:c * P + P, :].rearrange("k p n -> p k n")) for c in range(DC)]
            small += [(b1c[:, 0:E], rb1.rearrange("e p -> p e")), (b1c[:, E:E9], sb1.rearrange("(p a) -> p a", a=1))]
            small += [(roT[1][:, :, :], wr.rearrange("(c p) e -> p c e", p=P)),
                      (rb_bc[:, :].rearrange("p (b e) -> p b e", b=4),
                       rout_b.rearrange("(a b e) -> a b e", a=1, b=1).to_broadcast([P, 4, E]))]
            small += [(roT[0][:, c, :], rout_w[:, c * P:c * P + P].rearrange("e p -> p e")) for c in range(DC)]
            assert len(small) == SMALL
            for dst, src in small:
                ac.dma_start(dst, src).then_inc(s["small_in"], 16)
            ac.dma_start(wv_sb, wv.rearrange("(c p) n -> p c n", p=P)).then_inc(s["vo_in"], 16)
            ac.dma_start(wo_sb, wo.rearrange("(j p) n -> p j n", p=P)).then_inc(s["vo_in"], 16)

            ac.wait_ge(s["pre_t"], 1)
            act(ctxT, bank[0].rearrange("p (c n) -> p c n", c=DC), ACT.Copy).then_inc(s["pre_ts"], 1)
            for m in range(4):
                ac.wait_ge(s["wqt_p"], m + 1)
                act(wqT[:, 2 * m:2 * m + 2, :], bank[1 + m % 2].rearrange("p (j n) -> p j n", j=2), ACT.Copy).then_inc(s["wqt_sb"], 1)
            ac.wait_ge(s["ut_p"], 1)
            act(UT, bank[3].rearrange("p (c n) -> p c n", c=DC), ACT.Copy).then_inc(s["ut_sb"], 1)
            ac.wait_ge(s["c_p"], 1)
            act(C, bank[4][0:S, 0:D], ACT.Copy).then_inc(s["c_sb"], 1)
            ac.wait_ge(s["consts"], 2)
            ac.wait_ge(s["small_in"], 16 * SMALL)
            for j in range(PAIRS):
                for kind, bk_, dst, psem, done, bcol in (("k", 0, kbd, "k_p", "k_sb", 1), ("v", 1, vbd, "v_p", "v_sb", 2)):
                    ac.wait_ge(s[psem], j + 1)
                    if j >= 2:
                        if kind == "k":
                            ac.wait_ge(s["c2_p"], j - 1)
                        else:
                            ac.wait_ge(s["vw_p"], 2 * (j - 1))
                    for h in range(2):
                        r = slice(DH * h, DH * h + DH)
                        last = act(dst[j % 2][r, :].rearrange("p (b n) -> p b n", b=NB)[:, :, S * h:S * h + S],
                                   bank[bk_][r, 0:256].rearrange("p (b n) -> p b n", b=NB),
                                   ACT.Identity, bias=bcols[r, bcol, j:j + 1])
                    last.then_inc(s[done], 1)
                for c in range(DC):
                    ac.wait_ge(s["a_p"], DC * j + c + 1)
                    if j:
                        ac.wait_ge(s[f"a_out{c}"], 16 * j)
                    act(ast[c], bank[2 + c], ACT.Copy, scale=DH ** -0.5).then_inc(s["a_sb"], 1)
                ac.wait_ge(s["c2_p"], j + 1)
                if j >= 2:
                    ac.wait_ge(s[f"c2_out{j % 2}"], 16 * (j // 2))
                act(crow[0:1, 512 * (j % 2):512 * (j % 2) + 512], bank[4][0:1, :], ACT.Copy, scale=DH ** -0.5).then_inc(s["c2_sb"], 1)
                for h in range(2):
                    ac.wait_ge(s["vw_p"], 2 * j + h + 1)
                    if j:
                        ac.wait_ge(s[f"vw_out{h}"], 16 * j)
                    act(vst[h], bank[5 + h], ACT.Copy).then_inc(s["vw_sb"], 1)
            meet()

            def layer0():
                act(roh[:, :, :], roT[0][:, :, :], ACT.Copy).then_inc(s["l_xh"], 1)
                for q in range(QUADS):
                    ac.wait_ge(s["l_tp"], q + 1)
                    for c in range(DC):
                        act(xh[:, q, c, :], bank[2 * (q % 2) + c], ACT.Copy).then_inc(s["l_xh"], 1)
                ac.wait_ge(s["l0_in"], 16 * 10)
                act(b2h[:, :], b2_raw[:, :], ACT.Copy).then_inc(s["l_b2h"], 1)
                ac.wait_ge(s["spa"], 1)
                act(wk2[:, :, :], wk1[:, :, :], ACT.Exp)
                ac.drain()
                act(wk2[:, :, :], wk2[:, :, :], ACT.Ln, bias=1.0).then_inc(s["spd"], 1)
                ac.wait_ge(s["l_w"], 2)
                for q in range(QUADS // 2):
                    ac.wait_ge(s["l_cft"], q + 1)
                    act(cfT[:, q, :], bank[q][0:2 * E9, :], ACT.Copy)
                ac.drain()
                ac.sem_inc(s["l_cfa"], 1)

                def quad(q, v, early):
                    if not early:
                        ac.wait_ge(s["l_y"], q * E9 - E9)
                    else:
                        ac.wait_ge(s["l_cfd"], 1)
                    act(cfq[v][:, :], cfT[:, bass.ds(q, 1), :].rearrange("p a n -> p (a n)"), ACT.Copy).then_inc(s["l_cfq"], 1)

                def unit(n, u, e, early):
                    ac.wait_ge(s["l_h"], n + 1)
                    if not early:
                        ac.wait_ge(s["l_hg"], n - 1)
                    act(hsl[u % 2][:, :], bank[3 + u % 2], ACT.Silu, bias=b1c[:, e:e + 1]).then_inc(s["l_hs"], 1)
                    ac.wait_ge(s["l_hg"], n + 1)
                    if not early:
                        ac.wait_ge(s["l_y"], n - 1)
                    act(hh[u % 2][:, :], hg[u % 2][:, :], ACT.Copy).then_inc(s["l_hh"], 1)

                def pair(h, first):
                    for u in range(2 * E9):
                        if u % E9 == 0:
                            quad(h * 2 + u // E9, u // E9, first)
                        unit(h * (2 * E9) + u, u, u % E9, first and u < 2)

                pair(0, True)
                with ac.Fori(1, QUADS // 2) as h_:
                    pair(h_, False)

            def router(g):
                for q in range(4):
                    k = 4 * g + q
                    ac.wait_ge(s["xn4_r"], k + 1)
                    t0 = g * GT + 4 * q
                    act(N[:, t0:t0 + 4, 0:D], xn4, ACT.Copy).then_inc(s["n_cp"], 1)
                    ac.wait_ge(s["t_p"], k + 1)
                    if k:
                        ac.wait_ge(s["ro_p"], k)
                    act(xnT4[:, 0, :], bank[0], ACT.Copy).then_inc(s["xt_a"], 1)
                ac.wait_ge(s["spa"], g + 2)
                act(wt[1][:, g, :], wt[1][:, g, :], ACT.Exp).then_inc(s["spd"], 1)

            def experts(g):
                base = g * SLOT_TILES

                def xcopy(j, b, b4, early=False, fresh=False):
                    ac.wait_ge(s["e_tp"], base + j + 1)
                    if not early:
                        ac.wait_ge(s["e_g"], base + j - 1)
                    if not fresh:
                        ac.wait_ge(s["e_ys"], base + j - 3)
                    act(wcol[:, b4:b4 + 1], xs[b4][:, D:D + 1], ACT.Copy)
                    act(xT[b], bank[0][:, 0:D].rearrange("p (c n) -> p c n", c=DC), ACT.Copy).then_inc(s["e_xt"], 1)

                def silu(j, b, early=False):
                    ac.wait_ge(s["e_h"], base + j + 1)
                    if not early:
                        ac.wait_ge(s["e_htp"], base + j - 1)
                    act(hs[b], bank[2 + b][:, 0:H1], ACT.Silu).then_inc(s["e_hs"], 1)

                def scale(j, b, b4, early=False):
                    ac.wait_ge(s["e_y"], base + j + 1)
                    if not early:
                        ac.wait_ge(s[f"e_st{b}"], (j - b) * 8 + 8 * g * SLOT_TILES)
                    act(ys[b], bank[1][:, 0:D], ACT.Copy, scale=wcol[:, b4:b4 + 1]).then_inc(s["e_ys"], 1)

                xcopy(0, 0, 0, True, True)
                silu(0, 0, True)
                xcopy(1, 1, 1, True, True)
                silu(1, 1, True)
                xcopy(2, 0, 2, False, True)
                silu(2, 0)
                xcopy(3, 1, 3, False, True)
                scale(0, 0, 0, True)
                silu(3, 1)
                xcopy(4, 0, 0)
                scale(1, 1, 1, True)
                loops = (SLOT_TILES - 5) // 4
                with ac.Fori(0, loops) as h_:
                    i = h_ * 4
                    for r in range(4):
                        silu(i + (r + 4), r % 2)
                        xcopy(i + (r + 5), 1 - r % 2, (r + 1) % 4)
                        scale(i + (r + 2), r % 2, (r + 2) % 4)
                for j in range(4 * loops + 4, SLOT_TILES):
                    silu(j, j % 2)
                    if j + 1 < SLOT_TILES:
                        xcopy(j + 1, 1 - j % 2, (j + 1) % 4)
                    scale(j - 2, j % 2, (j - 2) % 4)
                scale(SLOT_TILES - 2, 0, 2)
                scale(SLOT_TILES - 1, 1, 3)

            def attention(g):
                for k in range(2):
                    b_ = 2 * g + k
                    base = b_ * BT

                    def xcopy(j, b, early):
                        ac.wait_ge(s["a_tp"], base + j + 1)
                        if not early:
                            ac.wait_ge(s["a_lg"], base + j - 1)
                        act(xnT_a[b], bank[6][:, 0:D].rearrange("p (c n) -> p c n", c=DC), ACT.Copy).then_inc(s["a_xt"], 1)

                    def expo(j, b):
                        ac.wait_ge(s["a_sub"], base + j + 1)
                        act(pr[b], pr[b], ACT.Exp).then_inc(s["a_ex"], 1)

                    def pcopy(j, b, early):
                        ac.wait_ge(s["a_ptp"], base + j + 1)
                        if not early:
                            ac.wait_ge(s["a_o"], base + j)
                        act(prT[:, 0:512], bank[4], ACT.Copy).then_inc(s["a_pta"], 1)

                    e0 = b_ == 0
                    xcopy(0, 0, e0)
                    xcopy(1, 1, e0)
                    expo(0, 0)
                    pcopy(0, 0, e0)
                    xcopy(2, 0, False)
                    expo(1, 1)
                    with ac.Fori(1, (BT - 2) // 2) as h_:
                        i = h_ * 2
                        for b in range(2):
                            pcopy(i + b - 1, 1 - b, False)
                            xcopy(i + b + 1, 1 - b, False)
                            expo(i + b, b)
                    z = BT - 2
                    pcopy(z - 1, 1, False)
                    xcopy(z + 1, 1, False)
                    expo(z, 0)
                    pcopy(z, 0, False)
                    expo(z + 1, 1)
                    pcopy(z + 1, 1, False)

            layer0()
            meet()
            for g in range(GROUPS):
                attention(g)
                router(g)
                meet()
            experts(0)
            meet()
            experts(1)
            meet()

        @block.vector
        def _(ve):
            meet = Marks(ve, "bar_dve").meet
            tt, ts, stt = nc.vector.tensor_tensor, nc.vector.tensor_scalar, nc.vector.scalar_tensor_tensor

            def bc(v, n):
                return v.rearrange("p (a b) -> p a b", b=1).to_broadcast([P, v.shape[1], n])

            def rep(v, n):
                return v.rearrange("p (b a) -> p b a", b=1).to_broadcast([P, n, v.shape[1]])

            def rsqrt(o, v, tmp):
                ts(o.bitcast(I32), v.bitcast(I32), 1, None, ALU.logical_shift_right)
                ve.drain()
                ts(o.bitcast(I32), o.bitcast(I32), -1.0, MAGIC, ALU.mult, ALU.add)
                ve.drain()
                for _ in range(3):
                    stt(tmp, o, -0.5, v, ALU.mult, ALU.mult)
                    ve.drain()
                    tt(tmp, tmp, o, ALU.mult)
                    ve.drain()
                    stt(o, tmp, 1.5, o, ALU.add, ALU.mult)
                    ve.drain()

            def ln_finish(w):
                a, b, c = ta[:, 0:w], tb[:, 0:w], tc_[:, 0:w]
                m, r = mean[:, 0:w], rstd[:, 0:w]

                def col(k):
                    return stats[:, 0:w, k:k + 1].rearrange("p t a -> p (t a)")

                ve.drain()
                tt(a, col(1), col(4), ALU.add)
                tt(b, col(1), col(4), ALU.subtract)
                tt(c, col(2), col(5), ALU.add)
                ve.drain()
                ts(m, a, 0.5, None, ALU.mult)
                tt(b, b, b, ALU.mult)
                ts(c, c, 1.0 / D, EPS, ALU.mult, ALU.add)
                ve.drain()
                stt(c, b, 0.25, c, ALU.mult, ALU.add)
                ve.drain()
                rsqrt(r, c, a)

            def ln_stats(buf, t0, tiles):
                with ve.Fori(0, tiles // 4) as h_:
                    i = h_ * 4
                    for u in range(4):
                        nc.vector.bn_stats(stats[:, bass.ds(i + u, 1), :].rearrange("p a n -> p (a n)"),
                                           buf[:, bass.ds(t0 + i + u, 1), 0:D].rearrange("p a n -> p (a n)"))
                ln_finish(tiles)

            ve.wait_ge(s["u_in"], 16 * NB)
            for q in range(2):
                nc.vector.bn_stats(stats[:, q, :], U[:, q, :])
            ln_finish(2)
            for q in range(2):
                last = ts(U[:, q, :], U[:, q, :], mean[:, q:q + 1], rstd[:, q:q + 1], ALU.subtract, ALU.mult)
            last.then_inc(s["u_norm"], 1)

            for g in range(GROUPS):
                ve.wait_ge(s[f"s_in{g}"], 16 * 8)
                ln_stats(N0, g * GT, GT)
                for t in range(GT):
                    r = S if t % BT == BT - 1 else P
                    v = N0[0:r, g * GT + t, :]
                    last = ts(v, v, mean[0:r, t:t + 1], rstd[0:r, t:t + 1], ALU.subtract, ALU.mult)
                last.then_inc(s["s_norm"], 1)
                ve.wait_ge(s["c_put"], 32 * (g + 1))
                ve.wait_ge(s[f"x_in{g}"], 32)
                v = X[:, g * GT:g * GT + GT, :]
                tt(v, v, N0[:, g * GT:g * GT + GT, :], ALU.add)
            meet()

            def first_max(src, m, oh, tiles):
                h = hot[:, 0:tiles]
                nc.vector.tensor_reduce(m, src, AX.X, ALU.max)
                ve.drain()
                tt(oh, src, bc(m, E), ALU.is_equal)
                ve.drain()
                tt(oh, oh, rep(prio[:, :], tiles), ALU.mult)
                ve.drain()
                nc.vector.tensor_reduce(h, oh, AX.X, ALU.max)
                ve.drain()
                tt(oh, oh, bc(h, E), ALU.is_equal)
                ve.drain()

            def top2(tiles):
                def fl(v):
                    return v[:, 0:tiles, :].rearrange("p t e -> p (t e)")
                first_max(L[:, 0:tiles, :], m1[:, 0:tiles], oh1[:, 0:tiles, :], tiles)
                stt(fl(wk1), fl(oh1), -3.0e38, fl(L), ALU.mult, ALU.add)
                ve.drain()
                first_max(wk1[:, 0:tiles, :], m2[:, 0:tiles], oh2[:, 0:tiles, :], tiles)

            def layer0():
                ve.wait_ge(s["l_xh"], 1)
                tt(rol[:, :, :], roT[0][:, :, :], roh[:, :, :].bitcast(F32), ALU.subtract).then_inc(s["l_ro"], 1)
                k2 = 2 * E9

                def plane(o):
                    return ident[0:k2, o:o + E9].rearrange("p (e a) -> p e a", a=1).to_broadcast([k2, E9, P])
                tt(sel[:, :, :], plane(0), plane(E9), ALU.add).then_inc(s["l_sel"], 1)
                ln_stats(X, 0, TILES)

                def rows_in(q):
                    if q >= 2:
                        ve.wait_ge(s["l_tp"], q - 1)
                    for t in range(QT):
                        u = QT * q + t
                        last = ts(xnq[q % 2][:, t, :], X[:, u, :], mean[:, u:u + 1], rstd[:, u:u + 1], ALU.subtract, ALU.mult)
                    last.then_inc(s["l_xn"], 1)

                rows_in(0)
                for q in range(QUADS):
                    if q + 1 < QUADS:
                        rows_in(q + 1)
                    for c in range(DC):
                        ve.wait_ge(s["l_xh"], DC * q + c + 2)
                        last = tt(xl[:, q, c, :], bank[2 * (q % 2) + c], xh[:, q, c, :].bitcast(F32), ALU.subtract)
                    last.then_inc(s["l_xl"], 1)
                ve.wait_ge(s["l_b2h"], 1)
                tt(b2l[:, :], b2_raw[:, :], b2h[:, :].bitcast(F32), ALU.subtract).then_inc(s["l_b2"], 1)
                ve.wait_ge(s["l_lg"], QUADS)
                for k in range(QUADS):
                    tt(L[:, QT * k:QT * k + QT, :].rearrange("p t e -> p (t e)"), bank[5][:, QT * E * k:QT * E * k + QT * E], rb_bc[:, :], ALU.add)
                ve.drain()
                flat = "p t e -> p (t e)"
                Lv = L[:, :, :]
                ts(wk1[:, :, :], Lv, -1.0, None, ALU.mult)
                ve.drain()
                tt(wk1[:, :, :], wk1[:, :, :], Lv, ALU.min).then_inc(s["spa"], 1)
                ve.wait_ge(s["spd"], 1)
                ve.drain()
                stt(wk1[:, :, :].rearrange(flat), Lv.rearrange(flat), 0.0, wk2[:, :, :].rearrange(flat), ALU.max, ALU.add)
                ve.drain()
                rsqrt(wk2[:, :, :].rearrange(flat), wk1[:, :, :].rearrange(flat), ta[:, :])
                tt(Lv, wk1[:, :, :], wk2[:, :, :], ALU.mult)
                ve.drain()
                top2(TILES)
                tt(wk1[:, :, :], oh1[:, :, :], oh2[:, :, :], ALU.add)
                nc.vector.memset(cf[:, :, E:E9].bitcast(F32), 1.0)
                nc.vector.memset(cf[:, :, E9 + E:].bitcast(F32), 0.0)
                ve.drain()
                tt(wk1[:, :, :], wk1[:, :, :], Lv, ALU.mult)
                ve.drain()
                nc.vector.tensor_copy(cf[:, :, 0:E], wk1[:, :, :])
                ve.drain()
                tt(cf[:, :, E9:E9 + E], wk1[:, :, :], cf[:, :, 0:E].bitcast(F32), ALU.subtract)
                ve.drain()
                ve.sem_inc(s["l_cf"], 1)
                ve.wait_ge(s["l_w"], 2)
                for q in range(QUADS // 2, QUADS):
                    ve.wait_ge(s["l_cft"], q + 1)
                    nc.vector.tensor_copy(cfT[:, q, :], bank[q][0:2 * E9, :])
                ve.drain()
                ve.sem_inc(s["l_cfd"], 1)

                def unit(n, u, early):
                    ve.wait_ge(s["l_bc"], n + 1)
                    ve.wait_ge(s["l_hs"], n + 1)
                    if not early:
                        ve.wait_ge(s["l_hl"], n - 1)
                        ve.wait_ge(s["l_hh"], n - 1)
                    tt(hg[u % 2][:, :], bank[u % 2], hsl[u % 2][:, :], ALU.mult).then_inc(s["l_hg"], 1)
                    ve.wait_ge(s["l_hh"], n + 1)
                    if not early:
                        ve.wait_ge(s["l_y"], n - 1)
                    tt(hl[u % 2][:, :], hg[u % 2][:, :], hh[u % 2][:, :].bitcast(F32), ALU.subtract).then_inc(s["l_hl"], 1)

                def add(n, q, v):
                    ve.wait_ge(s["l_y"], n + 1)
                    for h in range(2):
                        x2 = X[:, bass.ds(q * QT + 2 * h, 2), :].rearrange("p t n -> p (t n)")
                        last = tt(x2, bank[(6, 7, 2, 5)[2 * v + h]], x2, ALU.add)
                    last.then_inc(s["l_xu"], 1)

                def pair(h, first):
                    for u in range(2 * E9):
                        n = h * (2 * E9) + u
                        unit(n, u, first and u < 2)
                        if u % E9 == 1 and not (first and u < E9):
                            add(n + (-2), h * 2 + (u // E9 - 1), 1 - u // E9)

                pair(0, True)
                with ve.Fori(1, QUADS // 2) as h_:
                    pair(h_, False)
                add(UNITS - 1, QUADS - 1, 1)

            def router(g):
                ve.drain()
                ln_stats(X, g * GT, GT)
                if g == 0:
                    ve.wait_ge(s["consts"], 3)
                for q in range(4):
                    k = 4 * g + q
                    if k:
                        ve.wait_ge(s["t_p"], k)
                        ve.wait_ge(s["n_cp"], k)
                    for t in range(4):
                        u = 4 * q + t
                        last = ts(xn4[:, t, :], X[:, g * GT + u, :], mean[:, u:u + 1], rstd[:, u:u + 1], ALU.subtract, ALU.mult)
                    last.then_inc(s["xn4_r"], 1)
                    ve.wait_ge(s["t_p"], k + 1)
                    if k:
                        ve.wait_ge(s["ro_p"], k)
                    nc.vector.tensor_copy(xnT4[:, 1, :], bank[1]).then_inc(s["xt_d"], 1)
                    ve.wait_ge(s["ro_p"], k + 1)
                    nc.vector.tensor_copy(L[:, 4 * q:4 * q + 4, :].rearrange("p t e -> p (t e)"), bank[5][:, 0:4 * E]).then_inc(s["ro_sb"], 1)
                ve.drain()
                top2(GT)
                tt(M[:, :, :].rearrange("p e t -> p t e"), oh1[:, 0:GT, :], oh2[:, 0:GT, :], ALU.add).then_inc(s["r_m"], 1)
                w0, w1_ = wt[0][:, g, :], wt[1][:, g, :]
                tt(w1_, m2[:, 0:GT], m1[:, 0:GT], ALU.subtract).then_inc(s["spa"], 1)
                ve.wait_ge(s["spd"], g + 2)
                ts(w0, w1_, 1.0, None, ALU.add)
                ve.drain()
                nc.vector.reciprocal(w0, w0)
                ve.drain()
                tt(w1_, w1_, w0, ALU.mult)
                ve.drain()
                ve.wait_ge(s["n_cp"], 4 * g + 4)
                nc.vector.tensor_copy(N[:, g * GT:g * GT + GT, D:D + 1], w0.rearrange("p (t a) -> p t a", a=1))
                ve.wait_ge(s["r_pt"], g + 1)
                nc.vector.tensor_copy(tot, bank[7][:, 0:E * GT])
                ve.drain()
                nc.vector.tensor_tensor_scan(inc, segm[:, :], tot, 0.0, ALU.mult, ALU.add)
                ve.drain()
                last_t = inc.rearrange("p (e t) -> p e t", e=E)[:, :, GT - 1:GT]
                tt(ta[:, 0:E * GT].rearrange("p (e t) -> p e t", e=E), last_t.to_broadcast([P, E, GT]), rep(thr[:, :], E), ALU.is_gt)
                tt(tb[:, 0:E * GT], inc, tot, ALU.subtract)
                ve.drain()
                nc.vector.tensor_reduce(te[:, :], ta[:, 0:E * GT].rearrange("p (e t) -> p e t", e=E), AX.X, ALU.add)
                tt(tb[:, 0:E * GT], bank[6][:, 0:E * GT], tb[:, 0:E * GT], ALU.add)
                ve.drain()
                nc.vector.tensor_tensor_scan(ti[:, :], ones8[:, :], te[:, :], 0.0, ALU.mult, ALU.add)
                ve.drain()
                tt(te[:, :], ti[:, :], te[:, :], ALU.subtract)
                tt(cmp, bc(slotno[:, :], E), rep(ti[:, :], SLOT_TILES), ALU.is_ge)
                ve.drain()
                tb3 = tb[:, 0:E * GT].rearrange("p (e t) -> p e t", e=E)
                stt(tb3, bc(te[:, :], GT), float(P), tb3, ALU.mult, ALU.add)
                nc.vector.tensor_reduce(eid_f[:, :], cmp, AX.X, ALU.add)
                ve.drain()
                ts(eid[:, g, :], eid_f[:, :], float(E - 1), None, ALU.min)
                for k, oh in enumerate((oh1, oh2)):
                    tt(wk1[:, 0:GT, :], oh[:, 0:GT, :], tb3.rearrange("p e t -> p t e"), ALU.mult)
                    ve.drain()
                    nc.vector.tensor_reduce(hot[:, 0:GT], wk1[:, 0:GT, :], AX.X, ALU.add)
                    ve.drain()
                    nc.vector.tensor_copy(slot[k][:, g, :], hot[:, 0:GT])
                ve.drain()
                ve.sem_inc(s["rout"], 1)

            def experts(g):
                base = g * SLOT_TILES

                def gate(j, b):
                    ve.wait_ge(s["e_hs"], base + j + 1)
                    ve.wait_ge(s["e_g"], base + j + 1)
                    tt(hs[b], bank[4 + b][:, 0:H1], hs[b], ALU.mult).then_inc(s["e_hg"], 1)

                def hcopy(j, b, early=False):
                    ve.wait_ge(s["e_htp"], base + j + 1)
                    if not early:
                        ve.wait_ge(s["e_y"], base + j - 1)
                    nc.vector.tensor_copy(hT[b].rearrange("p c n -> p (c n)"), bank[6 + b][:, 0:H1]).then_inc(s["e_ht"], 1)

                gate(0, 0)
                gate(1, 1)
                hcopy(0, 0, True)
                gate(2, 0)
                hcopy(1, 1, True)
                gate(3, 1)
                hcopy(2, 0)
                with ve.Fori(2, SLOT_TILES // 2) as h_:
                    i = h_ * 2
                    for b in range(2):
                        gate(i + b, b)
                        hcopy(i + (b - 1), 1 - b)
                hcopy(SLOT_TILES - 1, 1)

            def attention(g):
                ln_stats(X, g * GT, GT)
                for k in range(2):
                    b_ = 2 * g + k
                    base = b_ * BT

                    def rows_in(j, b, early):
                        if not early:
                            ve.wait_ge(s["a_tp"], base + j - 1)
                        u = k * BT + j
                        ts(xn_a[b], X[:, bass.ds(g * GT + u, 1), :].rearrange("p a n -> p (a n)"),
                           mean[:, bass.ds(u, 1)], rstd[:, bass.ds(u, 1)], ALU.subtract, ALU.mult).then_inc(s["a_xn"], 1)

                    def shift(j, b, early):
                        ve.wait_ge(s["a_lg"], base + j + 1)
                        if not early:
                            ve.wait_ge(s["a_ptp"], base + j - 1)
                        lg = psum[:, 2 * b:2 * b + 2, :].rearrange("p a (h n) -> p (a h) n", n=S)
                        nc.vector.tensor_reduce(mx[:, :], lg, AX.X, ALU.max)
                        ve.drain()
                        tt(pr[b].rearrange("p (h n) -> p h n", n=S), lg, bc(mx[:, :], S), ALU.subtract).then_inc(s["a_sub"], 1)

                    def norm(j, b):
                        ve.wait_ge(s["a_ex"], base + j + 1)
                        v = pr[b].rearrange("p (h n) -> p h n", n=S)
                        nc.vector.tensor_reduce(sm[:, :], v, AX.X, ALU.add)
                        ve.drain()
                        nc.vector.reciprocal(sm[:, :], sm[:, :])
                        ve.drain()
                        tt(v, v, bc(sm[:, :], S), ALU.mult).then_inc(s["a_pn"], 1)

                    def pcopy(j, early):
                        ve.wait_ge(s["a_ptp"], base + j + 1)
                        if not early:
                            ve.wait_ge(s["a_o"], base + j)
                        nc.vector.tensor_copy(prT[:, 512:], bank[5]).then_inc(s["a_ptd"], 1)

                    def add(j):
                        ve.wait_ge(s["a_o"], base + j + 1)
                        v = X[:, bass.ds(g * GT + k * BT + j, 1), :].rearrange("p a n -> p (a n)")
                        tt(v, bank[7][:, 0:D], v, ALU.add).then_inc(s["a_xu"], 1)

                    e0 = b_ == 0
                    rows_in(0, 0, e0)
                    rows_in(1, 1, e0)
                    shift(0, 0, e0)
                    rows_in(2, 0, False)
                    norm(0, 0)
                    pcopy(0, e0)
                    shift(1, 1, e0)
                    add(0)
                    with ve.Fori(1, (BT - 2) // 2) as h_:
                        i = h_ * 2
                        for b in range(2):
                            rows_in(i + b + 1, 1 - b, False)
                            norm(i + b - 1, 1 - b)
                            pcopy(i + b - 1, False)
                            shift(i + b, b, False)
                            add(i + b - 1)
                    z = BT - 2
                    rows_in(z + 1, 1, False)
                    norm(z - 1, 1)
                    pcopy(z - 1, False)
                    shift(z, 0, False)
                    add(z - 1)
                    norm(z, 0)
                    pcopy(z, False)
                    shift(z + 1, 1, False)
                    add(z)
                    norm(z + 1, 1)
                    pcopy(z + 1, False)
                    add(z + 1)

            layer0()
            meet()
            for g in range(GROUPS):
                attention(g)
                router(g)
                meet()
            experts(0)
            meet()
            experts(1)
            meet()


_INS = ['x', 'ctx_1024', 'L0_xattn_conv_w', 'L0_xattn_conv_b', 'L0_ffn_routing_W', 'L0_ffn_expert_bias', 'L0_ffn_sW1',
        'L0_ffn_sb1', 'L0_ffn_sW2', 'L0_ffn_sb2', 'L0_ffn_rW1', 'L0_ffn_rb1', 'L0_ffn_rW2', 'L0_ffn_rb2',
        'L1_xattn_Wq', 'L1_xattn_bq', 'L1_xattn_Wk', 'L1_xattn_bk', 'L1_xattn_Wv', 'L1_xattn_bv', 'L1_xattn_Wo',
        'L1_xattn_bo', 'L1_ffn_Wr', 'L1_ffn_W1', 'L1_ffn_W2', 'L1_ffn_W3']


def kernel(**inputs):
    import numpy as _np
    import concourse.bacc as _bacc
    from concourse import mybir as _mybir
    from concourse.bass_utils import run_bass_kernel_spmd as _run

    nc = _bacc.Bacc("TRN2", target_bir_lowering=False, num_devices=1)
    arrays, args = {}, []
    for name in _INS:
        a = _np.ascontiguousarray(inputs[name])
        arrays[f"in_{name}_dram"] = a
        args.append(nc.dram_tensor(f"in_{name}_dram", a.shape, _mybir.dt.from_np(a.dtype), kind="ExternalInput").ap())
    args.append(nc.dram_tensor("out_0_dram", (NB, T, D), _mybir.dt.float32, kind="ExternalOutput").ap())
    build(nc, *args)
    r = _run(nc, [arrays], core_ids=[0])
    return r.results[0]["out_0_dram"]
```

```python
from contextlib import ExitStack

import numpy as np
import concourse.bass as bass
from concourse import mybir

F32 = mybir.dt.float32
F32R = mybir.dt.float32r
BF16 = mybir.dt.bfloat16
I32 = mybir.dt.int32
ALU = mybir.AluOpType
ACT = mybir.ActivationFunctionType
AX = mybir.AxisListType

P = 128
NB, T, D = 4, 1024, 256
DC = D // P
S = 64
TILES = NB * T // P
BT = T // P
BATCHES = ((0, 1, 2), (3,))
GROUPS = len(BATCHES)
G0 = [g[0] * BT for g in BATCHES]
GT = [len(g) * BT for g in BATCHES]
GM = max(GT)
E = 8
E9 = E + 1
H0, H1 = 128, 384
QT = 4
QN = QT * P
QUADS = TILES // QT
UNITS = QUADS * E9
HC1 = H1 // P
XW = 260
SLOTS = [2 * n + E for n in GT]
SLOT0 = [sum(SLOTS[:g]) for g in range(GROUPS)]
SM = max(SLOTS)
NHEAD, DH = 16, 64
PAIRS = NHEAD // 2
HK = NHEAD * S
CONV = 512
RATE = 4
EPS = 1e-5
SMALL = 13
MAGIC = 1597463007.0


def build(nc, x, ctx_in, conv_w, conv_b, rout_w, rout_b, sw1, sb1, sw2, sb2, rw1, rb1, rw2, rb2,
          wq, bq, wk, bk, wv, bv, wo, bo, wr, w1, w2, w3, out):
    st = ExitStack()
    with st:
        st.enter_context(nc.allow_non_contiguous_dma(reason="bias columns and router weights, small"))

        def sb(name, shape, dt=F32, stack=st):
            return stack.enter_context(nc.sbuf_tensor(name, shape, dt))

        def sem(name):
            return st.enter_context(nc.semaphore(name))

        X = sb("X", [P, TILES, D])
        crow = sb("crow", [65, 2 * D + P])
        zero4 = sb("zero4", [P, XW])
        def carve(mem, at, n, pattern=None, **k):
            v = mem[:, at:at + n]
            return v.rearrange(pattern, **k) if pattern else v

        ident = sb("ident", [P, P])
        ones = sb("ones", [P, P])
        upper = sb("upper", [P, P], BF16)
        ones_b = sb("ones_b", [P, P], BF16)
        bcols = sb("bcols", [P, 3, PAIRS])
        rows = crow[64:65, 0:2 * D]
        segones = crow[64:65, 2 * D:2 * D + P]
        roT = [sb(f"roT{l}", [P, DC, E]) for l in range(2)]
        rb_bc = sb("rb_bc", [P, 4 * E])
        prio = sb("prio", [P, E])
        stats = sb("stats", [P, TILES, 6])
        mean = sb("mean", [P, TILES])
        rstd = sb("rstd", [P, TILES])
        ta, tb, tc_ = (sb(n, [P, TILES * E]) for n in ("ta", "tb", "tc"))
        L = sb("L", [P, TILES, E])
        oh1, oh2, wk1, wk2 = (sb(n, [P, TILES, E]) for n in ("oh1", "oh2", "wk1", "wk2"))
        m1, m2, hot = (sb(n, [P, TILES]) for n in ("m1", "m2", "hot"))
        M = sb("M", [P, E * GM], BF16)
        segm = sb("segm", [P, GROUPS, E * GM])
        thr = sb("thr", [P, GM])
        slotno = sb("slotno", [P, SM])
        te, ti, ones8 = (sb(n, [P, E]) for n in ("te", "ti", "ones8"))
        wt = [sb(f"wt{k}", [P, TILES]) for k in range(2)]
        slot = [sb(f"slot{k}", [P, TILES], I32) for k in range(2)]
        eid_f = sb("eid_f", [P, SM])
        eid = sb("eid", [P, GROUPS, SM], I32)
        mx = sb("mx", [P, NHEAD])
        sm = [sb(f"sm{k}", [P, NHEAD]) for k in range(2)]
        xstats = sb("xstats", [P, TILES, 6])
        ones2 = sb("ones2", [2, P], F32R)
        b1c = sb("b1c", [P, E9])

        s1 = ExitStack()
        N0 = sb("N0", [P, TILES, D], stack=s1)
        C = sb("C", [S, D], stack=s1)[:, :]
        wq_sb, wk_sb, wv_sb = (sb(n, [P, DC, NHEAD * DH], stack=s1)[:, :, :] for n in ("wq_sb", "wk_sb", "wv_sb"))
        wo_sb = sb("wo_sb", [P, PAIRS, D], stack=s1)[:, :, :]
        wqT = sb("wqT", [P, PAIRS, D], stack=s1)[:, :, :]
        kbd, vbd = ([sb(f"{n}{k}", [P, NB * P], stack=s1)[:, :] for k in range(2)] for n in ("kbd", "vbd"))
        st_r = [sb(f"st_r{k}", [P, NB * P], stack=s1)[:, :] for k in range(4)]
        st_h, st_l = ([sb(f"{n}{k}", [P, NB * P], F32R, s1)[:, :] for k in range(4)] for n in ("st_h", "st_l"))
        c_col = sb("c_col", [P, PAIRS * NB], stack=s1)[:, :]
        c_r = sb("c_r", [PAIRS * NB, P], stack=s1)[:, :]
        c_h, c_l = (sb(n, [PAIRS * NB, P], F32R, s1)[:, :] for n in ("c_h", "c_l"))
        convw_sb = sb("convw_sb", [P, RATE, DC, D], stack=s1)[:, :, :, :]
        ctxT = sb("ctxT", [P, DC, NB * S], stack=s1)[:, :, :]
        CT = sb("CT", [P, 2, D], stack=s1)[:, :, :]
        U = sb("U", [P, 2, D], stack=s1)[:, :, :]
        UT = sb("UT", [P, DC, NB * S], stack=s1)[:, :, :]
        s1.close()

        s2 = ExitStack()
        stage = sb("stage", [P, DC * E9 * H0 + E9 * D], stack=s2)
        w1_raw = stage[:, 0:DC * E9 * H0].rearrange("p (c e h) -> p c e h", c=DC, e=E9)
        w2_raw = stage[:, DC * E9 * H0:].rearrange("p (e n) -> p e n", e=E9)
        cfT = stage[0:2 * E9, 0:TILES * P].rearrange("p (q n) -> p q n", q=QUADS)
        b2_raw = sb("b2_raw", [2 * E9, D], stack=s2)
        w1h, w1l = (sb(n, [P, DC, E9, H0], F32R, s2) for n in ("w1h", "w1l"))
        w2h, w2l = (sb(n, [P, E9, D], F32R, s2) for n in ("w2h", "w2l"))
        b2h, b2l = (sb(n, [2 * E9, D], F32R, s2) for n in ("b2h", "b2l"))
        roh, rol = (sb(n, [P, DC, E], F32R, s2) for n in ("roh", "rol"))
        sel = sb("sel", [2 * E9, E9, P], F32R, s2)
        cf = sb("cf", [P, TILES, 2 * E9], F32R, s2)
        cfq = [sb(f"cfq{k}", [2 * E9, QN], F32R, s2) for k in range(2)]
        xh, xl = (sb(n, [P, QUADS, DC, QN], F32R, s2) for n in ("xh", "xl"))
        xnq = [sb(f"xnq{k}", [P, QT, D], stack=s2) for k in range(2)]
        hsl = [sb(f"hsl{k}", [P, QN], stack=s2) for k in range(2)]
        hg = [sb(f"hg{k}", [P, QN], stack=s2) for k in range(2)]
        hh = [sb(f"hh{k}", [P, QN], F32R, s2) for k in range(2)]
        hl = [sb(f"hl{k}", [P, QN], F32R, s2) for k in range(2)]
        s2.close()

        N = sb("N", [P, TILES, XW])
        B = sb("B", [P, 4096])
        s3 = ExitStack()
        Ah, Al = (sb(n, [P, 2, DC, HK], F32R, s3) for n in ("Ah", "Al"))
        Vh, Vl = (sb(n, [P, 2, PAIRS, D], F32R, s3) for n in ("Vh", "Vl"))
        cb = [sb(f"cb{k}", [2, HK], F32R, s3) for k in range(2)]
        pr = [sb(f"pr{k}", [P, HK], stack=s3)[:, :] for k in range(2)]
        prh, prl = (sb(n, [P, HK], F32R, s3) for n in ("prh", "prl"))
        xn_a = [sb(f"xna{k}", [P, D], stack=s3)[:, :] for k in range(2)]
        xah, xal = ([sb(f"{n}{k}", [P, DC, P], F32R, s3) for k in range(2)] for n in ("xah", "xal"))
        s3.close()
        w13_sb = sb("w13_sb", [P, DC, E, 2 * H1])
        w2_sb = sb("w2_sb", [P, HC1, E, D])
        xs = [carve(B, XW * k, XW) for k in range(4)]
        xT = [carve(B, 1040 + 256 * k, 256, "p (c n) -> p c n", c=DC) for k in range(2)]
        hs = [carve(B, 1552 + H1 * k, H1) for k in range(2)]
        hT = [carve(B, 2320 + H1 * k, H1, "p (c n) -> p c n", c=HC1) for k in range(2)]
        ys = [carve(B, 3088 + 256 * k, 256) for k in range(2)]
        wcol = carve(B, 3600, 4)
        xnT4 = [carve(B, 1024 * k, 1024, "p (c n) -> p c n", c=DC) for k in range(2)]
        tot = carve(B, 0, E * GM)
        inc = carve(B, 256, E * GM)
        cmp = carve(B, 2048, SM * E)

        psum = st.enter_context(nc.psum_tensor("psum", [P, 8, 512], F32))
        bank = [psum[:, k, :] for k in range(8)]

        XS = [nc.dram_tensor(f"xs_dram{g}", [SLOTS[g] * P, XW], F32).ap() for g in range(GROUPS)]
        YS = [nc.dram_tensor(f"ys_dram{g}", [SLOTS[g] * P, D], F32).ap() for g in range(GROUPS)]
        AD = [nc.dram_tensor(f"a_dram{k}", [NB, P, DC, HK], F32).ap() for k in range(2)]
        VD = [nc.dram_tensor(f"vw_dram{k}", [NB, P, PAIRS, D], F32).ap() for k in range(2)]
        CD = nc.dram_tensor("c_dram", [NB, 2, HK], F32).ap()

        names = """consts ctx_in u_in x_in0 x_in1 x_in2 x_in3 s_in0 s_in1 s_in2 s_in3 qk_in vo_in small_in l0_in l1_in zeroed
            u_norm ut_p ut_sb c_p c_sb s_norm c_put
            pre_t pre_ts wqt_p wqt_sb k_p k_sb v_p v_sb a_p vw_p st_hr st_lo st_out0 st_out1 st_out2 st_out3
            c2_p c2_c c2_t c2_h c2_l c2_out
            l_ro l_sel l_w l_b2h l_b2 l_xn l_tp l_xh l_xl l_lg l_lt l_lgt l_cf l_cft l_cfa l_cfd
            l_cfq l_bc l_h l_hs l_hg l_hh l_hl l_y l_xu
            n_r t_p xt_a xt_d ro_p ro_sb
            spa spd r_m r_pt rout sc1 sc2
            xs_in0 xs_in1 xs_in2 xs_in3 e_tp e_xt e_h e_g e_hs e_hg e_htp e_ht e_y e_ys e_st0 e_st1
            av_in0 av_in1 a_xn a_tp a_xh a_xl a_lg a_sub a_ex a_sm a_pn a_ptp a_ph a_pl a_o a_xu
            gat1 gat2 stored bar_pe bar_act bar_dve bar_sp""".split()
        s = {n: sem(n) for n in names}

        class Marks:
            def __init__(self, eng, own):
                self.eng, self.own, self.n = eng, own, 0

            def meet(self):
                self.n += 1
                self.eng.drain()
                self.eng.sem_inc(s[self.own], 1)
                for other in ("bar_pe", "bar_act", "bar_dve", "bar_sp"):
                    if other != self.own:
                        self.eng.wait_ge(s[other], self.n)

        block = st.enter_context(nc.Block())

        @block.sync
        def _(sp):
            meet = Marks(sp, "bar_sp").meet
            sp.dma_start(CT, ctx_in.rearrange("(q b) s d -> (b s) q d", q=2)).then_inc(s["ctx_in"], 16)
            for b in range(NB):
                sp.dma_start(U[S * (b % 2):S * (b % 2) + S, b // 2, :],
                             x[b, CONV:CONV + S, :]).then_inc(s["u_in"], 16)
            for b in range(NB):
                t0 = b * BT
                k = S // RATE
                sp.dma_start(N0[:, t0:t0 + 4, :],
                             x[b, k:k + CONV, :].rearrange("(t p) d -> p t d", p=P)).then_inc(s[f"s_in{b}"], 16)
                sp.dma_start(N0[:, t0 + 4:t0 + 7, :],
                             x[b, CONV + S:T - S, :].rearrange("(t p) d -> p t d", p=P)).then_inc(s[f"s_in{b}"], 16)
                sp.dma_start(N0[0:S, t0 + 7, :], x[b, T - S:T, :]).then_inc(s[f"s_in{b}"], 16)
                sp.dma_start(N0[S:P, t0 + 7, :], ctx_in[b]).then_inc(s[f"s_in{b}"], 16)
                sp.dma_start(X[:, t0:t0 + BT, :], x[b].rearrange("(t p) d -> p t d", p=P)).then_inc(s[f"x_in{b}"], 16)
            for j in range(PAIRS):
                for i in range(4):
                    for part, (src, done) in enumerate(((st_h, "st_hr"), (st_l, "st_lo"))):
                        sp.wait_ge(s[done], 4 * j + i + 1)
                        if i < DC:
                            sp.dma_start(AD[part][:, :, i, P * j:P * j + P].rearrange("b p n -> p b n"),
                                         src[i].bitcast(F32).rearrange("p (b n) -> p b n", b=NB)).then_inc(s[f"st_out{i}"], 16)
                        else:
                            h = i - DC
                            sp.dma_start(VD[part][2 * h:2 * h + 2, :, j, :].rearrange("b p n -> p b n"),
                                         src[i].bitcast(F32).rearrange("p (b n) -> p b n", b=2)).then_inc(s[f"st_out{i}"], 16)
            for part, (src, done) in enumerate(((c_h, "c2_h"), (c_l, "c2_l"))):
                sp.wait_ge(s[done], 1)
                for b in range(NB):
                    sp.dma_start(CD[b, part, :].rearrange("(j n) -> j n", n=P), src.bitcast(F32)[b::NB, :]).then_inc(s["c2_out"], 16)
            sp.wait_ge(s["c2_out"], 16 * 2 * NB)
            for i in range(4):
                sp.wait_ge(s[f"st_out{i}"], 32 * PAIRS)
            meet()
            for c in range(DC):
                sp.dma_start(w1_raw[:, c, 0:E, :], rw1[:, c * P:c * P + P, :].rearrange("e p h -> p e h")).then_inc(s["l0_in"], 16)
                sp.dma_start(w1_raw[:, c, E, :], sw1[c * P:c * P + P, :]).then_inc(s["l0_in"], 16)
            sp.dma_start(w2_raw[:, 0:E, :], rw2.rearrange("e p n -> p e n")).then_inc(s["l0_in"], 16)
            sp.dma_start(w2_raw[:, E, :], sw2).then_inc(s["l0_in"], 16)
            for k in (0, E9):
                sp.dma_start(b2_raw[k:k + E, :], rb2).then_inc(s["l0_in"], 16)
                sp.dma_start(b2_raw[k + E:k + E9, :], sb2.rearrange("(a n) -> a n", a=1)).then_inc(s["l0_in"], 16)
            for g in range(GROUPS):
                sp.dma_start(XS[g].rearrange("(p r) d -> p r d", p=P),
                             zero4[:, :].rearrange("p (a d) -> p a d", a=1).to_broadcast([P, SLOTS[g], XW])).then_inc(s["zeroed"], 16)
            meet()

            def experts(g):
                sp.wait_ge(s["sc1"], 16 * (G0[g] + GT[g]))
                sp.wait_ge(s["sc2"], 16 * (G0[g] + GT[g]))
                base, n = SLOT0[g], SLOTS[g]

                def load(j, b, early=False):
                    if not early:
                        sp.wait_ge(s["e_xt"], base + j - 3)
                    sp.dma_start(xs[b], XS[g][bass.ds(j * P, P), :]).then_inc(s[f"xs_in{b}"], 16)

                def store(j, b):
                    sp.wait_ge(s["e_ys"], base + j + 1)
                    sp.dma_start(YS[g][bass.ds(j * P, P), :], ys[b]).then_inc(s[f"e_st{b}"], 16)

                for j in range(4):
                    load(j, j, True)
                load(4, 0)
                load(5, 1)
                loops = (n - 6) // 4
                with sp.Fori(0, loops) as h_:
                    i = h_ * 4
                    for r in range(4):
                        load(i + (r + 6), (r + 2) % 4)
                        store(i + r, r % 2)
                for j in range(4 * loops, n):
                    if j + 6 < n:
                        load(j + 6, (j + 6) % 4)
                    store(j, j % 2)
                for b in range(2):
                    sp.wait_ge(s[f"e_st{b}"], 8 * (base + n))

            for g in range(GROUPS):
                for b in BATCHES[g]:
                    k = b % 2
                    if b >= 2:
                        sp.wait_ge(s["a_o"], BT * (b - 1))
                    for dst, src in ((Ah, AD[0]), (Al, AD[1]), (Vh, VD[0]), (Vl, VD[1])):
                        sp.dma_start(dst[:, k, :, :].bitcast(F32), src[b]).then_inc(s[f"av_in{k}"], 16)
                    sp.dma_start(cb[k][:, :].bitcast(F32), CD[b]).then_inc(s[f"av_in{k}"], 16)
                if g == GROUPS - 1:
                    sp.wait_ge(s["a_xu"], TILES)
                    for e in range(E):
                        sp.dma_start(w13_sb[:, :, e, 0:H1], w1[e].rearrange("(c p) h -> p c h", p=P)).then_inc(s["l1_in"], 16)
                        sp.dma_start(w13_sb[:, :, e, H1:], w3[e].rearrange("(c p) h -> p c h", p=P)).then_inc(s["l1_in"], 16)
                        sp.dma_start(w2_sb[:, :, e, :], w2[e].rearrange("(c p) n -> p c n", p=P)).then_inc(s["l1_in"], 16)
                meet()
            experts(0)
            meet()
            experts(1)
            meet()
            for g in range(GROUPS):
                sp.wait_ge(s["gat2"], 16 * (G0[g] + GT[g]))
                for b in BATCHES[g]:
                    sp.dma_start(out[b].rearrange("(t p) d -> p t d", p=P), X[:, b * BT:b * BT + BT, :]).then_inc(s["stored"], 16)
            sp.wait_ge(s["stored"], 16 * NB)

        @block.gpsimd
        def _(po):
            po.memset(ident[:, :], 0.0)
            po.memset(upper[:, :], 0.0)
            po.memset(ones_b[:, :], 1.0)
            po.memset(ones8[:, :], 1.0)
            po.memset(ones[:, :], 1.0)
            po.memset(segm[:, :, :], 1.0)
            po.memset(ones2[:, :].bitcast(F32), 1.0)
            po.iota(prio[:, :], pattern=[[-1, E]], base=E, channel_multiplier=0,
                    allow_small_or_imprecise_dtypes=True)
            po.iota(thr[:, :], pattern=[[P, GM]], base=0, channel_multiplier=0,
                    allow_small_or_imprecise_dtypes=True)
            po.iota(slotno[:, :], pattern=[[1, SM]], base=0, channel_multiplier=0,
                    allow_small_or_imprecise_dtypes=True)
            po.memset(zero4[:, :], 0.0)
            po.drain()
            for g in range(GROUPS):
                po.memset(segm[:, g, 0:E * GT[g]].rearrange("p (e t) -> p e t", e=E)[:, :, 0:1], 0.0)
            po.affine_select(out=ident[:, :], in_=ident[:, :], compare_op=ALU.not_equal, fill=1.0,
                             base=0, pattern=[[-1, P]], channel_multiplier=1)
            po.affine_select(out=upper[:, :], in_=upper[:, :], compare_op=ALU.is_ge, fill=1.0,
                             base=0, pattern=[[-1, P]], channel_multiplier=1)
            po.drain()
            po.memset(segones, 0.0)
            po.drain()
            for k in range(2):
                po.memset(kbd[k], 0.0)
                po.memset(vbd[k], 0.0)
            po.drain()
            po.memset(segones[:, 0:S], 1.0)
            po.drain()
            po.sem_inc(s["consts"], 2)
            po.wait_ge(s["c_sb"], 1)
            k = S // RATE

            def put(b):
                po.wait_ge(s["s_norm"], b + 1)
                po.dma_start(N0[P - k:P, b * BT + 3, :], C[k * b:k * b + k, :]).then_inc(s["c_put"], 16)

            for j in range(PAIRS):
                if j % 2 == 0:
                    put(j // 2)
                for i in range(4):
                    po.wait_ge(s["st_hr"], 4 * j + i + 1)
                    if j:
                        po.wait_ge(s[f"st_out{i}"], 32 * j)
                    po.tensor_tensor(st_l[i], st_r[i], st_h[i].bitcast(F32), ALU.subtract).then_inc(s["st_lo"], 1)
            po.wait_ge(s["c2_h"], 1)
            po.tensor_tensor(c_l, c_r, c_h.bitcast(F32), ALU.subtract).then_inc(s["c2_l"], 1)

            def after(n):
                for other in ("bar_pe", "bar_act", "bar_dve", "bar_sp"):
                    po.wait_ge(s[other], n)

            after(1)
            po.wait_ge(s["l0_in"], 16 * 10)
            for raw, high, low in ((w1_raw, w1h[:, :, :, :], w1l[:, :, :, :]), (w2_raw, w2h[:, :, :], w2l[:, :, :])):
                po.tensor_copy(high, raw)
                po.drain()
                last = po.tensor_tensor(low, raw, high.bitcast(F32), ALU.subtract)
                last.then_inc(s["l_w"], 1)
            after(2)
            po.memset(N[:, :, D:XW], 0.0)
            po.drain()
            po.sem_inc(s["consts"], 1)

            def softmax_scale(tiles):
                def scale(n, b):
                    po.wait_ge(s["a_sm"], n + 1)
                    v = pr[b].rearrange("p (h n) -> p h n", n=S)
                    po.tensor_tensor(v, v, sm[b][:, :].rearrange("p (a b) -> p a b", b=1).to_broadcast([P, NHEAD, S]),
                                     ALU.mult).then_inc(s["a_pn"], 1)
                with po.Fori(tiles[0] // 2, tiles[1] // 2) as h_:
                    for b in range(2):
                        scale(h_ * 2 + b, b)

            def scatter(g):
                t0, n = G0[g], GT[g]
                if g == 0:
                    po.wait_ge(s["zeroed"], 16 * GROUPS)
                po.wait_ge(s["rout"], g + 1)
                for k in range(2):
                    if k == 1:
                        po.tensor_copy(N[:, t0:t0 + n, D:D + 1], wt[1][:, t0:t0 + n].rearrange("p (t a) -> p t a", a=1))
                        po.drain()
                    for t in range(t0, t0 + n):
                        po.indirect_dma_start(
                            XS[g], bass.IndirectOffsetOnAxis(ap=slot[k][:, t:t + 1], axis=0),
                            N[:, t, :], None).then_inc(s[f"sc{k + 1}"], 16)
                    po.wait_ge(s[f"sc{k + 1}"], 16 * (t0 + n))

            def gather(g):
                t0, n = G0[g], GT[g]
                for b in range(2):
                    po.wait_ge(s[f"e_st{b}"], 8 * (SLOT0[g] + SLOTS[g]))
                for k in range(2):
                    for t in range(t0, t0 + n):
                        po.indirect_dma_start(
                            X[:, t, :], None, YS[g],
                            bass.IndirectOffsetOnAxis(ap=slot[k][:, t:t + 1], axis=0),
                            compute_op=ALU.add).then_inc(s[f"gat{k + 1}"], 16)
                    po.wait_ge(s[f"gat{k + 1}"], 16 * (t0 + n))

            softmax_scale((G0[0], G0[0] + GT[0]))
            scatter(0)
            softmax_scale((G0[1], G0[1] + GT[1]))
            scatter(1)
            gather(0)
            gather(1)

        @block.tensor
        def _(pe):
            meet = Marks(pe, "bar_pe").meet

            def mm(o, l, r, start, stop):
                return nc.tensor.matmul(o, l, r, start=start, stop=stop)

            pe.wait_ge(s["consts"], 2)
            pe.wait_ge(s["ctx_in"], 16)
            for q in range(2):
                for c in range(DC):
                    last = nc.tensor.transpose(bank[0][:, 256 * c + P * q:256 * c + P * q + P],
                                               CT[:, q, c * P:c * P + P], ident[:, :])
            last.then_inc(s["pre_t"], 1)
            pe.wait_ge(s["qk_in"], 32)
            for m in range(4):
                if m >= 2:
                    pe.wait_ge(s["wqt_sb"], m - 1)
                for h in range(2):
                    for c in range(DC):
                        last = nc.tensor.transpose(bank[1 + m % 2][:, 256 * h + P * c:256 * h + P * c + P],
                                                   wq_sb[:, c, (2 * m + h) * P:(2 * m + h + 1) * P], ident[:, :])
                last.then_inc(s["wqt_p"], 1)
            pe.wait_ge(s["u_norm"], 1)
            for q in range(2):
                for c in range(DC):
                    last = nc.tensor.transpose(bank[3][:, 256 * c + P * q:256 * c + P * q + P],
                                               U[:, q, c * P:c * P + P], ident[:, :])
            last.then_inc(s["ut_p"], 1)
            pe.wait_ge(s["ut_sb"], 1)
            pe.wait_ge(s["small_in"], 16 * SMALL)
            for k in range(RATE):
                for c in range(DC):
                    mm(bank[4][0:S, 0:D], UT[:, c, k::RATE], convw_sb[:, k, c, :], k == 0 and c == 0, False)
            mm(bank[4][0:S, 0:D], ones[64:65, 0:S], rows[:, 0:D], False, True).then_inc(s["c_p"], 1)

            pe.wait_ge(s["pre_ts"], 1)
            pe.wait_ge(s["wqt_sb"], 4)
            pe.wait_ge(s["vo_in"], 32)
            for j in range(PAIRS):
                if j >= 1:
                    pe.wait_ge(s["k_sb"], j)
                for c in range(DC):
                    last = mm(bank[0][:, 0:256], wk_sb[:, c, j * P:j * P + P], ctxT[:, c, :], c == 0, c == DC - 1)
                last.then_inc(s["k_p"], 1)
                if j >= 1:
                    pe.wait_ge(s["v_sb"], j)
                if j == 0:
                    pe.wait_ge(s["ut_sb"], 1)
                for c in range(DC):
                    last = mm(bank[1][:, 0:256], wv_sb[:, c, j * P:j * P + P], ctxT[:, c, :], c == 0, c == DC - 1)
                last.then_inc(s["v_p"], 1)
                pe.wait_ge(s["k_sb"], j + 1)
                for c in range(DC):
                    if j >= 1:
                        pe.wait_ge(s["st_hr"], 4 * (j - 1) + c + 1)
                    mm(bank[2 + c], wqT[:, j, c * P:c * P + P], kbd[j % 2], True, True).then_inc(s["a_p"], 1)
                for b in range(NB):
                    last = mm(bank[7][:, NB * j + b:NB * j + b + 1], kbd[j % 2][:, b * P:b * P + P], bcols[:, 0, j:j + 1], True, True)
                last.then_inc(s["c2_p"], 1)
                pe.wait_ge(s["v_sb"], j + 1)
                for h in range(2):
                    if j >= 1:
                        pe.wait_ge(s["st_hr"], 4 * (j - 1) + DC + h + 1)
                    for b in (2 * h, 2 * h + 1):
                        o = bank[5 + h][:, 256 * (b % 2):256 * (b % 2) + 256]
                        last = mm(o, vbd[j % 2][:, b * P:b * P + P], wo_sb[:, j, :], True, j > 0)
                        if j == 0:
                            last = mm(o, segones, rows[:, D:2 * D], False, True)
                    last.then_inc(s["vw_p"], 1)
            pe.wait_ge(s["c2_c"], 1)
            nc.tensor.transpose(bank[4][0:PAIRS * NB, 0:P], c_col, ident[:, :]).then_inc(s["c2_t"], 1)
            meet()

            def layer0():
                def rows_t(q):
                    pe.wait_ge(s["l_xn"], q + 1)
                    if q >= 2:
                        pe.wait_ge(s["l_xl"], q - 1)
                    for c in range(DC):
                        for t in range(QT):
                            last = nc.tensor.transpose(bank[2 * (q % 2) + c][:, t * P:t * P + P],
                                                       xnq[q % 2][:, t, c * P:c * P + P], ident[:, :])
                    last.then_inc(s["l_tp"], 1)

                def logits(q):
                    if q == 0:
                        pe.wait_ge(s["l_ro"], 1)
                    pe.wait_ge(s["l_xl"], q + 1)
                    if q >= 2:
                        pe.wait_ge(s["l_lt"], q - 1)
                    for i, (w, a) in enumerate(((roh, xh), (roh, xl), (rol, xh))):
                        for c in range(DC):
                            last = nc.tensor.matmul(bank[6 + q % 2][0:E, :], w[:, c, :], a[:, q, c, :],
                                                    start=i == c == 0, stop=i == 2 and c == DC - 1)
                    last.then_inc(s["l_lg"], 1)

                def turn(q):
                    pe.wait_ge(s["l_lt"], q + 1)
                    for t in range(QT):
                        last = nc.tensor.transpose(bank[5][:, (QT * q + t) * E:(QT * q + t) * E + E],
                                                   hsl[q % 2][0:E, t * P:t * P + P], ident[0:E, 0:E])
                    last.then_inc(s["l_lgt"], 1)

                for q in range(QUADS + 2):
                    if q < QUADS:
                        rows_t(q)
                    if 1 <= q <= QUADS:
                        logits(q - 1)
                    if q >= 2:
                        turn(q - 2)
                pe.wait_ge(s["l_cf"], 1)
                for q in range(QUADS):
                    for t in range(QT):
                        last = nc.tensor.transpose(bank[q][0:2 * E9, t * P:t * P + P],
                                                   cf[:, QT * q + t, :].bitcast(F32), ident[:, :])
                    last.then_inc(s["l_cft"], 1)
                pe.wait_ge(s["l_cfa"], 1)
                pe.wait_ge(s["l_cfd"], 1)
                pe.wait_ge(s["l_w"], 2)
                pe.wait_ge(s["l_b2"], 1)
                pe.wait_ge(s["l_sel"], 1)

                def up(n, u, q, v, e, early):
                    if e == 0:
                        pe.wait_ge(s["l_cfq"], q + 1)
                    if not early:
                        pe.wait_ge(s["l_hg"], n - 1)
                        pe.wait_ge(s["l_hs"], n - 1)
                    nc.tensor.matmul(bank[u % 2], sel[:, e, :], cfq[v][:, :], start=True, stop=True).then_inc(s["l_bc"], 1)
                    for i, (w, a) in enumerate(((w1h, xh), (w1h, xl), (w1l, xh))):
                        for c in range(DC):
                            last = nc.tensor.matmul(bank[3 + u % 2], w[:, c, e, :],
                                                    a[:, bass.ds(q, 1), c, :].rearrange("p a n -> p (a n)"),
                                                    start=i == c == 0, stop=i == 2 and c == DC - 1)
                    last.then_inc(s["l_h"], 1)

                def down(n, u, q, v, e, early):
                    pe.wait_ge(s["l_hl"], n + 1)
                    if e == 0 and not early:
                        pe.wait_ge(s["l_xu"], q - 1)
                    for t in range(QT):
                        o = bank[(6, 7, 2, 5)[2 * v + t // 2]][:, D * (t % 2):D * (t % 2) + D]
                        if e == 0:
                            for w in (b2h, b2l):
                                nc.tensor.matmul(o, cfq[v][:, t * P:t * P + P], w[:, :],
                                                 start=t % 2 == 0 and w is b2h, stop=False, skip_group_check=True)
                        for a, w in ((hh, w2h), (hl, w2h), (hh, w2l)):
                            last = nc.tensor.matmul(o, a[u % 2][:, t * P:t * P + P], w[:, e, :],
                                                    start=False, stop=False, skip_group_check=True)
                    last.then_inc(s["l_y"], 1)

                def pair(h, first):
                    for u in range(2 * E9):
                        up(h * (2 * E9) + u, u, h * 2 + u // E9, u // E9, u % E9, first and u < 2)
                        w = u - 2
                        if w >= 0:
                            down(h * (2 * E9) + w, w, h * 2 + w // E9, w // E9, w % E9, first)
                        elif not first:
                            down(h * (2 * E9) + w, w + 2 * E9, h * 2 - 1, 1, w + E9, False)

                pair(0, True)
                with pe.Fori(1, QUADS // 2) as h_:
                    pair(h_, False)
                for w in (2, 1):
                    down(UNITS - w, 2 * E9 - w, QUADS - 1, 1, E9 - w, False)

            def router(g):
                k0, quads, cols = G0[g] // QT, GT[g] // QT, E * GT[g]

                def rows_t(k):
                    pe.wait_ge(s["n_r"], k + 1)
                    if k >= 2:
                        pe.wait_ge(s["xt_a"], k - 1)
                        pe.wait_ge(s["xt_d"], k - 1)
                    for c in range(DC):
                        for t in range(QT):
                            last = nc.tensor.transpose(bank[2 * (k % 2) + c][:, t * P:t * P + P],
                                                       N[:, k * QT + t, c * P:c * P + P], ident[:, :])
                    last.then_inc(s["t_p"], 1)

                rows_t(k0)
                for k in range(k0, k0 + quads):
                    if k + 1 < k0 + quads:
                        rows_t(k + 1)
                    pe.wait_ge(s["xt_a"], k + 1)
                    pe.wait_ge(s["xt_d"], k + 1)
                    if k:
                        pe.wait_ge(s["ro_sb"], k)
                    for t in range(QT):
                        for c in range(DC):
                            last = mm(bank[5][:, t * E:t * E + E], xnT4[k % 2][:, c, t * P:t * P + P], roT[1][:, c, :],
                                      c == 0, c == DC - 1)
                    last.then_inc(s["ro_p"], 1)
                pe.wait_ge(s["r_m"], g + 1)
                mm(bank[6][:, 0:cols], upper[:, :], M[:, 0:cols], True, True)
                mm(bank[7][:, 0:cols], ones_b[:, :], M[:, 0:cols], True, True).then_inc(s["r_pt"], 1)

            def experts(g):
                base, tiles = SLOT0[g], SLOTS[g]

                def xpose(j, b, b4, early=False):
                    pe.wait_ge(s[f"xs_in{b4}"], (j - b4) * 4 + 16 * (base // 4 + 1))
                    if not early:
                        pe.wait_ge(s["e_xt"], base + j)
                    for c in range(DC):
                        last = nc.tensor.transpose(bank[0][:, c * P:c * P + P], xs[b4][:, c * P:c * P + P], ident[:, :])
                    last.then_inc(s["e_tp"], 1)

                def up(j, b, early=False):
                    ex = pe.value_load(eid[0:1, g, bass.ds(j, 1)], min_val=0, max_val=E - 1)
                    pe.wait_ge(s["e_xt"], base + j + 1)
                    if not early:
                        pe.wait_ge(s["e_hg"], base + j - 1)
                    for half, sm_name in enumerate(("e_h", "e_g")):
                        for c in range(DC):
                            last = mm(bank[2 + 2 * half + b][:, 0:H1], xT[b][:, c, :],
                                      w13_sb[:, c, bass.ds(ex, 1), half * H1:half * H1 + H1].rearrange("p a n -> p (a n)"),
                                      c == 0, c == DC - 1)
                        last.then_inc(s[sm_name], 1)

                def hpose(j, b, early=False):
                    pe.wait_ge(s["e_hg"], base + j + 1)
                    if not early:
                        pe.wait_ge(s["e_ht"], base + j - 1)
                    for c in range(HC1):
                        last = nc.tensor.transpose(bank[6 + b][:, c * P:c * P + P], hs[b][:, c * P:c * P + P], ident[:, :])
                    last.then_inc(s["e_htp"], 1)

                def down(j, b, early=False):
                    ex = pe.value_load(eid[0:1, g, bass.ds(j, 1)], min_val=0, max_val=E - 1)
                    pe.wait_ge(s["e_ht"], base + j + 1)
                    if not early:
                        pe.wait_ge(s["e_ys"], base + j)
                    for c in range(HC1):
                        last = mm(bank[1][:, 0:D], hT[b][:, c, :], w2_sb[:, c, bass.ds(ex, 1), :].rearrange("p a n -> p (a n)"),
                                  c == 0, c == HC1 - 1)
                    last.then_inc(s["e_y"], 1)

                if g == 0:
                    pe.wait_ge(s["l1_in"], 48 * E)
                xpose(0, 0, 0, True)
                up(0, 0, True)
                xpose(1, 1, 1)
                up(1, 1, True)
                hpose(0, 0, True)
                xpose(2, 0, 2)
                up(2, 0)
                hpose(1, 1, True)
                xpose(3, 1, 3)
                down(0, 0, True)
                with pe.Fori(0, (tiles - 4) // 4) as h_:
                    i = h_ * 4
                    for r in range(4):
                        j, b = i + (r + 3), (r + 3) % 2
                        up(j, b)
                        hpose(i + (r + 2), 1 - b)
                        xpose(i + (r + 4), 1 - b, r)
                        down(i + (r + 1), b)
                z = tiles - 1
                up(z, 1)
                hpose(z - 1, 0)
                down(z - 2, 1)
                hpose(z, 1)
                down(z - 1, 0)
                down(z, 1)

            def attention(g):
                def xpose(n, b, first):
                    pe.wait_ge(s["a_xn"], n + 1)
                    if not first:
                        pe.wait_ge(s["a_xl"], n)
                    for c in range(DC):
                        last = nc.tensor.transpose(bank[6][:, c * P:c * P + P], xn_a[b][:, c * P:c * P + P], ident[:, :])
                    last.then_inc(s["a_tp"], 1)

                def logits(n, b, k, early):
                    pe.wait_ge(s["a_xl"], n + 1)
                    if not early:
                        pe.wait_ge(s["a_sub"], n - 1)
                    for h in range(2):
                        cols = slice(512 * h, 512 * h + 512)
                        nc.tensor.matmul(bank[2 * b + h], ones2[:, :], cb[k][:, cols], start=True, stop=False)
                        for i, (a, w) in enumerate(((xah, Ah), (xal, Ah), (xah, Al))):
                            for c in range(DC):
                                last = nc.tensor.matmul(bank[2 * b + h], a[b][:, c, :], w[:, k, c, cols],
                                                        start=False, stop=i == 2 and c == DC - 1)
                    last.then_inc(s["a_lg"], 1)

                def ppose(n, b, first):
                    pe.wait_ge(s["a_pn"], n + 1)
                    if not first:
                        pe.wait_ge(s["a_ph"], n * 2)
                        pe.wait_ge(s["a_pl"], n)
                    for c in range(PAIRS):
                        last = nc.tensor.transpose(bank[4 + c // 4][:, (c % 4) * P:(c % 4) * P + P], pr[b][:, c * P:c * P + P], ident[:, :])
                    last.then_inc(s["a_ptp"], 1)

                def values(n, k, first):
                    pe.wait_ge(s["a_pl"], n + 1)
                    if not first:
                        pe.wait_ge(s["a_xu"], n)
                    for i, (a, w) in enumerate(((prh, Vh), (prl, Vh), (prh, Vl))):
                        for c in range(PAIRS):
                            last = nc.tensor.matmul(bank[7][:, 0:D], a[:, c * P:c * P + P], w[:, k, c, :],
                                                    start=i == c == 0, stop=i == 2 and c == PAIRS - 1)
                    last.then_inc(s["a_o"], 1)

                n0, n1 = G0[g], G0[g] + GT[g]
                xpose(n0, 0, n0 == 0)
                for b_ in BATCHES[g]:
                    k, first = b_ % 2, b_ * BT
                    pe.wait_ge(s[f"av_in{k}"], 80 * (b_ // 2 + 1))
                    for r in range(2):
                        n = first + r
                        if n - 2 >= n0:
                            ppose(n - 2, r, False)
                        logits(n, r, k, n < 2)
                        xpose(n + 1, 1 - r, False)
                        if n - 2 >= n0:
                            values(n - 2, 1 - k, False)
                    from_h = first // 2 + 1
                    if b_ == 0:
                        for n in (2, 3):
                            ppose(n - 2, n % 2, n == 2)
                            logits(n, n % 2, k, False)
                            xpose(n + 1, 1 - n % 2, False)
                            values(n - 2, k, n == 2)
                        from_h += 1
                    with pe.Fori(from_h, (first + BT) // 2 - (b_ == BATCHES[g][-1])) as h_:
                        n = h_ * 2
                        for r in range(2):
                            ppose(n + (r - 2), r, False)
                            logits(n + r, r, k, False)
                            xpose(n + (r + 1), 1 - r, False)
                            values(n + (r - 2), k, False)
                for n in range(n1 - 2, n1 + 2):
                    ppose(n - 2, n % 2, False)
                    if n < n1:
                        logits(n, n % 2, k, False)
                    if n + 1 < n1:
                        xpose(n + 1, 1 - n % 2, False)
                    values(n - 2, k, False)

            layer0()
            meet()
            for g in range(GROUPS):
                attention(g)
                router(g)
                meet()
            experts(0)
            meet()
            experts(1)
            meet()

        @block.scalar
        def _(ac):
            meet = Marks(ac, "bar_act").meet
            act = nc.scalar.activation

            for dst, src in ((wk_sb, wk), (wq_sb, wq)):
                ac.dma_start(dst, src.rearrange("(c p) n -> p c n", p=P)).then_inc(s["qk_in"], 16)
            small = [(bcols[:, k, :], v.rearrange("(j p) -> p j", p=P)) for k, v in enumerate((bq, bk, bv))]
            small += [(rows[:, k * D:k * D + D], v.rearrange("(a n) -> a n", a=1)) for k, v in enumerate((conv_b, bo))]
            small += [(convw_sb[:, :, c, :], conv_w[:, c * P:c * P + P, :].rearrange("k p n -> p k n")) for c in range(DC)]
            small += [(b1c[:, 0:E], rb1.rearrange("e p -> p e")), (b1c[:, E:E9], sb1.rearrange("(p a) -> p a", a=1))]
            small += [(roT[1][:, :, :], wr.rearrange("(c p) e -> p c e", p=P)),
                      (rb_bc[:, :].rearrange("p (b e) -> p b e", b=4),
                       rout_b.rearrange("(a b e) -> a b e", a=1, b=1).to_broadcast([P, 4, E]))]
            small += [(roT[0][:, c, :], rout_w[:, c * P:c * P + P].rearrange("e p -> p e")) for c in range(DC)]
            assert len(small) == SMALL
            for dst, src in small:
                ac.dma_start(dst, src).then_inc(s["small_in"], 16)
            ac.dma_start(wv_sb, wv.rearrange("(c p) n -> p c n", p=P)).then_inc(s["vo_in"], 16)
            ac.dma_start(wo_sb, wo.rearrange("(j p) n -> p j n", p=P)).then_inc(s["vo_in"], 16)

            ac.wait_ge(s["pre_t"], 1)
            act(ctxT, bank[0].rearrange("p (c n) -> p c n", c=DC), ACT.Copy).then_inc(s["pre_ts"], 1)
            for m in range(4):
                ac.wait_ge(s["wqt_p"], m + 1)
                act(wqT[:, 2 * m:2 * m + 2, :], bank[1 + m % 2].rearrange("p (j n) -> p j n", j=2), ACT.Copy).then_inc(s["wqt_sb"], 1)
            ac.wait_ge(s["ut_p"], 1)
            act(UT, bank[3].rearrange("p (c n) -> p c n", c=DC), ACT.Copy).then_inc(s["ut_sb"], 1)
            ac.wait_ge(s["c_p"], 1)
            act(C, bank[4][0:S, 0:D], ACT.Copy).then_inc(s["c_sb"], 1)
            ac.wait_ge(s["consts"], 2)
            ac.wait_ge(s["small_in"], 16 * SMALL)
            for j in range(PAIRS):
                for kind, bk_, dst, psem, done, bcol in (("k", 0, kbd, "k_p", "k_sb", 1), ("v", 1, vbd, "v_p", "v_sb", 2)):
                    ac.wait_ge(s[psem], j + 1)
                    if j >= 2:
                        if kind == "k":
                            ac.wait_ge(s["c2_p"], j - 1)
                        else:
                            ac.wait_ge(s["vw_p"], 2 * (j - 1))
                    for h in range(2):
                        r = slice(DH * h, DH * h + DH)
                        last = act(dst[j % 2][r, :].rearrange("p (b n) -> p b n", b=NB)[:, :, S * h:S * h + S],
                                   bank[bk_][r, 0:256].rearrange("p (b n) -> p b n", b=NB),
                                   ACT.Identity, bias=bcols[r, bcol, j:j + 1])
                    last.then_inc(s[done], 1)
                for i in range(4):
                    ac.wait_ge(s["a_p" if i < DC else "vw_p"], DC * j + i % DC + 1)
                    if j:
                        ac.wait_ge(s["st_lo"], 4 * (j - 1) + i + 1)
                        ac.wait_ge(s[f"st_out{i}"], 32 * j)
                    bk_, sc = (bank[2 + i], DH ** -0.5) if i < DC else (bank[3 + i], 1.0)
                    act(st_r[i], bk_, ACT.Copy, scale=sc)
                    act(st_h[i], bk_, ACT.Copy, scale=sc)
                    ac.drain()
                    ac.sem_inc(s["st_hr"], 1)
            ac.wait_ge(s["c2_p"], PAIRS)
            act(c_col, bank[7][:, 0:PAIRS * NB], ACT.Copy, scale=DH ** -0.5).then_inc(s["c2_c"], 1)
            ac.wait_ge(s["c2_t"], 1)
            act(c_r, bank[4][0:PAIRS * NB, 0:P], ACT.Copy)
            act(c_h, bank[4][0:PAIRS * NB, 0:P], ACT.Copy)
            ac.drain()
            ac.sem_inc(s["c2_h"], 1)
            meet()

            def layer0():
                act(roh[:, :, :], roT[0][:, :, :], ACT.Copy).then_inc(s["l_xh"], 1)
                for q in range(QUADS + 1):
                    if q < QUADS:
                        ac.wait_ge(s["l_tp"], q + 1)
                        for c in range(DC):
                            act(xh[:, q, c, :], bank[2 * (q % 2) + c], ACT.Copy).then_inc(s["l_xh"], 1)
                    if q:
                        ac.wait_ge(s["l_lg"], q)
                        if q >= 3:
                            ac.wait_ge(s["l_lgt"], q - 2)
                        act(hsl[(q - 1) % 2][0:E, :], bank[6 + (q - 1) % 2][0:E, :], ACT.Copy).then_inc(s["l_lt"], 1)
                ac.wait_ge(s["l0_in"], 16 * 10)
                act(b2h[:, :], b2_raw[:, :], ACT.Copy).then_inc(s["l_b2h"], 1)
                ac.wait_ge(s["spa"], 1)
                act(wk2[:, :, :], wk1[:, :, :], ACT.Exp)
                ac.drain()
                act(wk2[:, :, :], wk2[:, :, :], ACT.Ln, bias=1.0).then_inc(s["spd"], 1)
                ac.wait_ge(s["l_w"], 2)
                for q in range(QUADS // 2):
                    ac.wait_ge(s["l_cft"], q + 1)
                    act(cfT[:, q, :], bank[q][0:2 * E9, :], ACT.Copy)
                ac.drain()
                ac.sem_inc(s["l_cfa"], 1)

                def quad(q, v, early):
                    if not early:
                        ac.wait_ge(s["l_y"], q * E9 - E9)
                    else:
                        ac.wait_ge(s["l_cfd"], 1)
                    act(cfq[v][:, :], cfT[:, bass.ds(q, 1), :].rearrange("p a n -> p (a n)"), ACT.Copy).then_inc(s["l_cfq"], 1)

                def unit(n, u, e, early):
                    ac.wait_ge(s["l_h"], n + 1)
                    if not early:
                        ac.wait_ge(s["l_hg"], n - 1)
                    act(hsl[u % 2][:, :], bank[3 + u % 2], ACT.Silu, bias=b1c[:, e:e + 1]).then_inc(s["l_hs"], 1)
                    ac.wait_ge(s["l_hg"], n + 1)
                    if not early:
                        ac.wait_ge(s["l_y"], n - 1)
                    act(hh[u % 2][:, :], hg[u % 2][:, :], ACT.Copy).then_inc(s["l_hh"], 1)

                def pair(h, first):
                    for u in range(2 * E9):
                        if u % E9 == 0:
                            quad(h * 2 + u // E9, u // E9, first)
                        unit(h * (2 * E9) + u, u, u % E9, first and u < 2)

                pair(0, True)
                with ac.Fori(1, QUADS // 2) as h_:
                    pair(h_, False)

            def router(g):
                for k in range(G0[g] // QT, (G0[g] + GT[g]) // QT):
                    ac.wait_ge(s["t_p"], k + 1)
                    if k >= 2:
                        ac.wait_ge(s["ro_p"], k - 1)
                    act(xnT4[k % 2][:, 0, :], bank[2 * (k % 2)], ACT.Copy).then_inc(s["xt_a"], 1)
                ac.wait_ge(s["spa"], g + 2)
                w = wt[1][:, G0[g]:G0[g] + GT[g]]
                act(w, w, ACT.Exp).then_inc(s["spd"], 1)

            def experts(g):
                base, tiles = SLOT0[g], SLOTS[g]

                def xcopy(j, b, b4, early=False, fresh=False):
                    ac.wait_ge(s["e_tp"], base + j + 1)
                    if not early:
                        ac.wait_ge(s["e_g"], base + j - 1)
                    if not fresh:
                        ac.wait_ge(s["e_ys"], base + j - 3)
                    act(wcol[:, b4:b4 + 1], xs[b4][:, D:D + 1], ACT.Copy)
                    act(xT[b], bank[0][:, 0:D].rearrange("p (c n) -> p c n", c=DC), ACT.Copy).then_inc(s["e_xt"], 1)

                def silu(j, b, early=False):
                    ac.wait_ge(s["e_h"], base + j + 1)
                    if not early:
                        ac.wait_ge(s["e_htp"], base + j - 1)
                    act(hs[b], bank[2 + b][:, 0:H1], ACT.Silu).then_inc(s["e_hs"], 1)

                def scale(j, b, b4, early=False):
                    ac.wait_ge(s["e_y"], base + j + 1)
                    if not early:
                        ac.wait_ge(s[f"e_st{b}"], (j - b) * 8 + 8 * base)
                    act(ys[b], bank[1][:, 0:D], ACT.Copy, scale=wcol[:, b4:b4 + 1]).then_inc(s["e_ys"], 1)

                xcopy(0, 0, 0, True, True)
                silu(0, 0, True)
                xcopy(1, 1, 1, True, True)
                silu(1, 1, True)
                xcopy(2, 0, 2, False, True)
                silu(2, 0)
                xcopy(3, 1, 3, False, True)
                scale(0, 0, 0, True)
                silu(3, 1)
                xcopy(4, 0, 0)
                scale(1, 1, 1, True)
                loops = (tiles - 5) // 4
                with ac.Fori(0, loops) as h_:
                    i = h_ * 4
                    for r in range(4):
                        silu(i + (r + 4), r % 2)
                        xcopy(i + (r + 5), 1 - r % 2, (r + 1) % 4)
                        scale(i + (r + 2), r % 2, (r + 2) % 4)
                for j in range(4 * loops + 4, tiles):
                    silu(j, j % 2)
                    if j + 1 < tiles:
                        xcopy(j + 1, 1 - j % 2, (j + 1) % 4)
                    scale(j - 2, j % 2, (j - 2) % 4)
                scale(tiles - 2, 0, 2)
                scale(tiles - 1, 1, 3)

            def attention(g):
                def xhigh(n, b, early):
                    ac.wait_ge(s["a_tp"], n + 1)
                    if not early:
                        ac.wait_ge(s["a_lg"], n - 1)
                    act(xah[b][:, :, :], bank[6][:, 0:D].rearrange("p (c n) -> p c n", c=DC), ACT.Copy).then_inc(s["a_xh"], 1)

                def expo(n, b):
                    ac.wait_ge(s["a_sub"], n + 1)
                    act(pr[b], pr[b], ACT.Exp).then_inc(s["a_ex"], 1)

                def phigh(n, first):
                    ac.wait_ge(s["a_ptp"], n + 1)
                    if not first:
                        ac.wait_ge(s["a_o"], n)
                    for h in range(2):
                        act(prh[:, 512 * h:512 * h + 512], bank[4 + h], ACT.Copy).then_inc(s["a_ph"], 1)

                n0, n1 = G0[g], G0[g] + GT[g]
                e0 = 4 if n0 == 0 else 2
                xhigh(n0, 0, n0 == 0)
                for n in range(n0, n0 + e0):
                    if n - 2 >= n0:
                        phigh(n - 2, n == 2)
                    xhigh(n + 1, 1 - n % 2, n + 1 < 2)
                    expo(n, n % 2)
                with ac.Fori((n0 + e0) // 2, n1 // 2 - 1) as h_:
                    n = h_ * 2
                    for r in range(2):
                        phigh(n + (r - 2), False)
                        xhigh(n + (r + 1), 1 - r, False)
                        expo(n + r, r)
                for n in range(n1 - 2, n1 + 2):
                    phigh(n - 2, False)
                    if n + 1 < n1:
                        xhigh(n + 1, 1 - n % 2, False)
                    if n < n1:
                        expo(n, n % 2)

            layer0()
            meet()
            for g in range(GROUPS):
                attention(g)
                router(g)
                meet()
            experts(0)
            meet()
            experts(1)
            meet()

        @block.vector
        def _(ve):
            meet = Marks(ve, "bar_dve").meet
            tt, ts, stt = nc.vector.tensor_tensor, nc.vector.tensor_scalar, nc.vector.scalar_tensor_tensor

            def bc(v, n):
                return v.rearrange("p (a b) -> p a b", b=1).to_broadcast([P, v.shape[1], n])

            def rep(v, n):
                return v.rearrange("p (b a) -> p b a", b=1).to_broadcast([P, n, v.shape[1]])

            def rsqrt(o, v, tmp):
                ts(o.bitcast(I32), v.bitcast(I32), 1, None, ALU.logical_shift_right)
                ve.drain()
                ts(o.bitcast(I32), o.bitcast(I32), -1.0, MAGIC, ALU.mult, ALU.add)
                ve.drain()
                for _ in range(3):
                    stt(tmp, o, -0.5, v, ALU.mult, ALU.mult)
                    ve.drain()
                    tt(tmp, tmp, o, ALU.mult)
                    ve.drain()
                    stt(o, tmp, 1.5, o, ALU.add, ALU.mult)
                    ve.drain()

            def ln_finish(st_, w0, w1):
                w = w1 - w0
                a, b, c = ta[:, 0:w], tb[:, 0:w], tc_[:, 0:w]
                m, r = mean[:, w0:w1], rstd[:, w0:w1]

                def col(k):
                    return st_[:, w0:w1, k:k + 1].rearrange("p t a -> p (t a)")

                ve.drain()
                tt(a, col(1), col(4), ALU.add)
                tt(b, col(1), col(4), ALU.subtract)
                tt(c, col(2), col(5), ALU.add)
                ve.drain()
                ts(m, a, 0.5, None, ALU.mult)
                tt(b, b, b, ALU.mult)
                ts(c, c, 1.0 / D, EPS, ALU.mult, ALU.add)
                ve.drain()
                stt(c, b, 0.25, c, ALU.mult, ALU.add)
                ve.drain()
                rsqrt(r, c, a)

            def row_stats(st_, buf, t0, t1):
                with ve.Fori(t0 // 4, t1 // 4) as h_:
                    i = h_ * 4
                    for u in range(4):
                        nc.vector.bn_stats(st_[:, bass.ds(i + u, 1), :].rearrange("p a n -> p (a n)"),
                                           buf[:, bass.ds(i + u, 1), :].rearrange("p a n -> p (a n)"))

            ve.wait_ge(s["u_in"], 16 * NB)
            for q in range(2):
                nc.vector.bn_stats(stats[:, q, :], U[:, q, :])
            ln_finish(stats, 0, 2)
            for q in range(2):
                last = ts(U[:, q, :], U[:, q, :], mean[:, q:q + 1], rstd[:, q:q + 1], ALU.subtract, ALU.mult)
            last.then_inc(s["u_norm"], 1)

            for b in range(NB):
                t0, t1 = b * BT, b * BT + BT
                ve.wait_ge(s[f"s_in{b}"], 16 * 4)
                row_stats(stats, N0, t0, t1)
                ln_finish(stats, t0, t1)
                for t in range(t0, t1):
                    r = S if t == t1 - 1 else P
                    v = N0[0:r, t, :]
                    last = ts(v, v, mean[0:r, t:t + 1], rstd[0:r, t:t + 1], ALU.subtract, ALU.mult)
                last.then_inc(s["s_norm"], 1)
                ve.wait_ge(s["c_put"], 16 * (b + 1))
                ve.wait_ge(s[f"x_in{b}"], 16)
                v = X[:, t0:t1, :]
                tt(v, v, N0[:, t0:t1, :], ALU.add)
                ve.drain()
                row_stats(xstats, X, t0, t1)
            meet()

            def first_max(src, m, oh, tiles):
                h = hot[:, 0:tiles]
                nc.vector.tensor_reduce(m, src, AX.X, ALU.max)
                ve.drain()
                tt(oh, src, bc(m, E), ALU.is_equal)
                ve.drain()
                tt(oh, oh, rep(prio[:, :], tiles), ALU.mult)
                ve.drain()
                nc.vector.tensor_reduce(h, oh, AX.X, ALU.max)
                ve.drain()
                tt(oh, oh, bc(h, E), ALU.is_equal)
                ve.drain()

            def top2(tiles):
                def fl(v):
                    return v[:, 0:tiles, :].rearrange("p t e -> p (t e)")
                first_max(L[:, 0:tiles, :], m1[:, 0:tiles], oh1[:, 0:tiles, :], tiles)
                stt(fl(wk1), fl(oh1), -3.0e38, fl(L), ALU.mult, ALU.add)
                ve.drain()
                first_max(wk1[:, 0:tiles, :], m2[:, 0:tiles], oh2[:, 0:tiles, :], tiles)

            def layer0():
                ve.wait_ge(s["l_xh"], 1)
                tt(rol[:, :, :], roT[0][:, :, :], roh[:, :, :].bitcast(F32), ALU.subtract).then_inc(s["l_ro"], 1)
                k2 = 2 * E9

                def plane(o):
                    return ident[0:k2, o:o + E9].rearrange("p (e a) -> p e a", a=1).to_broadcast([k2, E9, P])
                tt(sel[:, :, :], plane(0), plane(E9), ALU.add).then_inc(s["l_sel"], 1)
                ln_finish(xstats, 0, TILES)

                def rows_in(q):
                    if q >= 2:
                        ve.wait_ge(s["l_tp"], q - 1)
                    for t in range(QT):
                        u = QT * q + t
                        last = ts(xnq[q % 2][:, t, :], X[:, u, :], mean[:, u:u + 1], rstd[:, u:u + 1], ALU.subtract, ALU.mult)
                    last.then_inc(s["l_xn"], 1)

                rows_in(0)
                for q in range(QUADS):
                    if q + 1 < QUADS:
                        rows_in(q + 1)
                    for c in range(DC):
                        ve.wait_ge(s["l_xh"], DC * q + c + 2)
                        last = tt(xl[:, q, c, :], bank[2 * (q % 2) + c], xh[:, q, c, :].bitcast(F32), ALU.subtract)
                    last.then_inc(s["l_xl"], 1)
                ve.wait_ge(s["l_b2h"], 1)
                tt(b2l[:, :], b2_raw[:, :], b2h[:, :].bitcast(F32), ALU.subtract).then_inc(s["l_b2"], 1)
                ve.wait_ge(s["l_lgt"], QUADS)
                for k in range(QUADS):
                    tt(L[:, QT * k:QT * k + QT, :].rearrange("p t e -> p (t e)"), bank[5][:, QT * E * k:QT * E * k + QT * E], rb_bc[:, :], ALU.add)
                ve.drain()
                flat = "p t e -> p (t e)"
                Lv = L[:, :, :]
                ts(wk1[:, :, :], Lv, -1.0, None, ALU.mult)
                ve.drain()
                tt(wk1[:, :, :], wk1[:, :, :], Lv, ALU.min).then_inc(s["spa"], 1)
                ve.wait_ge(s["spd"], 1)
                ve.drain()
                stt(wk1[:, :, :].rearrange(flat), Lv.rearrange(flat), 0.0, wk2[:, :, :].rearrange(flat), ALU.max, ALU.add)
                ve.drain()
                rsqrt(wk2[:, :, :].rearrange(flat), wk1[:, :, :].rearrange(flat), ta[:, :])
                tt(Lv, wk1[:, :, :], wk2[:, :, :], ALU.mult)
                ve.drain()
                top2(TILES)
                tt(wk1[:, :, :], oh1[:, :, :], oh2[:, :, :], ALU.add)
                nc.vector.memset(cf[:, :, E:E9].bitcast(F32), 1.0)
                nc.vector.memset(cf[:, :, E9 + E:].bitcast(F32), 0.0)
                ve.drain()
                tt(wk1[:, :, :], wk1[:, :, :], Lv, ALU.mult)
                ve.drain()
                nc.vector.tensor_copy(cf[:, :, 0:E], wk1[:, :, :])
                ve.drain()
                tt(cf[:, :, E9:E9 + E], wk1[:, :, :], cf[:, :, 0:E].bitcast(F32), ALU.subtract)
                ve.drain()
                ve.sem_inc(s["l_cf"], 1)
                ve.wait_ge(s["l_w"], 2)
                for q in range(QUADS // 2, QUADS):
                    ve.wait_ge(s["l_cft"], q + 1)
                    nc.vector.tensor_copy(cfT[:, q, :], bank[q][0:2 * E9, :])
                ve.drain()
                ve.sem_inc(s["l_cfd"], 1)

                def unit(n, u, early):
                    ve.wait_ge(s["l_bc"], n + 1)
                    ve.wait_ge(s["l_hs"], n + 1)
                    if not early:
                        ve.wait_ge(s["l_hl"], n - 1)
                        ve.wait_ge(s["l_hh"], n - 1)
                    tt(hg[u % 2][:, :], bank[u % 2], hsl[u % 2][:, :], ALU.mult).then_inc(s["l_hg"], 1)
                    ve.wait_ge(s["l_hh"], n + 1)
                    if not early:
                        ve.wait_ge(s["l_y"], n - 1)
                    tt(hl[u % 2][:, :], hg[u % 2][:, :], hh[u % 2][:, :].bitcast(F32), ALU.subtract).then_inc(s["l_hl"], 1)

                def add(n, q, v):
                    ve.wait_ge(s["l_y"], n + 1)
                    for h in range(2):
                        x2 = X[:, bass.ds(q * QT + 2 * h, 2), :].rearrange("p t n -> p (t n)")
                        last = tt(x2, bank[(6, 7, 2, 5)[2 * v + h]], x2, ALU.add)
                    last.then_inc(s["l_xu"], 1)
                    ve.drain()
                    for t in range(QT):
                        nc.vector.bn_stats(xstats[:, bass.ds(q * QT + t, 1), :].rearrange("p a n -> p (a n)"),
                                           X[:, bass.ds(q * QT + t, 1), :].rearrange("p a n -> p (a n)"))

                def pair(h, first):
                    for u in range(2 * E9):
                        n = h * (2 * E9) + u
                        unit(n, u, first and u < 2)
                        if u % E9 == 1 and not (first and u < E9):
                            add(n + (-2), h * 2 + (u // E9 - 1), 1 - u // E9)

                pair(0, True)
                with ve.Fori(1, QUADS // 2) as h_:
                    pair(h_, False)
                add(UNITS - 1, QUADS - 1, 1)

            def router(g):
                t0, n, k0 = G0[g], GT[g], G0[g] // QT
                quads, cols = n // QT, E * n
                ln_finish(xstats, t0, t0 + n)
                if g == 0:
                    ve.wait_ge(s["consts"], 3)

                def rows_in(k):
                    for t in range(QT * k, QT * k + QT):
                        last = ts(N[:, t, 0:D], X[:, t, :], mean[:, t:t + 1], rstd[:, t:t + 1], ALU.subtract, ALU.mult)
                    last.then_inc(s["n_r"], 1)

                def logits(k):
                    ve.wait_ge(s["ro_p"], k + 1)
                    q = k - k0
                    nc.vector.tensor_copy(L[:, QT * q:QT * q + QT, :].rearrange("p t e -> p (t e)"), bank[5][:, 0:QT * E]).then_inc(s["ro_sb"], 1)

                rows_in(k0)
                for k in range(k0, k0 + quads):
                    if k + 1 < k0 + quads:
                        rows_in(k + 1)
                    ve.wait_ge(s["t_p"], k + 1)
                    if k >= 2:
                        ve.wait_ge(s["ro_p"], k - 1)
                    nc.vector.tensor_copy(xnT4[k % 2][:, 1, :], bank[2 * (k % 2) + 1]).then_inc(s["xt_d"], 1)
                    if k > k0:
                        logits(k - 1)
                logits(k0 + quads - 1)
                ve.drain()
                top2(n)
                M3 = M[:, 0:cols].rearrange("p (e t) -> p t e", e=E)
                tt(M3, oh1[:, 0:n, :], oh2[:, 0:n, :], ALU.add).then_inc(s["r_m"], 1)
                w0, w1_ = wt[0][:, t0:t0 + n], wt[1][:, t0:t0 + n]
                tt(w1_, m2[:, 0:n], m1[:, 0:n], ALU.subtract).then_inc(s["spa"], 1)
                ve.wait_ge(s["spd"], g + 2)
                ts(w0, w1_, 1.0, None, ALU.add)
                ve.drain()
                nc.vector.reciprocal(w0, w0)
                ve.drain()
                tt(w1_, w1_, w0, ALU.mult)
                ve.drain()
                nc.vector.tensor_copy(N[:, t0:t0 + n, D:D + 1], w0.rearrange("p (t a) -> p t a", a=1))
                ve.wait_ge(s["r_pt"], g + 1)
                e3 = "p (e t) -> p e t"
                ta_, tb_, tot_, inc_ = ta[:, 0:cols], tb[:, 0:cols], tot[:, 0:cols], inc[:, 0:cols]
                nc.vector.tensor_copy(tot_, bank[7][:, 0:cols])
                ve.drain()
                nc.vector.tensor_tensor_scan(inc_, segm[:, g, 0:cols], tot_, 0.0, ALU.mult, ALU.add)
                ve.drain()
                last_t = inc_.rearrange(e3, e=E)[:, :, n - 1:n]
                tt(ta_.rearrange(e3, e=E), last_t.to_broadcast([P, E, n]), rep(thr[:, 0:n], E), ALU.is_gt)
                tt(tb_, inc_, tot_, ALU.subtract)
                ve.drain()
                nc.vector.tensor_reduce(te[:, :], ta_.rearrange(e3, e=E), AX.X, ALU.add)
                tt(tb_, bank[6][:, 0:cols], tb_, ALU.add)
                ve.drain()
                nc.vector.tensor_tensor_scan(ti[:, :], ones8[:, :], te[:, :], 0.0, ALU.mult, ALU.add)
                ve.drain()
                tt(te[:, :], ti[:, :], te[:, :], ALU.subtract)
                cm = cmp[:, 0:SLOTS[g] * E].rearrange("p (j e) -> p j e", e=E)
                tt(cm, bc(slotno[:, 0:SLOTS[g]], E), rep(ti[:, :], SLOTS[g]), ALU.is_ge)
                ve.drain()
                tb3 = tb_.rearrange(e3, e=E)
                stt(tb3, bc(te[:, :], n), float(P), tb3, ALU.mult, ALU.add)
                nc.vector.tensor_reduce(eid_f[:, 0:SLOTS[g]], cm, AX.X, ALU.add)
                ve.drain()
                ts(eid[:, g, 0:SLOTS[g]], eid_f[:, 0:SLOTS[g]], float(E - 1), None, ALU.min)
                for k, oh in enumerate((oh1, oh2)):
                    tt(wk1[:, 0:n, :], oh[:, 0:n, :], tb3.rearrange("p e t -> p t e"), ALU.mult)
                    ve.drain()
                    nc.vector.tensor_reduce(hot[:, 0:n], wk1[:, 0:n, :], AX.X, ALU.add)
                    ve.drain()
                    nc.vector.tensor_copy(slot[k][:, t0:t0 + n], hot[:, 0:n])
                ve.drain()
                ve.sem_inc(s["rout"], 1)

            def experts(g):
                base, tiles = SLOT0[g], SLOTS[g]

                def gate(j, b):
                    ve.wait_ge(s["e_hs"], base + j + 1)
                    ve.wait_ge(s["e_g"], base + j + 1)
                    tt(hs[b], bank[4 + b][:, 0:H1], hs[b], ALU.mult).then_inc(s["e_hg"], 1)

                def hcopy(j, b, early=False):
                    ve.wait_ge(s["e_htp"], base + j + 1)
                    if not early:
                        ve.wait_ge(s["e_y"], base + j - 1)
                    nc.vector.tensor_copy(hT[b].rearrange("p c n -> p (c n)"), bank[6 + b][:, 0:H1]).then_inc(s["e_ht"], 1)

                gate(0, 0)
                gate(1, 1)
                hcopy(0, 0, True)
                gate(2, 0)
                hcopy(1, 1, True)
                gate(3, 1)
                hcopy(2, 0)
                with ve.Fori(2, tiles // 2) as h_:
                    i = h_ * 2
                    for b in range(2):
                        gate(i + b, b)
                        hcopy(i + (b - 1), 1 - b)
                hcopy(tiles - 1, 1)

            def attention(g):
                def row(v, n):
                    return v[:, bass.ds(n, 1), :].rearrange("p a n -> p (a n)")

                def rows_in(n, b, early):
                    if not early:
                        ve.wait_ge(s["a_tp"], n - 1)
                    ts(xn_a[b], row(X, n), mean[:, bass.ds(n, 1)], rstd[:, bass.ds(n, 1)], ALU.subtract, ALU.mult).then_inc(s["a_xn"], 1)

                def xlow(n, b, early):
                    ve.wait_ge(s["a_xh"], n + 1)
                    if not early:
                        ve.wait_ge(s["a_lg"], n - 1)
                    tt(xal[b][:, :, :], bank[6][:, 0:D].rearrange("p (c n) -> p c n", c=DC), xah[b][:, :, :].bitcast(F32),
                       ALU.subtract).then_inc(s["a_xl"], 1)

                def shift(n, b, early):
                    ve.wait_ge(s["a_lg"], n + 1)
                    if not early:
                        ve.wait_ge(s["a_ptp"], n - 1)
                    lg = psum[:, 2 * b:2 * b + 2, :].rearrange("p a (h n) -> p (a h) n", n=S)
                    nc.vector.tensor_reduce(mx[:, :], lg, AX.X, ALU.max)
                    ve.drain()
                    tt(pr[b].rearrange("p (h n) -> p h n", n=S), lg, bc(mx[:, :], S), ALU.subtract).then_inc(s["a_sub"], 1)

                def sums(n, b):
                    ve.wait_ge(s["a_ex"], n + 1)
                    nc.vector.tensor_reduce(sm[b][:, :], pr[b].rearrange("p (h n) -> p h n", n=S), AX.X, ALU.add)
                    ve.drain()
                    nc.vector.reciprocal(sm[b][:, :], sm[b][:, :]).then_inc(s["a_sm"], 1)

                def plow(n, first):
                    for h in range(2):
                        ve.wait_ge(s["a_ph"], n * 2 + (h + 1))
                        if h == 0 and not first:
                            ve.wait_ge(s["a_o"], n)
                        cols = slice(512 * h, 512 * h + 512)
                        last = tt(prl[:, cols], bank[4 + h], prh[:, cols].bitcast(F32), ALU.subtract)
                    last.then_inc(s["a_pl"], 1)

                def add(n):
                    ve.wait_ge(s["a_o"], n + 1)
                    tt(row(X, n), bank[7][:, 0:D], row(X, n), ALU.add).then_inc(s["a_xu"], 1)
                    ve.drain()
                    nc.vector.bn_stats(row(xstats, n), row(X, n))

                n0, n1 = G0[g], G0[g] + GT[g]
                e0 = 4 if n0 == 0 else 2
                if g == 0:
                    ln_finish(xstats, 0, TILES)
                    ve.drain()
                rows_in(n0, 0, n0 == 0)
                rows_in(n0 + 1, 1, n0 == 0)
                xlow(n0, 0, n0 == 0)
                for n in range(n0, n0 + e0):
                    if n - 2 >= n0:
                        plow(n - 2, n == 2)
                    if n > n0:
                        sums(n - 1, 1 - n % 2)
                    shift(n, n % 2, n < 2)
                    xlow(n + 1, 1 - n % 2, n + 1 < 2)
                    rows_in(n + 2, n % 2, False)
                    if n - 2 >= n0:
                        add(n - 2)
                with ve.Fori((n0 + e0) // 2, n1 // 2 - 1) as h_:
                    n = h_ * 2
                    for r in range(2):
                        plow(n + (r - 2), False)
                        sums(n + (r - 1), 1 - r)
                        shift(n + r, r, False)
                        xlow(n + (r + 1), 1 - r, False)
                        rows_in(n + (r + 2), r, False)
                        add(n + (r - 2))
                for n in range(n1 - 2, n1 + 2):
                    plow(n - 2, False)
                    if n - 1 < n1:
                        sums(n - 1, 1 - n % 2)
                    if n < n1:
                        shift(n, n % 2, False)
                    if n + 1 < n1:
                        xlow(n + 1, 1 - n % 2, False)
                    add(n - 2)
                ve.drain()

            layer0()
            meet()
            for g in range(GROUPS):
                attention(g)
                router(g)
                meet()
            experts(0)
            meet()
            experts(1)
            meet()


_INS = ['x', 'ctx_1024', 'L0_xattn_conv_w', 'L0_xattn_conv_b', 'L0_ffn_routing_W', 'L0_ffn_expert_bias', 'L0_ffn_sW1',
        'L0_ffn_sb1', 'L0_ffn_sW2', 'L0_ffn_sb2', 'L0_ffn_rW1', 'L0_ffn_rb1', 'L0_ffn_rW2', 'L0_ffn_rb2',
        'L1_xattn_Wq', 'L1_xattn_bq', 'L1_xattn_Wk', 'L1_xattn_bk', 'L1_xattn_Wv', 'L1_xattn_bv', 'L1_xattn_Wo',
        'L1_xattn_bo', 'L1_ffn_Wr', 'L1_ffn_W1', 'L1_ffn_W2', 'L1_ffn_W3']


def kernel(**inputs):
    import numpy as _np
    import concourse.bacc as _bacc
    from concourse import mybir as _mybir
    from concourse.bass_utils import run_bass_kernel_spmd as _run

    nc = _bacc.Bacc("TRN2", target_bir_lowering=False, num_devices=1)
    arrays, args = {}, []
    for name in _INS:
        a = _np.ascontiguousarray(inputs[name])
        arrays[f"in_{name}_dram"] = a
        args.append(nc.dram_tensor(f"in_{name}_dram", a.shape, _mybir.dt.from_np(a.dtype), kind="ExternalInput").ap())
    args.append(nc.dram_tensor("out_0_dram", (NB, T, D), _mybir.dt.float32, kind="ExternalOutput").ap())
    build(nc, *args)
    r = _run(nc, [arrays], core_ids=[0])
    return r.results[0]["out_0_dram"]
```

```python
from contextlib import ExitStack

import numpy as np
import concourse.bass as bass
from concourse import mybir

F32 = mybir.dt.float32
F32R = mybir.dt.float32r
BF16 = mybir.dt.bfloat16
I32 = mybir.dt.int32
ALU = mybir.AluOpType
ACT = mybir.ActivationFunctionType
AX = mybir.AxisListType

P = 128
NB, T, D = 4, 1024, 256
DC = D // P
S = 64
TILES = NB * T // P
BT = T // P
BATCHES = ((0, 1, 2), (3,))
GROUPS = len(BATCHES)
G0 = [g[0] * BT for g in BATCHES]
GT = [len(g) * BT for g in BATCHES]
GM = max(GT)
E = 8
E9 = E + 1
H0, H1 = 128, 384
QT = 4
QN = QT * P
QUADS = TILES // QT
UNITS = QUADS * E9
HC1 = H1 // P
XW = 260
SLOTS = [2 * n + E for n in GT]
SLOT0 = [sum(SLOTS[:g]) for g in range(GROUPS)]
SM = max(SLOTS)
SA = sum(SLOTS)
NHEAD, DH = 16, 64
PAIRS = NHEAD // 2
HK = NHEAD * S
CONV = 512
RATE = 4
DEEP = 3
EPS = 1e-5
SMALL = 5
REST = 6
MAGIC = 1597463007.0


def build(nc, x, ctx_in, conv_w, conv_b, rout_w, rout_b, sw1, sb1, sw2, sb2, rw1, rb1, rw2, rb2,
          wq, bq, wk, bk, wv, bv, wo, bo, wr, w1, w2, w3, out):
    st = ExitStack()
    with st:
        st.enter_context(nc.allow_non_contiguous_dma(reason="bias columns and router weights, small"))

        def sb(name, shape, dt=F32, stack=st):
            return stack.enter_context(nc.sbuf_tensor(name, shape, dt))

        def sem(name):
            return st.enter_context(nc.semaphore(name))

        X = sb("X", [P, TILES, D])
        crow = sb("crow", [65, 2 * D + P])
        zero4 = sb("zero4", [P, XW])
        def carve(mem, at, n, pattern=None, **k):
            v = mem[:, at:at + n]
            return v.rearrange(pattern, **k) if pattern else v

        ident = sb("ident", [P, P])
        ones = sb("ones", [P, P])
        upper = sb("upper", [P, P], BF16)
        ones_b = sb("ones_b", [P, P], BF16)
        bcols = sb("bcols", [P, 3, PAIRS])
        rows = crow[64:65, 0:2 * D]
        segones = crow[64:65, 2 * D:2 * D + P]
        roT = [sb(f"roT{l}", [P, DC, E]) for l in range(2)]
        rb_bc = sb("rb_bc", [P, E])
        prio = sb("prio", [P, E])
        stats = sb("stats", [P, TILES, 6])
        mean = sb("mean", [P, TILES])
        rstd = sb("rstd", [P, TILES])
        ta, tb, tc_ = (sb(n, [P, TILES * E]) for n in ("ta", "tb", "tc"))
        L = sb("L", [P, TILES, E])
        oh1, oh2, wk1, wk2 = (sb(n, [P, TILES, E]) for n in ("oh1", "oh2", "wk1", "wk2"))
        m1, m2, hot = (sb(n, [P, TILES]) for n in ("m1", "m2", "hot"))
        M = sb("M", [P, E * GM], BF16)
        segm = sb("segm", [P, GROUPS, E * GM])
        thr = sb("thr", [P, GM])
        slotno = sb("slotno", [P, SM])
        te, ti, ones8 = (sb(n, [P, E]) for n in ("te", "ti", "ones8"))
        wt = [sb(f"wt{k}", [P, TILES]) for k in range(2)]
        slot = [sb(f"slot{k}", [P, TILES], I32) for k in range(2)]
        eid_f = sb("eid_f", [P, SM])
        eid = sb("eid", [P, SA], I32)
        mx = sb("mx", [P, NHEAD])
        sm = [sb(f"sm{k}", [P, NHEAD]) for k in range(2)]
        xstats = sb("xstats", [P, TILES, 6])
        ones2 = sb("ones2", [2, P], F32R)
        warm = sb("warm", [P, 8])
        b1c = sb("b1c", [P, E9])

        araw = sb("araw", [P, 4, HK // 2])
        xnq = [araw[:, 2 * k:2 * k + 2, :].rearrange("p a (t n) -> p (a t) n", n=D) for k in range(2)]

        s1 = ExitStack()
        N0 = sb("N0", [P, TILES, D], stack=s1)
        C = sb("C", [S, D], stack=s1)[:, :]
        wq_sb, wk_sb, wv_sb = (sb(n, [P, DC, NHEAD * DH], stack=s1)[:, :, :] for n in ("wq_sb", "wk_sb", "wv_sb"))
        wo_sb = sb("wo_sb", [P, PAIRS, D], stack=s1)[:, :, :]
        wqT = sb("wqT", [P, PAIRS, D], stack=s1)[:, :, :]
        kbd, vbd = ([sb(f"{n}{k}", [P, NB * P], stack=s1)[:, :] for k in range(2)] for n in ("kbd", "vbd"))
        st_r = [[sb(f"st_r{k}{d}", [P, NB * P], stack=s1)[:, :] for d in range(DEEP)] for k in range(4)]
        c_col = sb("c_col", [P, PAIRS * NB], stack=s1)[:, :]
        c_r = sb("c_r", [PAIRS * NB, P], stack=s1)[:, :]
        c_h, c_l = (sb(n, [PAIRS * NB, P], F32R, s1)[:, :] for n in ("c_h", "c_l"))
        convw_sb = sb("convw_sb", [P, RATE, DC, D], stack=s1)[:, :, :, :]
        ctxT = sb("ctxT", [P, DC, NB * S], stack=s1)[:, :, :]
        CT = sb("CT", [P, 2, D], stack=s1)[:, :, :]
        U = sb("U", [P, 2, D], stack=s1)[:, :, :]
        UT = sb("UT", [P, DC, NB * S], stack=s1)[:, :, :]
        s1.close()

        s2 = ExitStack()
        stage = sb("stage", [P, DC * E9 * H0 + E9 * D], stack=s2)
        w1_raw = stage[:, 0:DC * E9 * H0].rearrange("p (c e h) -> p c e h", c=DC, e=E9)
        w2_raw = stage[:, DC * E9 * H0:].rearrange("p (e n) -> p e n", e=E9)
        cfT = stage[0:2 * E9, 0:TILES * P].rearrange("p (q n) -> p q n", q=QUADS)
        b2_raw = sb("b2_raw", [2 * E9, D], stack=s2)
        w1h, w1l = (sb(n, [P, DC, E9, H0], F32R, s2) for n in ("w1h", "w1l"))
        w2h, w2l = (sb(n, [P, E9, D], F32R, s2) for n in ("w2h", "w2l"))
        b2h, b2l = (sb(n, [2 * E9, D], F32R, s2) for n in ("b2h", "b2l"))
        roh, rol = (sb(n, [P, DC, E], F32R, s2) for n in ("roh", "rol"))
        sel = sb("sel", [2 * E9, E9, P], F32R, s2)
        cf = sb("cf", [P, TILES, 2 * E9], F32R, s2)
        cfq = [sb(f"cfq{k}", [2 * E9, QN], F32R, s2) for k in range(2)]
        xh, xl = (sb(n, [P, QUADS, DC, QN], F32R, s2) for n in ("xh", "xl"))
        hsl = [sb(f"hsl{k}", [P, QN], stack=s2) for k in range(2)]
        hg = [sb(f"hg{k}", [P, QN], stack=s2) for k in range(2)]
        hh = [sb(f"hh{k}", [P, QN], F32R, s2) for k in range(2)]
        hl = [sb(f"hl{k}", [P, QN], F32R, s2) for k in range(2)]
        s2.close()

        N = [None, sb("N1", [P, GT[1], XW])]
        B = sb("B", [P, 4096])
        s3 = ExitStack()
        Ah, Al, Vh, Vl = [], [], [], []
        for k in range(2):
            for lst, n, shape in ((Ah, "Ah", [P, DC, HK]), (Al, "Al", [P, DC, HK]), (Vh, "Vh", [P, PAIRS, D]), (Vl, "Vl", [P, PAIRS, D])):
                lst.append(sb(f"{n}{k}", shape, F32R, s3))
        vraw = B[:, 0:2048].rearrange("p (m n) -> p m n", m=4)

        def pieces(v, k):
            v = v[k][:, :, :]
            return v.rearrange("p c (m n) -> p (c m) n", n=512) if v.shape[1] == DC else v.rearrange("p (m c) n -> p m (c n)", c=2)
        cb = [sb(f"cb{k}", [2, HK], F32R, s3) for k in range(2)]
        pr = [sb(f"pr{k}", [P, HK], stack=s3)[:, :] for k in range(2)]
        prh, prl = (sb(n, [P, HK], F32R, s3) for n in ("prh", "prl"))
        xn_a = [sb(f"xna{k}", [P, D], stack=s3)[:, :] for k in range(2)]
        xah, xal = ([sb(f"{n}{k}", [P, DC, P], F32R, s3) for k in range(2)] for n in ("xah", "xal"))
        N[0] = sb("N0g", [P, GT[0], XW], stack=s3)
        s3.close()
        w13l = sb("w13l", [P, DC, E, 2 * H1], F32R)
        w2_sb = sb("w2_sb", [P, HC1, E, D])
        w13h = sb("w13h", [P, DC, E, 2 * H1], F32R)
        xs = [carve(B, XW * k, XW) for k in range(4)]
        xTh, xTl = ([sb(f"{n}{k}", [P, DC, P], F32R) for k in range(2)] for n in ("xTh", "xTl"))
        hs = [carve(B, 1552 + H1 * k, H1) for k in range(2)]
        hT = [carve(B, 2320 + H1 * k, H1, "p (c n) -> p c n", c=HC1) for k in range(2)]
        ys = [carve(B, 3088 + 256 * k, 256) for k in range(2)]
        wcol = carve(B, 3600, 4)
        xnT4 = [carve(B, 1024 * k, 1024, "p (c n) -> p c n", c=DC) for k in range(2)]
        tot = carve(B, 0, E * GM)
        inc = carve(B, 256, E * GM)
        cmp = carve(B, 2048, SM * E)
        lgT = [B[0:E, 2560 + 512 * k:3072 + 512 * k] for k in range(2)]

        psum = st.enter_context(nc.psum_tensor("psum", [P, 8, 512], F32))
        bank = [psum[:, k, :] for k in range(8)]

        XS = [nc.dram_tensor(f"xs_dram{g}", [SLOTS[g] * P, XW], F32).ap() for g in range(GROUPS)]
        YS = [nc.dram_tensor(f"ys_dram{g}", [SLOTS[g] * P, D], F32).ap() for g in range(GROUPS)]
        AD = nc.dram_tensor("a_dram", [NB, P, DC, HK], F32).ap()
        VD = nc.dram_tensor("vw_dram", [NB, P, PAIRS, D], F32).ap()
        WD = nc.dram_tensor("w13_dram", [DC, P, E, 2 * H1], F32).ap()
        CD = nc.dram_tensor("c_dram", [NB, 2, HK], F32).ap()

        names = """consts ctx_in u_in x_in0 x_in1 x_in2 x_in3 s_in0 s_in1 s_in2 s_in3 qk_in wd_in w_in0 w_in1 w_in2 w_in3 w_hi w_lop w_lod vo_in small_in rest_in cw_in l0_in l1_in zeroed
            u_norm ut_p ut_sb c_p c_sb s_norm c_put0 c_put1 c_put2 c_put3 x_sum
            pre_t pre_ts wqt_p wqt_sb k_p k_sb v_p v_sb a_p vw_p st_sb st_out00 st_out01 st_out02 st_out10 st_out11 st_out12 st_out20 st_out21 st_out22 st_out30 st_out31 st_out32
            c2_p c2_c c2_t c2_h c2_l c2_out
            l_ro l_sel l_w l_b2h l_b2 l_xn l_tp l_xh l_xl l_lg l_lt l_lgt l_cf l_cft l_cfa l_cfd
            l_cfq l_bc l_h l_hs l_hg l_hh l_hl l_y l_xu
            n_r t_p xt_a xt_d ro_p ro_sb ro_t
            spa spd r_m r_pt rout sc1 sc2
            xs_in0 xs_in1 xs_in2 xs_in3 e_tp e_xt e_xl e_h e_g e_hs e_hg e_htp e_ht e_y e_ys e_st0 e_st1
            a_in v_in av_ld cb_in0 cb_in1 av_h av_l a_xn a_tp a_xh a_xl a_lg a_sub a_ex a_sm a_pn a_ptp a_ph a_pl a_o a_xu
            gat10 gat11 gat20 gat21 stored bar_pe bar_act bar_dve bar_sp""".split()
        s = {n: sem(n) for n in names}

        class Marks:
            def __init__(self, eng, own):
                self.eng, self.own, self.n = eng, own, 0

            def meet(self):
                self.n += 1
                self.eng.drain()
                self.eng.sem_inc(s[self.own], 1)
                for other in ("bar_pe", "bar_act", "bar_dve", "bar_sp"):
                    if other != self.own:
                        self.eng.wait_ge(s[other], self.n)

        block = st.enter_context(nc.Block())

        @block.sync
        def _(sp):
            meet = Marks(sp, "bar_sp").meet
            sp.dma_start(CT, ctx_in.rearrange("(q b) s d -> (b s) q d", q=2)).then_inc(s["ctx_in"], 16)
            sp.dma_start(wv_sb, wv.rearrange("(c p) n -> p c n", p=P)).then_inc(s["vo_in"], 16)
            sp.dma_start(wo_sb, wo.rearrange("(j p) n -> p j n", p=P)).then_inc(s["vo_in"], 16)
            for b in range(NB):
                sp.dma_start(U[S * (b % 2):S * (b % 2) + S, b // 2, :],
                             x[b, CONV:CONV + S, :]).then_inc(s["u_in"], 16)
            for c in range(DC):
                sp.dma_start(convw_sb[:, :, c, :], conv_w[:, c * P:c * P + P, :].rearrange("k p n -> p k n")).then_inc(s["cw_in"], 16)
            for b in range(NB):
                t0 = b * BT
                k = S // RATE
                sp.dma_start(N0[:, t0:t0 + 4, :],
                             x[b, k:k + CONV, :].rearrange("(t p) d -> p t d", p=P)).then_inc(s[f"s_in{b}"], 16)
                sp.dma_start(N0[:, t0 + 4:t0 + 7, :],
                             x[b, CONV + S:T - S, :].rearrange("(t p) d -> p t d", p=P)).then_inc(s[f"s_in{b}"], 16)
                sp.dma_start(N0[0:S, t0 + 7, :], x[b, T - S:T, :]).then_inc(s[f"s_in{b}"], 16)
                sp.dma_start(N0[S:P, t0 + 7, :], ctx_in[b]).then_inc(s[f"s_in{b}"], 16)
                sp.dma_start(X[:, t0:t0 + BT, :], x[b].rearrange("(t p) d -> p t d", p=P)).then_inc(s[f"x_in{b}"], 16)
            for j in range(PAIRS):
                for i in range(4):
                    sp.wait_ge(s["st_sb"], 4 * j + i + 1)
                    if i < DC:
                        sp.dma_start(AD[:, :, i, P * j:P * j + P].rearrange("b p n -> p b n"),
                                     st_r[i][j % DEEP].rearrange("p (b n) -> p b n", b=NB)).then_inc(s[f"st_out{i}{j % DEEP}"], 16)
                    else:
                        h = i - DC
                        sp.dma_start(VD[2 * h:2 * h + 2, :, j, :].rearrange("b p n -> p b n"),
                                     st_r[i][j % DEEP].rearrange("p (b n) -> p b n", b=2)).then_inc(s[f"st_out{i}{j % DEEP}"], 16)
            for part, (src, done) in enumerate(((c_h, "c2_h"), (c_l, "c2_l"))):
                sp.wait_ge(s[done], 1)
                for b in range(NB):
                    sp.dma_start(CD[b, part, :].rearrange("(j n) -> j n", n=P), src.bitcast(F32)[b::NB, :]).then_inc(s["c2_out"], 16)
            sp.wait_ge(s["c2_out"], 16 * 2 * NB)
            for i in range(4):
                for d in range(DEEP):
                    sp.wait_ge(s[f"st_out{i}{d}"], 16 * len(range(d, PAIRS, DEEP)))
            meet()
            for c in range(DC):
                sp.dma_start(w1_raw[:, c, 0:E, :], rw1[:, c * P:c * P + P, :].rearrange("e p h -> p e h")).then_inc(s["l0_in"], 16)
                sp.dma_start(w1_raw[:, c, E, :], sw1[c * P:c * P + P, :]).then_inc(s["l0_in"], 16)
            sp.dma_start(w2_raw[:, 0:E, :], rw2.rearrange("e p n -> p e n")).then_inc(s["l0_in"], 16)
            sp.dma_start(w2_raw[:, E, :], sw2).then_inc(s["l0_in"], 16)
            for k in (0, E9):
                sp.dma_start(b2_raw[k:k + E, :], rb2).then_inc(s["l0_in"], 16)
                sp.dma_start(b2_raw[k + E:k + E9, :], sb2.rearrange("(a n) -> a n", a=1)).then_inc(s["l0_in"], 16)
            for g in range(GROUPS):
                sp.dma_start(XS[g].rearrange("(p r) d -> p r d", p=P),
                             zero4[:, :].rearrange("p (a d) -> p a d", a=1).to_broadcast([P, SLOTS[g], XW])).then_inc(s["zeroed"], 16)
            for c in range(DC):
                for half, w in enumerate((w1, w3)):
                    sp.dma_start(WD[c, :, :, half * H1:half * H1 + H1],
                                 w[:, c * P:c * P + P, :].rearrange("e p h -> p e h")).then_inc(s["wd_in"], 16)
            sp.wait_ge(s["l_tp"], QUADS)
            sp.dma_start(araw[:, :, :], AD[0].rearrange("p c (m n) -> p (c m) n", n=512)).then_inc(s["a_in"], 16)
            meet()

            def store_rows(g):
                half = GT[g] // 2
                for part in range(2):
                    sp.wait_ge(s[f"gat2{part}"], 8 * (G0[g] + GT[g]))
                    t0, t1 = G0[g] + half * part, G0[g] + half * part + half
                    for b in BATCHES[g]:
                        a, z = max(t0, b * BT), min(t1, b * BT + BT)
                        if a < z:
                            o = out[b, (a - b * BT) * P:(z - b * BT) * P, :].rearrange("(t p) d -> p t d", p=P)
                            sp.dma_start(o, X[:, a:z, :]).then_inc(s["stored"], 16)

            def experts():
                def load(j, b, g, early=False):
                    if not early:
                        sp.wait_ge(s["e_xt"], j - 3)
                    sp.dma_start(xs[b], XS[g][bass.ds((j + (-SLOT0[g])) * P, P), :]).then_inc(s[f"xs_in{b}"], 16)

                def store(j, b, g):
                    sp.wait_ge(s["e_ys"], j + 1)
                    sp.dma_start(YS[g][bass.ds((j + (-SLOT0[g])) * P, P), :], ys[b]).then_inc(s[f"e_st{b}"], 16)

                def steps(h0, h1, g):
                    with sp.Fori(h0, h1) as h_:
                        i = h_ * 4
                        for r in range(4):
                            load(i + (r + 6), (r + 2) % 4, g)
                            store(i + r, r % 2, g)

                def step(j):
                    if j + 6 < SA:
                        load(j + 6, (j + 6) % 4, int(j + 6 >= SLOTS[0]))
                    store(j, j % 2, int(j >= SLOTS[0]))

                sp.wait_ge(s["sc1"], 16 * GT[0])
                sp.wait_ge(s["sc2"], 16 * GT[0])
                for j in range(6):
                    load(j, j % 4, 0, j < 4)
                first, last = (SLOTS[0] - 6) // 4, (SA - 6) // 4
                steps(0, first, 0)
                sp.wait_ge(s["sc1"], 16 * TILES)
                sp.wait_ge(s["sc2"], 16 * TILES)
                for j in range(4 * first, SLOTS[0]):
                    step(j)
                steps(SLOTS[0] // 4, last, 1)
                store_rows(0)
                for j in range(4 * last, SA):
                    step(j)

            for g in range(GROUPS):
                for b in range(NB) if g == 0 else ():
                    k = b % 2
                    if b:
                        if b == 1:
                            sp.wait_ge(s["av_ld"], 2)
                        sp.wait_ge(s["av_l"], 8 * b - 2)
                        sp.dma_start(araw[:, :, :], AD[b].rearrange("p c (m n) -> p (c m) n", n=512)).then_inc(s["a_in"], 16)
                    sp.dma_start(vraw, VD[b].rearrange("p (m c) n -> p m (c n)", c=2)).then_inc(s["v_in"], 16)
                    if b >= 2:
                        sp.wait_ge(s["a_lg"], BT * (b - 1))
                    sp.dma_start(cb[k][:, :].bitcast(F32), CD[b]).then_inc(s[f"cb_in{k}"], 16)
                if g == GROUPS - 1:
                    sp.wait_ge(s["wd_in"], 32 * DC)
                    sp.wait_ge(s["a_o"], TILES - BT)
                    for i in range(4):
                        if i == 2:
                            sp.wait_ge(s["a_xu"], TILES)
                        c, e = i // 2, E // 2 * (i % 2)
                        sp.dma_start(w13l[:, c, e:e + E // 2, :].bitcast(F32), WD[c, :, e:e + E // 2, :]).then_inc(s[f"w_in{i}"], 16)
                    sp.wait_ge(s["sc2"], 16 * GT[0])
                    for c in range(HC1):
                        sp.dma_start(w2_sb[:, c, :, :], w2[:, c * P:c * P + P, :].rearrange("e p n -> p e n")).then_inc(s["l1_in"], 16)
            meet()
            experts()
            store_rows(1)
            sp.wait_ge(s["stored"], 16 * (NB + 2))

        @block.gpsimd
        def _(po):
            po.memset(ident[:, :], 0.0)
            po.memset(upper[:, :], 0.0)
            po.memset(ones_b[:, :], 1.0)
            po.memset(ones8[:, :], 1.0)
            po.memset(ones[:, :], 1.0)
            po.memset(segm[:, :, :], 1.0)
            po.memset(ones2[:, :].bitcast(F32), 1.0)
            po.memset(warm[:, :], 0.0)
            po.iota(prio[:, :], pattern=[[-1, E]], base=E, channel_multiplier=0,
                    allow_small_or_imprecise_dtypes=True)
            po.iota(thr[:, :], pattern=[[P, GM]], base=0, channel_multiplier=0,
                    allow_small_or_imprecise_dtypes=True)
            po.iota(slotno[:, :], pattern=[[1, SM]], base=0, channel_multiplier=0,
                    allow_small_or_imprecise_dtypes=True)
            po.memset(zero4[:, :], 0.0)
            po.drain()
            for g in range(GROUPS):
                po.memset(segm[:, g, 0:E * GT[g]].rearrange("p (e t) -> p e t", e=E)[:, :, 0:1], 0.0)
            po.affine_select(out=ident[:, :], in_=ident[:, :], compare_op=ALU.not_equal, fill=1.0,
                             base=0, pattern=[[-1, P]], channel_multiplier=1)
            po.affine_select(out=upper[:, :], in_=upper[:, :], compare_op=ALU.is_ge, fill=1.0,
                             base=0, pattern=[[-1, P]], channel_multiplier=1)
            po.drain()
            po.memset(segones, 0.0)
            po.drain()
            for k in range(2):
                po.memset(kbd[k], 0.0)
                po.memset(vbd[k], 0.0)
            po.drain()
            po.memset(segones[:, 0:S], 1.0)
            po.drain()
            po.sem_inc(s["consts"], 2)
            po.wait_ge(s["c_sb"], 1)
            k = S // RATE

            def put(b):
                po.wait_ge(s["s_norm"], b + 1)
                po.dma_start(N0[P - k:P, b * BT + 3, :], C[k * b:k * b + k, :]).then_inc(s[f"c_put{b}"], 16)

            put(0)
            for b in range(NB - 1):
                put(b + 1)
                po.wait_ge(s[f"c_put{b}"], 16)
                po.wait_ge(s[f"x_in{b}"], 16)
                for t in range(b * BT, b * BT + BT, 2):
                    last = po.tensor_tensor(X[:, t:t + 2, :], X[:, t:t + 2, :], N0[:, t:t + 2, :], ALU.add)
                last.then_inc(s["x_sum"], 1)
            po.wait_ge(s["c2_h"], 1)
            po.tensor_tensor(c_l, c_r, c_h.bitcast(F32), ALU.subtract).then_inc(s["c2_l"], 1)

            def after(n):
                for other in ("bar_pe", "bar_act", "bar_dve", "bar_sp"):
                    po.wait_ge(s[other], n)

            after(1)
            po.wait_ge(s["l0_in"], 16 * 10)
            for raw, high, low in ((w1_raw, w1h[:, :, :, :], w1l[:, :, :, :]), (w2_raw, w2h[:, :, :], w2l[:, :, :])):
                po.tensor_copy(high, raw)
                po.drain()
                last = po.tensor_tensor(low, raw, high.bitcast(F32), ALU.subtract)
                last.then_inc(s["l_w"], 1)
            after(2)
            for g in range(GROUPS):
                po.memset(N[g][:, :, D:XW], 0.0)
            po.drain()
            po.sem_inc(s["consts"], 1)

            def split_low(k, m, v):
                raw, high, low = ((araw, Ah, Al), (vraw, Vh, Vl))[v]
                po.tensor_tensor(pieces(low, k)[:, m, :], raw[:, m, :], pieces(high, k)[:, m, :].bitcast(F32),
                                 ALU.subtract).then_inc(s["av_l"], 1)

            def scale(n):
                v = pr[n % 2].rearrange("p (h n) -> p h n", n=S)
                po.wait_ge(s["a_sm"], n + 1)
                po.tensor_tensor(v, v, sm[n % 2][:, :].rearrange("p (a b) -> p a b", b=1).to_broadcast([P, NHEAD, S]),
                                 ALU.mult).then_inc(s["a_pn"], 1)

            def scatter(g, k, t0, t1):
                for t in range(G0[g] + t0, G0[g] + t1):
                    po.indirect_dma_start(
                        XS[g], bass.IndirectOffsetOnAxis(ap=slot[k][:, t:t + 1], axis=0),
                        N[g][:, t - G0[g], :], None).then_inc(s[f"sc{k + 1}"], 16)

            def second(g):
                t0, n = G0[g], GT[g]
                po.wait_ge(s["sc1"], 16 * (t0 + n))
                po.tensor_copy(N[g][:, :, D:D + 1], wt[1][:, t0:t0 + n].rearrange("p (t a) -> p t a", a=1))
                po.drain()

            def gather(g):
                for b in range(2):
                    po.wait_ge(s[f"e_st{b}"], 8 * (SLOT0[g] + SLOTS[g]))
                half = GT[g] // 2
                for k in range(2):
                    for part in range(2):
                        t0 = G0[g] + half * part
                        if k:
                            po.wait_ge(s[f"gat1{part}"], 8 * (G0[g] + GT[g]))
                        for t in range(t0, t0 + half):
                            po.indirect_dma_start(
                                X[:, t, :], None, YS[g],
                                bass.IndirectOffsetOnAxis(ap=slot[k][:, t:t + 1], axis=0),
                                compute_op=ALU.add).then_inc(s[f"gat{k + 1}{part}"], 16)
                for part in range(2):
                    po.wait_ge(s[f"gat2{part}"], 8 * (G0[g] + GT[g]))

            for v in range(2):
                for m in range(4):
                    if v or m < 2:
                        po.wait_ge(s["av_h"], 4 * v + m + 1)
                        split_low(0, m, v)
            for b in BATCHES[0]:
                for r in range(BT):
                    scale(b * BT + r)
                    if 2 <= r < 6:
                        for v in range(2):
                            po.wait_ge(s["av_h"], 8 * (b + 1) + 2 * (r - 2) + v + 1)
                            split_low(1 - b % 2, r - 2, v)
            po.wait_ge(s["zeroed"], 16 * GROUPS)
            po.wait_ge(s["rout"], 1)
            half, step = BT // 2, 5
            ahead = GT[0] - half * step
            scatter(0, 0, 0, ahead)
            for r in range(BT):
                scale(G0[1] + r)
                if r < half:
                    scatter(0, 0, ahead + step * r, ahead + step * r + step)
                else:
                    if r == half:
                        second(0)
                    scatter(0, 1, step * (r - half), step * (r - half) + step)
            scatter(0, 1, step * (BT - half), GT[0])
            for i in range(3):
                po.wait_ge(s["w_hi"], i + 1)
                low, high = (v[:, i // 2, E // 2 * (i % 2):E // 2 * (i % 2) + E // 2, :] for v in (w13l, w13h))
                po.tensor_tensor(low, low.bitcast(F32), high.bitcast(F32), ALU.subtract).then_inc(s["w_lop"], 1)
            po.wait_ge(s["sc2"], 16 * GT[0])
            po.wait_ge(s["rout"], 2)
            scatter(1, 0, 0, GT[1])
            second(1)
            scatter(1, 1, 0, GT[1])
            po.wait_ge(s["sc2"], 16 * TILES)
            gather(0)
            gather(1)

        @block.tensor
        def _(pe):
            meet = Marks(pe, "bar_pe").meet

            def mm(o, l, r, start, stop):
                return nc.tensor.matmul(o, l, r, start=start, stop=stop)

            pe.wait_ge(s["consts"], 2)
            pe.wait_ge(s["ctx_in"], 16)
            for q in range(2):
                for c in range(DC):
                    last = nc.tensor.transpose(bank[0][:, 256 * c + P * q:256 * c + P * q + P],
                                               CT[:, q, c * P:c * P + P], ident[:, :])
            last.then_inc(s["pre_t"], 1)
            pe.wait_ge(s["qk_in"], 32)
            for m in range(4):
                if m >= 2:
                    pe.wait_ge(s["wqt_sb"], m - 1)
                for h in range(2):
                    for c in range(DC):
                        last = nc.tensor.transpose(bank[1 + m % 2][:, 256 * h + P * c:256 * h + P * c + P],
                                                   wq_sb[:, c, (2 * m + h) * P:(2 * m + h + 1) * P], ident[:, :])
                last.then_inc(s["wqt_p"], 1)
            pe.wait_ge(s["pre_ts"], 1)
            pe.wait_ge(s["wqt_sb"], 4)
            pe.wait_ge(s["small_in"], 16 * SMALL)
            pe.wait_ge(s["vo_in"], 32)

            def keys_values(j):
                if j >= 1:
                    pe.wait_ge(s["k_sb"], j)
                for c in range(DC):
                    last = mm(bank[0][:, 0:256], wk_sb[:, c, j * P:j * P + P], ctxT[:, c, :], c == 0, c == DC - 1)
                last.then_inc(s["k_p"], 1)
                if j >= 1:
                    pe.wait_ge(s["v_sb"], j)
                for c in range(DC):
                    last = mm(bank[1][:, 0:256], wv_sb[:, c, j * P:j * P + P], ctxT[:, c, :], c == 0, c == DC - 1)
                last.then_inc(s["v_p"], 1)

            keys_values(0)
            for j in range(PAIRS):
                if j + 1 < PAIRS:
                    keys_values(j + 1)
                pe.wait_ge(s["k_sb"], j + 1)
                for c in range(DC):
                    if j >= 1:
                        pe.wait_ge(s["st_sb"], 4 * (j - 1) + c + 1)
                    mm(bank[2 + c], wqT[:, j, c * P:c * P + P], kbd[j % 2], True, True).then_inc(s["a_p"], 1)
                for b in range(NB):
                    last = mm(bank[7][:, NB * j + b:NB * j + b + 1], kbd[j % 2][:, b * P:b * P + P], bcols[:, 0, j:j + 1], True, True)
                last.then_inc(s["c2_p"], 1)
                pe.wait_ge(s["v_sb"], j + 1)
                for h in range(2):
                    if j >= 1:
                        pe.wait_ge(s["st_sb"], 4 * (j - 1) + DC + h + 1)
                    for b in (2 * h, 2 * h + 1):
                        o = bank[5 + h][:, 256 * (b % 2):256 * (b % 2) + 256]
                        last = mm(o, vbd[j % 2][:, b * P:b * P + P], wo_sb[:, j, :], True, j > 0)
                        if j == 0:
                            last = mm(o, segones, rows[:, D:2 * D], False, True)
                    last.then_inc(s["vw_p"], 1)
                if j == 1:
                    pe.wait_ge(s["u_norm"], 1)
                    for q in range(2):
                        for c in range(DC):
                            last = nc.tensor.transpose(bank[4][:, 256 * c + P * q:256 * c + P * q + P],
                                                       U[:, q, c * P:c * P + P], ident[:, :])
                    last.then_inc(s["ut_p"], 1)
                    pe.wait_ge(s["ut_sb"], 1)
                    pe.wait_ge(s["cw_in"], 16 * DC)
                    for k in range(RATE):
                        for c in range(DC):
                            mm(bank[4][0:S, 0:D], UT[:, c, k::RATE], convw_sb[:, k, c, :], k == 0 and c == 0, False)
                    mm(bank[4][0:S, 0:D], ones[64:65, 0:S], rows[:, 0:D], False, True).then_inc(s["c_p"], 1)
            pe.wait_ge(s["c2_c"], 1)
            pe.wait_ge(s["c_sb"], 1)
            nc.tensor.transpose(bank[4][0:PAIRS * NB, 0:P], c_col, ident[:, :]).then_inc(s["c2_t"], 1)
            meet()

            def layer0():
                def rows_t(q):
                    pe.wait_ge(s["l_xn"], q + 1)
                    if q >= 2:
                        pe.wait_ge(s["l_xl"], q - 1)
                    for c in range(DC):
                        for t in range(QT):
                            last = nc.tensor.transpose(bank[2 * (q % 2) + c][:, t * P:t * P + P],
                                                       xnq[q % 2][:, t, c * P:c * P + P], ident[:, :])
                    last.then_inc(s["l_tp"], 1)

                def logits(q):
                    if q == 0:
                        pe.wait_ge(s["l_ro"], 1)
                    pe.wait_ge(s["l_xl"], q + 1)
                    if q >= 2:
                        pe.wait_ge(s["l_lt"], q - 1)
                    for i, (w, a) in enumerate(((roh, xh), (roh, xl), (rol, xh))):
                        for c in range(DC):
                            last = nc.tensor.matmul(bank[6 + q % 2][0:E, :], w[:, c, :], a[:, q, c, :],
                                                    start=i == c == 0, stop=i == 2 and c == DC - 1)
                    last.then_inc(s["l_lg"], 1)

                def turn(q):
                    pe.wait_ge(s["l_lt"], q + 1)
                    for t in range(QT):
                        last = nc.tensor.transpose(bank[5][:, (QT * q + t) * E:(QT * q + t) * E + E],
                                                   hsl[q % 2][0:E, t * P:t * P + P], ident[0:E, 0:E])
                    last.then_inc(s["l_lgt"], 1)

                for q in range(QUADS + 2):
                    if q < QUADS:
                        rows_t(q)
                    if 1 <= q <= QUADS:
                        logits(q - 1)
                    if q >= 2:
                        turn(q - 2)
                pe.wait_ge(s["l_cf"], 1)
                for q in range(QUADS):
                    for t in range(QT):
                        last = nc.tensor.transpose(bank[q][0:2 * E9, t * P:t * P + P],
                                                   cf[:, QT * q + t, :].bitcast(F32), ident[:, :])
                    last.then_inc(s["l_cft"], 1)
                pe.wait_ge(s["l_cfa"], 1)
                pe.wait_ge(s["l_cfd"], 1)
                pe.wait_ge(s["l_w"], 2)
                pe.wait_ge(s["l_b2"], 1)
                pe.wait_ge(s["l_sel"], 1)

                def up(n, u, q, v, e, early):
                    if e == 0:
                        pe.wait_ge(s["l_cfq"], q + 1)
                    if not early:
                        pe.wait_ge(s["l_hg"], n - 1)
                        pe.wait_ge(s["l_hs"], n - 1)
                    nc.tensor.matmul(bank[u % 2], sel[:, e, :], cfq[v][:, :], start=True, stop=True).then_inc(s["l_bc"], 1)
                    for i, (w, a) in enumerate(((w1h, xh), (w1h, xl), (w1l, xh))):
                        for c in range(DC):
                            last = nc.tensor.matmul(bank[3 + u % 2], w[:, c, e, :],
                                                    a[:, bass.ds(q, 1), c, :].rearrange("p a n -> p (a n)"),
                                                    start=i == c == 0, stop=i == 2 and c == DC - 1)
                    last.then_inc(s["l_h"], 1)

                def down(n, u, q, v, e, early):
                    pe.wait_ge(s["l_hl"], n + 1)
                    if e == 0 and not early:
                        pe.wait_ge(s["l_xu"], q - 1)
                    for t in range(QT):
                        o = bank[(6, 7, 2, 5)[2 * v + t // 2]][:, D * (t % 2):D * (t % 2) + D]
                        if e == 0:
                            for w in (b2h, b2l):
                                nc.tensor.matmul(o, cfq[v][:, t * P:t * P + P], w[:, :],
                                                 start=t % 2 == 0 and w is b2h, stop=False, skip_group_check=True)
                        for a, w in ((hh, w2h), (hl, w2h), (hh, w2l)):
                            last = nc.tensor.matmul(o, a[u % 2][:, t * P:t * P + P], w[:, e, :],
                                                    start=False, stop=False, skip_group_check=True)
                    last.then_inc(s["l_y"], 1)

                def pair(h, first):
                    for u in range(2 * E9):
                        up(h * (2 * E9) + u, u, h * 2 + u // E9, u // E9, u % E9, first and u < 2)
                        w = u - 2
                        if w >= 0:
                            down(h * (2 * E9) + w, w, h * 2 + w // E9, w // E9, w % E9, first)
                        elif not first:
                            down(h * (2 * E9) + w, w + 2 * E9, h * 2 - 1, 1, w + E9, False)

                pair(0, True)
                with pe.Fori(1, QUADS // 2) as h_:
                    pair(h_, False)
                for w in (2, 1):
                    down(UNITS - w, 2 * E9 - w, QUADS - 1, 1, E9 - w, False)

            def router(g):
                k0, quads, cols = G0[g] // QT, GT[g] // QT, E * GT[g]

                def rows_t(k):
                    pe.wait_ge(s["n_r"], k + 1)
                    if k >= 2:
                        pe.wait_ge(s["xt_a"], k - 1)
                        pe.wait_ge(s["xt_d"], k - 1)
                    for c in range(DC):
                        for t in range(QT):
                            last = nc.tensor.transpose(bank[2 * (k % 2) + c][:, t * P:t * P + P],
                                                       N[g][:, (k - k0) * QT + t, c * P:c * P + P], ident[:, :])
                    last.then_inc(s["t_p"], 1)

                def turn(k):
                    pe.wait_ge(s["ro_sb"], k + 1)
                    for t in range(QT):
                        u = (k - k0) * QT + t
                        last = nc.tensor.transpose(bank[4][:, u * E:u * E + E], lgT[k % 2][:, t * P:t * P + P], ident[0:E, 0:E])
                    last.then_inc(s["ro_t"], 1)

                rows_t(k0)
                for k in range(k0, k0 + quads):
                    if k + 1 < k0 + quads:
                        rows_t(k + 1)
                    pe.wait_ge(s["xt_a"], k + 1)
                    pe.wait_ge(s["xt_d"], k + 1)
                    if k >= 2:
                        pe.wait_ge(s["ro_sb"], k - 1)
                    for c in range(DC):
                        last = mm(bank[5 + 2 * (k % 2)][0:E, :], roT[1][:, c, :], xnT4[k % 2][:, c, :], c == 0, c == DC - 1)
                    last.then_inc(s["ro_p"], 1)
                    if k > k0:
                        turn(k - 1)
                turn(k0 + quads - 1)
                if g == 0:
                    attention(1, rest=False)
                pe.wait_ge(s["r_m"], g + 1)
                mm(bank[4][:, 0:cols], upper[:, :], M[:, 0:cols], True, True)
                mm(bank[5][:, 0:cols], ones_b[:, :], M[:, 0:cols], True, True).then_inc(s["r_pt"], 1)

            def experts():
                def xpose(j, b, b4, early=False):
                    pe.wait_ge(s[f"xs_in{b4}"], (j - b4) * 4 + 16)
                    if not early:
                        pe.wait_ge(s["e_xl"], j)
                    for c in range(DC):
                        last = nc.tensor.transpose(bank[0][:, c * P:c * P + P], xs[b4][:, c * P:c * P + P], ident[:, :])
                    last.then_inc(s["e_tp"], 1)

                def up(j, b, early=False):
                    ex = pe.value_load(eid[0:1, bass.ds(j, 1)], min_val=0, max_val=E - 1)
                    pe.wait_ge(s["e_xl"], j + 1)
                    if not early:
                        pe.wait_ge(s["e_hg"], j - 1)
                    for half, sm_name in enumerate(("e_h", "e_g")):
                        for c in range(DC):
                            wh, wl = (v[:, c, bass.ds(ex, 1), half * H1:half * H1 + H1].rearrange("p a n -> p (a n)") for v in (w13h, w13l))
                            for i, (a, w) in enumerate(((xTh, wh), (xTh, wl), (xTl, wh))):
                                last = nc.tensor.matmul(bank[2 + 2 * half + b][:, 0:H1], a[b][:, c, :], w,
                                                        start=c == i == 0, stop=c == DC - 1 and i == 2)
                        last.then_inc(s[sm_name], 1)

                def hpose(j, b, early=False):
                    pe.wait_ge(s["e_hg"], j + 1)
                    if not early:
                        pe.wait_ge(s["e_ht"], j - 1)
                    for c in range(HC1):
                        last = nc.tensor.transpose(bank[6 + b][:, c * P:c * P + P], hs[b][:, c * P:c * P + P], ident[:, :])
                    last.then_inc(s["e_htp"], 1)

                def down(j, b, early=False):
                    ex = pe.value_load(eid[0:1, bass.ds(j, 1)], min_val=0, max_val=E - 1)
                    pe.wait_ge(s["e_ht"], j + 1)
                    if not early:
                        pe.wait_ge(s["e_ys"], j)
                    for c in range(HC1):
                        last = mm(bank[1][:, 0:D], hT[b][:, c, :], w2_sb[:, c, bass.ds(ex, 1), :].rearrange("p a n -> p (a n)"),
                                  c == 0, c == HC1 - 1)
                    last.then_inc(s["e_y"], 1)

                pe.wait_ge(s["w_lop"], 3)
                pe.wait_ge(s["w_lod"], 1)
                xpose(0, 0, 0, True)
                up(0, 0, True)
                xpose(1, 1, 1)
                up(1, 1, True)
                hpose(0, 0, True)
                xpose(2, 0, 2)
                up(2, 0)
                hpose(1, 1, True)
                xpose(3, 1, 3)
                pe.wait_ge(s["l1_in"], 16 * HC1)
                down(0, 0, True)
                with pe.Fori(0, (SA - 4) // 4) as h_:
                    i = h_ * 4
                    for r in range(4):
                        j, b = i + (r + 3), (r + 3) % 2
                        up(j, b)
                        hpose(i + (r + 2), 1 - b)
                        xpose(i + (r + 4), 1 - b, r)
                        down(i + (r + 1), b)
                z = SA - 1
                up(z, 1)
                hpose(z - 1, 0)
                down(z - 2, 1)
                hpose(z, 1)
                down(z - 1, 0)
                down(z, 1)

            def attention(g, begin=True, rest=True):
                def xpose(n, b, first):
                    pe.wait_ge(s["a_xn"], n + 1)
                    if not first:
                        pe.wait_ge(s["a_xl"], n)
                    for c in range(DC):
                        last = nc.tensor.transpose(bank[6][:, c * P:c * P + P], xn_a[b][:, c * P:c * P + P], ident[:, :])
                    last.then_inc(s["a_tp"], 1)

                def logits(n, b, k, early):
                    pe.wait_ge(s["a_xl"], n + 1)
                    if not early:
                        pe.wait_ge(s["a_sub"], n - 1)
                    for h in range(2):
                        cols = slice(512 * h, 512 * h + 512)
                        nc.tensor.matmul(bank[2 * b + h], ones2[:, :], cb[k][:, cols], start=True, stop=False)
                        for i, (a, w) in enumerate(((xah, Ah), (xal, Ah), (xah, Al))):
                            for c in range(DC):
                                last = nc.tensor.matmul(bank[2 * b + h], a[b][:, c, :], w[k][:, c, cols],
                                                        start=False, stop=i == 2 and c == DC - 1)
                    last.then_inc(s["a_lg"], 1)

                def ppose(n, b, first):
                    pe.wait_ge(s["a_pn"], n + 1)
                    if not first:
                        pe.wait_ge(s["a_ph"], n * 2)
                        pe.wait_ge(s["a_pl"], n)
                    for c in range(PAIRS):
                        last = nc.tensor.transpose(bank[4 + c // 4][:, (c % 4) * P:(c % 4) * P + P], pr[b][:, c * P:c * P + P], ident[:, :])
                    last.then_inc(s["a_ptp"], 1)

                def values(n, k, first):
                    pe.wait_ge(s["a_pl"], n + 1)
                    if not first:
                        pe.wait_ge(s["a_xu"], n)
                    for i, (a, w) in enumerate(((prh, Vh), (prl, Vh), (prh, Vl))):
                        for c in range(PAIRS):
                            last = nc.tensor.matmul(bank[7][:, 0:D], a[:, c * P:c * P + P], w[k][:, c, :],
                                                    start=i == c == 0, stop=i == 2 and c == PAIRS - 1)
                    last.then_inc(s["a_o"], 1)

                n0, n1 = G0[g], G0[g] + GT[g]

                def first_two():
                    logits(n0, 0, 1, False)
                    xpose(n0 + 1, 1, False)
                    logits(n0 + 1, 1, 1, False)

                if begin:
                    xpose(n0, 0, n0 == 0)
                    if g:
                        pe.wait_ge(s["cb_in1"], 16 * (NB // 2))
                        pe.wait_ge(s["av_l"], 8 * NB - 2)
                        first_two()
                if not rest:
                    return
                if g:
                    pe.wait_ge(s["rout"], 1)
                for b_ in BATCHES[g]:
                    k, first = b_ % 2, b_ * BT
                    pe.wait_ge(s[f"cb_in{k}"], 16 * (b_ // 2 + 1))
                    if b_ == 0:
                        pe.wait_ge(s["av_ld"], 2)
                    pe.wait_ge(s["av_l"], 2 if b_ == 0 else 8 * b_ + 6)
                    for r in range(2):
                        n = first + r
                        if n - 2 >= n0:
                            ppose(n - 2, r, False)
                        if not (g and n < n0 + 2):
                            logits(n, r, k, n < 2)
                        if not (g and n == n0):
                            xpose(n + 1, 1 - r, False)
                        if n - 2 >= n0:
                            values(n - 2, 1 - k, False)
                    from_h = first // 2 + 1
                    if b_ == 0:
                        for n in (2, 3):
                            ppose(n - 2, n % 2, n == 2)
                            logits(n, n % 2, k, False)
                            if n == 2:
                                pe.wait_ge(s["av_l"], 6)
                            xpose(n + 1, 1 - n % 2, False)
                            values(n - 2, k, n == 2)
                        from_h += 1
                    with pe.Fori(from_h, (first + BT) // 2 - (b_ == BATCHES[g][-1])) as h_:
                        n = h_ * 2
                        for r in range(2):
                            ppose(n + (r - 2), r, False)
                            logits(n + r, r, k, False)
                            xpose(n + (r + 1), 1 - r, False)
                            values(n + (r - 2), k, False)
                for n in range(n1 - 2, n1 + 2):
                    ppose(n - 2, n % 2, False)
                    if n < n1:
                        logits(n, n % 2, k, False)
                    if n + 1 < n1:
                        xpose(n + 1, 1 - n % 2, False)
                    values(n - 2, k, False)

            layer0()
            meet()
            attention(0)
            router(0)
            attention(1, begin=False)
            router(1)
            meet()
            experts()

        @block.scalar
        def _(ac):
            meet = Marks(ac, "bar_act").meet
            act = nc.scalar.activation

            def table(k, func):
                act(warm[:, k + 4:k + 5], warm[:, k:k + 1], func, bias=1.0)

            for dst, src in ((wk_sb, wk), (wq_sb, wq)):
                ac.dma_start(dst, src.rearrange("(c p) n -> p c n", p=P)).then_inc(s["qk_in"], 16)
            small = [(bcols[:, k, :], v.rearrange("(j p) -> p j", p=P)) for k, v in enumerate((bq, bk, bv))]
            small += [(rows[:, k * D:k * D + D], v.rearrange("(a n) -> a n", a=1)) for k, v in enumerate((conv_b, bo))]
            assert len(small) == SMALL
            for dst, src in small:
                ac.dma_start(dst, src).then_inc(s["small_in"], 16)
            rest = [(b1c[:, 0:E], rb1.rearrange("e p -> p e")), (b1c[:, E:E9], sb1.rearrange("(p a) -> p a", a=1))]
            rest += [(roT[1][:, :, :], wr.rearrange("(c p) e -> p c e", p=P)),
                     (rb_bc[:, :], rout_b.rearrange("(a e) -> a e", a=1).to_broadcast([P, E]))]
            rest += [(roT[0][:, c, :], rout_w[:, c * P:c * P + P].rearrange("e p -> p e")) for c in range(DC)]
            assert len(rest) == REST
            for dst, src in rest:
                ac.dma_start(dst, src).then_inc(s["rest_in"], 16)

            ac.wait_ge(s["pre_t"], 1)
            act(ctxT, bank[0].rearrange("p (c n) -> p c n", c=DC), ACT.Copy).then_inc(s["pre_ts"], 1)
            for m in range(4):
                ac.wait_ge(s["wqt_p"], m + 1)
                act(wqT[:, 2 * m:2 * m + 2, :], bank[1 + m % 2].rearrange("p (j n) -> p j n", j=2), ACT.Copy).then_inc(s["wqt_sb"], 1)
            ac.wait_ge(s["consts"], 2)
            ac.wait_ge(s["small_in"], 16 * SMALL)

            def keys_values(j):
                for kind, bk_, dst, psem, done, bcol in (("k", 0, kbd, "k_p", "k_sb", 1), ("v", 1, vbd, "v_p", "v_sb", 2)):
                    ac.wait_ge(s[psem], j + 1)
                    if j >= 2:
                        if kind == "k":
                            ac.wait_ge(s["c2_p"], j - 1)
                        else:
                            ac.wait_ge(s["vw_p"], 2 * (j - 1))
                    for h in range(2):
                        r = slice(DH * h, DH * h + DH)
                        last = act(dst[j % 2][r, :].rearrange("p (b n) -> p b n", b=NB)[:, :, S * h:S * h + S],
                                   bank[bk_][r, 0:256].rearrange("p (b n) -> p b n", b=NB),
                                   ACT.Identity, bias=bcols[r, bcol, j:j + 1])
                    last.then_inc(s[done], 1)

            keys_values(0)
            for j in range(PAIRS):
                if j + 1 < PAIRS:
                    keys_values(j + 1)
                for i in range(4):
                    ac.wait_ge(s["a_p" if i < DC else "vw_p"], DC * j + i % DC + 1)
                    if j >= DEEP:
                        ac.wait_ge(s[f"st_out{i}{j % DEEP}"], 16 * (j // DEEP))
                    bk_, sc = (bank[2 + i], DH ** -0.5) if i < DC else (bank[3 + i], 1.0)
                    act(st_r[i][j % DEEP], bk_, ACT.Copy, scale=sc).then_inc(s["st_sb"], 1)
                if j == 1:
                    ac.wait_ge(s["ut_p"], 1)
                    act(UT, bank[4].rearrange("p (c n) -> p c n", c=DC), ACT.Copy).then_inc(s["ut_sb"], 1)
                    ac.wait_ge(s["c_p"], 1)
                    act(C, bank[4][0:S, 0:D], ACT.Copy).then_inc(s["c_sb"], 1)
            ac.wait_ge(s["c2_p"], PAIRS)
            act(c_col, bank[7][:, 0:PAIRS * NB], ACT.Copy, scale=DH ** -0.5).then_inc(s["c2_c"], 1)
            ac.wait_ge(s["c2_t"], 1)
            act(c_r, bank[4][0:PAIRS * NB, 0:P], ACT.Copy)
            act(c_h, bank[4][0:PAIRS * NB, 0:P], ACT.Copy)
            ac.drain()
            ac.sem_inc(s["c2_h"], 1)
            meet()

            def layer0():
                ac.wait_ge(s["rest_in"], 16 * REST)
                act(roh[:, :, :], roT[0][:, :, :], ACT.Copy).then_inc(s["l_xh"], 1)
                for q in range(QUADS + 1):
                    if q < QUADS:
                        ac.wait_ge(s["l_tp"], q + 1)
                        for c in range(DC):
                            act(xh[:, q, c, :], bank[2 * (q % 2) + c], ACT.Copy).then_inc(s["l_xh"], 1)
                    if q:
                        ac.wait_ge(s["l_lg"], q)
                        if q >= 3:
                            ac.wait_ge(s["l_lgt"], q - 2)
                        act(hsl[(q - 1) % 2][0:E, :], bank[6 + (q - 1) % 2][0:E, :], ACT.Copy).then_inc(s["l_lt"], 1)
                ac.wait_ge(s["l0_in"], 16 * 10)
                act(b2h[:, :], b2_raw[:, :], ACT.Copy).then_inc(s["l_b2h"], 1)
                table(0, ACT.Ln)
                ac.wait_ge(s["spa"], 1)
                act(wk2[:, :, :], wk1[:, :, :], ACT.Exp)
                ac.drain()
                act(wk2[:, :, :], wk2[:, :, :], ACT.Ln, bias=1.0).then_inc(s["spd"], 1)
                table(1, ACT.Silu)
                ac.wait_ge(s["l_w"], 2)
                for q in range(QUADS // 2):
                    ac.wait_ge(s["l_cft"], q + 1)
                    act(cfT[:, q, :], bank[q][0:2 * E9, :], ACT.Copy)
                ac.drain()
                ac.sem_inc(s["l_cfa"], 1)

                def quad(q, v, early):
                    if not early:
                        ac.wait_ge(s["l_y"], q * E9 - E9)
                    act(cfq[v][:, :], cfT[:, bass.ds(q, 1), :].rearrange("p a n -> p (a n)"), ACT.Copy).then_inc(s["l_cfq"], 1)

                def unit(n, u, e, early):
                    ac.wait_ge(s["l_h"], n + 1)
                    if not early:
                        ac.wait_ge(s["l_hg"], n - 1)
                    act(hsl[u % 2][:, :], bank[3 + u % 2], ACT.Silu, bias=b1c[:, e:e + 1]).then_inc(s["l_hs"], 1)
                    ac.wait_ge(s["l_hg"], n + 1)
                    if not early:
                        ac.wait_ge(s["l_y"], n - 1)
                    act(hh[u % 2][:, :], hg[u % 2][:, :], ACT.Copy).then_inc(s["l_hh"], 1)

                def pair(h, first, last):
                    for u in range(2 * E9):
                        unit(h * (2 * E9) + u, u, u % E9, first and u < 2)
                        if u == 4:
                            quad(h * 2 + 1, 1, first)
                        if u == E9 + 4 and not last:
                            quad(h * 2 + 2, 0, False)

                ac.wait_ge(s["l_cfd"], 1)
                quad(0, 0, True)
                pair(0, True, False)
                with ac.Fori(1, QUADS // 2 - 1) as h_:
                    pair(h_, False, False)
                pair(QUADS // 2 - 1, False, True)

            def router(g):
                def high(i):
                    c, e = i // 2, E // 2 * (i % 2)
                    ac.wait_ge(s[f"w_in{i}"], 16)
                    act(w13h[:, c, e:e + E // 2, :], w13l[:, c, e:e + E // 2, :].bitcast(F32), ACT.Copy).then_inc(s["w_hi"], 1)

                if g == GROUPS - 1:
                    ac.wait_ge(s["a_xu"], TILES)
                    high(0)
                def logits(k):
                    ac.wait_ge(s["ro_p"], k + 1)
                    if k >= 2:
                        ac.wait_ge(s["ro_t"], k - 1)
                    act(lgT[k % 2], bank[5 + 2 * (k % 2)][0:E, :], ACT.Copy).then_inc(s["ro_sb"], 1)

                for k in range(G0[g] // QT, (G0[g] + GT[g]) // QT):
                    ac.wait_ge(s["t_p"], k + 1)
                    if k >= 2:
                        ac.wait_ge(s["ro_p"], k - 1)
                    act(xnT4[k % 2][:, 0, :], bank[2 * (k % 2)], ACT.Copy).then_inc(s["xt_a"], 1)
                    if k > G0[g] // QT:
                        logits(k - 1)
                logits((G0[g] + GT[g]) // QT - 1)
                if g == 0:
                    attention(1, rest=False)
                if g == GROUPS - 1:
                    ac.wait_ge(s["sc1"], 16 * GT[0])
                    ac.wait_ge(s["sc2"], 16 * GT[0])
                    high(1)
                    high(2)
                ac.wait_ge(s["spa"], g + 2)
                w = wt[1][:, G0[g]:G0[g] + GT[g]]
                act(w, w, ACT.Exp).then_inc(s["spd"], 1)
                if g == GROUPS - 1:
                    high(3)
                    table(3, ACT.Silu)

            def experts():
                def xcopy(j, b, b4, early=False, fresh=False):
                    ac.wait_ge(s["e_tp"], j + 1)
                    if not early:
                        ac.wait_ge(s["e_g"], j - 1)
                    if not fresh:
                        ac.wait_ge(s["e_ys"], j - 3)
                    act(wcol[:, b4:b4 + 1], xs[b4][:, D:D + 1], ACT.Copy)
                    act(xTh[b][:, :, :], bank[0][:, 0:D].rearrange("p (c n) -> p c n", c=DC), ACT.Copy).then_inc(s["e_xt"], 1)

                def silu(j, b, early=False):
                    ac.wait_ge(s["e_h"], j + 1)
                    if not early:
                        ac.wait_ge(s["e_htp"], j - 1)
                    act(hs[b], bank[2 + b][:, 0:H1], ACT.Silu).then_inc(s["e_hs"], 1)

                def scale(j, b, b4, early=False):
                    ac.wait_ge(s["e_y"], j + 1)
                    if not early:
                        ac.wait_ge(s[f"e_st{b}"], (j - b) * 8)
                    act(ys[b], bank[1][:, 0:D], ACT.Copy, scale=wcol[:, b4:b4 + 1]).then_inc(s["e_ys"], 1)

                xcopy(0, 0, 0, True, True)
                silu(0, 0, True)
                xcopy(1, 1, 1, True, True)
                silu(1, 1, True)
                xcopy(2, 0, 2, False, True)
                silu(2, 0)
                xcopy(3, 1, 3, False, True)
                scale(0, 0, 0, True)
                silu(3, 1)
                xcopy(4, 0, 0)
                scale(1, 1, 1, True)
                loops = (SA - 5) // 4
                with ac.Fori(0, loops) as h_:
                    i = h_ * 4
                    for r in range(4):
                        silu(i + (r + 4), r % 2)
                        xcopy(i + (r + 5), 1 - r % 2, (r + 1) % 4)
                        scale(i + (r + 2), r % 2, (r + 2) % 4)
                for j in range(4 * loops + 4, SA):
                    silu(j, j % 2)
                    if j + 1 < SA:
                        xcopy(j + 1, 1 - j % 2, (j + 1) % 4)
                    scale(j - 2, j % 2, (j - 2) % 4)
                scale(SA - 2, 0, 2)
                scale(SA - 1, 1, 3)

            def attention(g, begin=True, rest=True):
                def xhigh(n, b, early):
                    ac.wait_ge(s["a_tp"], n + 1)
                    if not early:
                        ac.wait_ge(s["a_lg"], n - 1)
                    act(xah[b][:, :, :], bank[6][:, 0:D].rearrange("p (c n) -> p c n", c=DC), ACT.Copy).then_inc(s["a_xh"], 1)

                def expo(n, b):
                    ac.wait_ge(s["a_sub"], n + 1)
                    act(pr[b], pr[b], ACT.Exp).then_inc(s["a_ex"], 1)

                def phigh(n, first):
                    ac.wait_ge(s["a_ptp"], n + 1)
                    if not first:
                        ac.wait_ge(s["a_o"], n)
                    for h in range(2):
                        act(prh[:, 512 * h:512 * h + 512], bank[4 + h], ACT.Copy).then_inc(s["a_ph"], 1)

                def split_high(k, m, v):
                    raw, high = ((araw, Ah), (vraw, Vh))[v]
                    act(pieces(high, k)[:, bass.ds(m, 1), :], raw[:, bass.ds(m, 1), :], ACT.Copy).then_inc(s["av_h"], 1)

                n0, n1 = G0[g], G0[g] + GT[g]
                if begin and g:
                    xhigh(n0, 0, False)
                    xhigh(n0 + 1, 1, False)
                if not rest:
                    return
                if g == 0:
                    table(2, ACT.Exp)
                    ac.wait_ge(s["a_in"], 16)
                    for m in range(4):
                        split_high(0, m, 0)
                if g == 0:
                    xhigh(n0, 0, True)
                    ac.wait_ge(s["v_in"], 16)
                    for m in range(4):
                        split_high(0, m, 1)

                def step(n, r, at, first, split=None):
                    if at >= 2:
                        phigh(n + (r - 2), first)
                    if split:
                        split_high(*split, 0)
                    if at < GT[g] - 1 and not (g and at == 0):
                        xhigh(n + (r + 1), 1 - r, first and at == 0)
                    if split:
                        split_high(*split, 1)
                    expo(n + r, r)

                for b_ in BATCHES[g]:
                    t0 = b_ * BT
                    for r in range(2):
                        step(t0, r, t0 + r - n0, b_ == 0 and r == 0)
                    if g == 0:
                        ac.wait_ge(s["a_in"], 16 * (b_ + 2))
                        ac.wait_ge(s["v_in"], 16 * (b_ + 2))

                    def two(h, first):
                        for r in range(2):
                            step(h * 2 + (t0 + 2), r, 2, first and r == 0, None if g else (1 - b_ % 2, h * 2 + r))

                    if b_ == 0:
                        two(0, True)
                        two(1, False)
                    else:
                        with ac.Fori(0, 2) as h_:
                            two(h_, False)
                    for r in range(2):
                        step(t0 + 6, r, t0 + 6 + r - n0, False)
                for n in range(n1, n1 + 2):
                    phigh(n - 2, False)

            layer0()
            meet()
            attention(0)
            router(0)
            attention(1, begin=False)
            router(1)
            meet()
            experts()

        @block.vector
        def _(ve):
            meet = Marks(ve, "bar_dve").meet
            tt, ts, stt = nc.vector.tensor_tensor, nc.vector.tensor_scalar, nc.vector.scalar_tensor_tensor

            def bc(v, n):
                return v.rearrange("p (a b) -> p a b", b=1).to_broadcast([P, v.shape[1], n])

            def rep(v, n):
                return v.rearrange("p (b a) -> p b a", b=1).to_broadcast([P, n, v.shape[1]])

            def rsqrt(o, v, tmp):
                ts(o.bitcast(I32), v.bitcast(I32), 1, None, ALU.logical_shift_right)
                ve.drain()
                ts(o.bitcast(I32), o.bitcast(I32), -1.0, MAGIC, ALU.mult, ALU.add)
                ve.drain()
                for _ in range(3):
                    stt(tmp, o, -0.5, v, ALU.mult, ALU.mult)
                    ve.drain()
                    tt(tmp, tmp, o, ALU.mult)
                    ve.drain()
                    stt(o, tmp, 1.5, o, ALU.add, ALU.mult)
                    ve.drain()

            def ln_finish(st_, w0, w1):
                w = w1 - w0
                a, b, c = ta[:, 0:w], tb[:, 0:w], tc_[:, 0:w]
                m, r = mean[:, w0:w1], rstd[:, w0:w1]

                def col(k):
                    return st_[:, w0:w1, k:k + 1].rearrange("p t a -> p (t a)")

                ve.drain()
                tt(a, col(1), col(4), ALU.add)
                tt(b, col(1), col(4), ALU.subtract)
                tt(c, col(2), col(5), ALU.add)
                ve.drain()
                ts(m, a, 0.5, None, ALU.mult)
                tt(b, b, b, ALU.mult)
                ts(c, c, 1.0 / D, EPS, ALU.mult, ALU.add)
                ve.drain()
                stt(c, b, 0.25, c, ALU.mult, ALU.add)
                ve.drain()
                rsqrt(r, c, a)

            def row_stats(st_, buf, t0, t1):
                with ve.Fori(t0 // 4, t1 // 4) as h_:
                    i = h_ * 4
                    for u in range(4):
                        nc.vector.bn_stats(st_[:, bass.ds(i + u, 1), :].rearrange("p a n -> p (a n)"),
                                           buf[:, bass.ds(i + u, 1), :].rearrange("p a n -> p (a n)"))

            ve.wait_ge(s["u_in"], 16 * NB)
            for q in range(2):
                nc.vector.bn_stats(stats[:, q, :], U[:, q, :])
            ln_finish(stats, 0, 2)
            for q in range(2):
                last = ts(U[:, q, :], U[:, q, :], mean[:, q:q + 1], rstd[:, q:q + 1], ALU.subtract, ALU.mult)
            last.then_inc(s["u_norm"], 1)

            for b in range(NB):
                t0, t1 = b * BT, b * BT + BT
                ve.wait_ge(s[f"s_in{b}"], 16 * 4)
                row_stats(stats, N0, t0, t1)
                ln_finish(stats, t0, t1)
                for t in range(t0, t1):
                    r = S if t == t1 - 1 else P
                    v = N0[0:r, t, :]
                    last = ts(v, v, mean[0:r, t:t + 1], rstd[0:r, t:t + 1], ALU.subtract, ALU.mult)
                last.then_inc(s["s_norm"], 1)
            ve.wait_ge(s[f"c_put{NB - 1}"], 16)
            ve.wait_ge(s[f"x_in{NB - 1}"], 16)
            v = X[:, TILES - BT:, :]
            tt(v, v, N0[:, TILES - BT:, :], ALU.add)
            ve.drain()
            row_stats(xstats, X, TILES - BT, TILES)
            for b in range(NB - 1):
                ve.wait_ge(s["x_sum"], b + 1)
                row_stats(xstats, X, b * BT, b * BT + BT)
            ln_finish(xstats, 0, TILES)
            meet()

            def first_max(src, m, oh, tiles):
                h = hot[:, 0:tiles]
                nc.vector.tensor_reduce(m, src, AX.X, ALU.max)
                ve.drain()
                tt(oh, src, bc(m, E), ALU.is_equal)
                ve.drain()
                tt(oh, oh, rep(prio[:, :], tiles), ALU.mult)
                ve.drain()
                nc.vector.tensor_reduce(h, oh, AX.X, ALU.max)
                ve.drain()
                tt(oh, oh, bc(h, E), ALU.is_equal)
                ve.drain()

            def top2(tiles, between=None, after=None):
                def fl(v):
                    return v[:, 0:tiles, :].rearrange("p t e -> p (t e)")
                first_max(L[:, 0:tiles, :], m1[:, 0:tiles], oh1[:, 0:tiles, :], tiles)
                if between:
                    between()
                stt(fl(wk1), fl(oh1), -3.0e38, fl(L), ALU.mult, ALU.add)
                ve.drain()
                first_max(wk1[:, 0:tiles, :], m2[:, 0:tiles], oh2[:, 0:tiles, :], tiles)
                if after:
                    after()

            def layer0():
                def rows_in(q):
                    if q >= 2:
                        ve.wait_ge(s["l_tp"], q - 1)
                    for t in range(QT):
                        u = QT * q + t
                        last = ts(xnq[q % 2][:, t, :], X[:, u, :], mean[:, u:u + 1], rstd[:, u:u + 1], ALU.subtract, ALU.mult)
                    last.then_inc(s["l_xn"], 1)

                rows_in(0)
                ve.wait_ge(s["l_xh"], 1)
                tt(rol[:, :, :], roT[0][:, :, :], roh[:, :, :].bitcast(F32), ALU.subtract).then_inc(s["l_ro"], 1)
                for q in range(QUADS):
                    if q + 1 < QUADS:
                        rows_in(q + 1)
                    for c in range(DC):
                        ve.wait_ge(s["l_xh"], DC * q + c + 2)
                        last = tt(xl[:, q, c, :], bank[2 * (q % 2) + c], xh[:, q, c, :].bitcast(F32), ALU.subtract)
                    last.then_inc(s["l_xl"], 1)
                k2 = 2 * E9

                def plane(o):
                    return ident[0:k2, o:o + E9].rearrange("p (e a) -> p e a", a=1).to_broadcast([k2, E9, P])
                tt(sel[:, :, :], plane(0), plane(E9), ALU.add).then_inc(s["l_sel"], 1)
                ve.wait_ge(s["l_b2h"], 1)
                tt(b2l[:, :], b2_raw[:, :], b2h[:, :].bitcast(F32), ALU.subtract).then_inc(s["l_b2"], 1)
                ve.wait_ge(s["l_lgt"], QUADS)
                tt(L[:, :, :], bank[5][:, 0:TILES * E].rearrange("p (t e) -> p t e", e=E), rep(rb_bc[:, :], TILES), ALU.add)
                ve.drain()
                flat = "p t e -> p (t e)"
                Lv = L[:, :, :]
                ts(wk1[:, :, :], Lv, -1.0, None, ALU.mult)
                ve.drain()
                tt(wk1[:, :, :], wk1[:, :, :], Lv, ALU.min).then_inc(s["spa"], 1)
                ve.wait_ge(s["spd"], 1)
                ve.drain()
                stt(wk1[:, :, :].rearrange(flat), Lv.rearrange(flat), 0.0, wk2[:, :, :].rearrange(flat), ALU.max, ALU.add)
                ve.drain()
                rsqrt(wk2[:, :, :].rearrange(flat), wk1[:, :, :].rearrange(flat), ta[:, :])
                tt(Lv, wk1[:, :, :], wk2[:, :, :], ALU.mult)
                ve.drain()
                top2(TILES)
                tt(wk1[:, :, :], oh1[:, :, :], oh2[:, :, :], ALU.add)
                nc.vector.memset(cf[:, :, E:E9].bitcast(F32), 1.0)
                nc.vector.memset(cf[:, :, E9 + E:].bitcast(F32), 0.0)
                ve.drain()
                tt(wk1[:, :, :], wk1[:, :, :], Lv, ALU.mult)
                ve.drain()
                nc.vector.tensor_copy(cf[:, :, 0:E], wk1[:, :, :])
                ve.drain()
                tt(cf[:, :, E9:E9 + E], wk1[:, :, :], cf[:, :, 0:E].bitcast(F32), ALU.subtract)
                ve.drain()
                ve.sem_inc(s["l_cf"], 1)
                ve.wait_ge(s["l_w"], 2)
                for q in range(QUADS // 2, QUADS):
                    ve.wait_ge(s["l_cft"], q + 1)
                    nc.vector.tensor_copy(cfT[:, q, :], bank[q][0:2 * E9, :])
                ve.drain()
                ve.sem_inc(s["l_cfd"], 1)

                def unit(n, u, early):
                    ve.wait_ge(s["l_bc"], n + 1)
                    ve.wait_ge(s["l_hs"], n + 1)
                    if not early:
                        ve.wait_ge(s["l_hl"], n - 1)
                        ve.wait_ge(s["l_hh"], n - 1)
                    tt(hg[u % 2][:, :], bank[u % 2], hsl[u % 2][:, :], ALU.mult).then_inc(s["l_hg"], 1)
                    ve.wait_ge(s["l_hh"], n + 1)
                    if not early:
                        ve.wait_ge(s["l_y"], n - 1)
                    tt(hl[u % 2][:, :], hg[u % 2][:, :], hh[u % 2][:, :].bitcast(F32), ALU.subtract).then_inc(s["l_hl"], 1)

                def add(n, q, v):
                    ve.wait_ge(s["l_y"], n + 1)
                    for h in range(2):
                        x2 = X[:, bass.ds(q * QT + 2 * h, 2), :].rearrange("p t n -> p (t n)")
                        last = tt(x2, bank[(6, 7, 2, 5)[2 * v + h]], x2, ALU.add)
                    last.then_inc(s["l_xu"], 1)
                    ve.drain()
                    for t in range(QT):
                        nc.vector.bn_stats(xstats[:, bass.ds(q * QT + t, 1), :].rearrange("p a n -> p (a n)"),
                                           X[:, bass.ds(q * QT + t, 1), :].rearrange("p a n -> p (a n)"))

                def pair(h, first):
                    for u in range(2 * E9):
                        n = h * (2 * E9) + u
                        unit(n, u, first and u < 2)
                        if u % E9 == 1 and not (first and u < E9):
                            add(n + (-2), h * 2 + (u // E9 - 1), 1 - u // E9)

                pair(0, True)
                with ve.Fori(1, QUADS // 2) as h_:
                    pair(h_, False)
                ln_finish(xstats, 0, TILES - QT)
                add(UNITS - 1, QUADS - 1, 1)

            def router(g):
                t0, n, k0 = G0[g], GT[g], G0[g] // QT
                quads, cols = n // QT, E * n
                ln_finish(xstats, t0, TILES)
                if g == 0:
                    ve.wait_ge(s["consts"], 3)

                def rows_in(k):
                    for t in range(QT * k, QT * k + QT):
                        last = ts(N[g][:, t - t0, 0:D], X[:, t, :], mean[:, t:t + 1], rstd[:, t:t + 1], ALU.subtract, ALU.mult)
                    last.then_inc(s["n_r"], 1)

                rows_in(k0)
                for k in range(k0, k0 + quads):
                    if k + 1 < k0 + quads:
                        rows_in(k + 1)
                    ve.wait_ge(s["t_p"], k + 1)
                    if k >= 2:
                        ve.wait_ge(s["ro_p"], k - 1)
                    nc.vector.tensor_copy(xnT4[k % 2][:, 1, :], bank[2 * (k % 2) + 1]).then_inc(s["xt_d"], 1)
                ve.wait_ge(s["ro_t"], k0 + quads)
                nc.vector.tensor_copy(L[:, 0:n, :].rearrange("p t e -> p (t e)"), bank[4][:, 0:cols])
                ve.drain()
                if g == 0:
                    rows, low = attention(1, rest=False)
                    rows()
                    top2(n, lambda: low(0), lambda: low(1))
                else:
                    top2(n)
                M3 = M[:, 0:cols].rearrange("p (e t) -> p t e", e=E)
                tt(M3, oh1[:, 0:n, :], oh2[:, 0:n, :], ALU.add).then_inc(s["r_m"], 1)
                w0, w1_ = wt[0][:, t0:t0 + n], wt[1][:, t0:t0 + n]
                tt(w1_, m2[:, 0:n], m1[:, 0:n], ALU.subtract).then_inc(s["spa"], 1)
                ve.wait_ge(s["spd"], g + 2)
                ts(w0, w1_, 1.0, None, ALU.add)
                ve.drain()
                nc.vector.reciprocal(w0, w0)
                ve.drain()
                tt(w1_, w1_, w0, ALU.mult)
                ve.drain()
                nc.vector.tensor_copy(N[g][:, :, D:D + 1], w0.rearrange("p (t a) -> p t a", a=1))
                ve.wait_ge(s["r_pt"], g + 1)
                e3 = "p (e t) -> p e t"
                ta_, tb_, tot_, inc_ = ta[:, 0:cols], tb[:, 0:cols], tot[:, 0:cols], inc[:, 0:cols]
                nc.vector.tensor_copy(tot_, bank[5][:, 0:cols])
                ve.drain()
                nc.vector.tensor_tensor_scan(inc_, segm[:, g, 0:cols], tot_, 0.0, ALU.mult, ALU.add)
                ve.drain()
                last_t = inc_.rearrange(e3, e=E)[:, :, n - 1:n]
                tt(ta_.rearrange(e3, e=E), last_t.to_broadcast([P, E, n]), rep(thr[:, 0:n], E), ALU.is_gt)
                tt(tb_, inc_, tot_, ALU.subtract)
                ve.drain()
                nc.vector.tensor_reduce(te[:, :], ta_.rearrange(e3, e=E), AX.X, ALU.add)
                tt(tb_, bank[4][:, 0:cols], tb_, ALU.add)
                ve.drain()
                nc.vector.tensor_tensor_scan(ti[:, :], ones8[:, :], te[:, :], 0.0, ALU.mult, ALU.add)
                ve.drain()
                tt(te[:, :], ti[:, :], te[:, :], ALU.subtract)
                cm = cmp[:, 0:SLOTS[g] * E].rearrange("p (j e) -> p j e", e=E)
                tt(cm, bc(slotno[:, 0:SLOTS[g]], E), rep(ti[:, :], SLOTS[g]), ALU.is_ge)
                ve.drain()
                tb3 = tb_.rearrange(e3, e=E)
                stt(tb3, bc(te[:, :], n), float(P), tb3, ALU.mult, ALU.add)
                nc.vector.tensor_reduce(eid_f[:, 0:SLOTS[g]], cm, AX.X, ALU.add)
                ve.drain()
                ts(eid[:, SLOT0[g]:SLOT0[g] + SLOTS[g]], eid_f[:, 0:SLOTS[g]], float(E - 1), None, ALU.min)
                for k, oh in enumerate((oh1, oh2)):
                    tt(wk1[:, 0:n, :], oh[:, 0:n, :], tb3.rearrange("p e t -> p t e"), ALU.mult)
                    ve.drain()
                    nc.vector.tensor_reduce(hot[:, 0:n], wk1[:, 0:n, :], AX.X, ALU.add)
                    ve.drain()
                    nc.vector.tensor_copy(slot[k][:, t0:t0 + n], hot[:, 0:n])
                ve.drain()
                ve.sem_inc(s["rout"], 1)
                if g == GROUPS - 1:
                    ve.wait_ge(s["w_hi"], 4)
                    low, high = (v[:, 1, E // 2:E, :] for v in (w13l, w13h))
                    tt(low, low.bitcast(F32), high.bitcast(F32), ALU.subtract).then_inc(s["w_lod"], 1)

            def experts():
                def gate(j, b):
                    ve.wait_ge(s["e_hs"], j + 1)
                    ve.wait_ge(s["e_g"], j + 1)
                    tt(hs[b], bank[4 + b][:, 0:H1], hs[b], ALU.mult).then_inc(s["e_hg"], 1)

                def hcopy(j, b, early=False):
                    ve.wait_ge(s["e_htp"], j + 1)
                    if not early:
                        ve.wait_ge(s["e_y"], j - 1)
                    nc.vector.tensor_copy(hT[b].rearrange("p c n -> p (c n)"), bank[6 + b][:, 0:H1]).then_inc(s["e_ht"], 1)

                def xlow(j, b, early=False):
                    ve.wait_ge(s["e_xt"], j + 1)
                    if not early:
                        ve.wait_ge(s["e_g"], j - 1)
                    tt(xTl[b][:, :, :], bank[0][:, 0:D].rearrange("p (c n) -> p c n", c=DC), xTh[b][:, :, :].bitcast(F32),
                       ALU.subtract).then_inc(s["e_xl"], 1)

                xlow(0, 0, True)
                xlow(1, 1, True)
                gate(0, 0)
                gate(1, 1)
                hcopy(0, 0, True)
                xlow(2, 0)
                gate(2, 0)
                hcopy(1, 1, True)
                xlow(3, 1)
                gate(3, 1)
                hcopy(2, 0)
                xlow(4, 0)
                with ve.Fori(2, SA // 2 - 1) as h_:
                    i = h_ * 2
                    for b in range(2):
                        gate(i + b, b)
                        hcopy(i + (b - 1), 1 - b)
                        xlow(i + (b + 1), 1 - b)
                gate(SA - 2, 0)
                hcopy(SA - 3, 1)
                xlow(SA - 1, 1)
                gate(SA - 1, 1)
                hcopy(SA - 2, 0)
                hcopy(SA - 1, 1)

            def attention(g, begin=True, rest=True):
                def row(v, n):
                    return v[:, bass.ds(n, 1), :].rearrange("p a n -> p (a n)")

                def rows_in(n, b, early):
                    if not early:
                        ve.wait_ge(s["a_tp"], n - 1)
                    ts(xn_a[b], row(X, n), mean[:, bass.ds(n, 1)], rstd[:, bass.ds(n, 1)], ALU.subtract, ALU.mult).then_inc(s["a_xn"], 1)

                def xlow(n, b, early):
                    ve.wait_ge(s["a_xh"], n + 1)
                    if not early:
                        ve.wait_ge(s["a_lg"], n - 1)
                    tt(xal[b][:, :, :], bank[6][:, 0:D].rearrange("p (c n) -> p c n", c=DC), xah[b][:, :, :].bitcast(F32),
                       ALU.subtract).then_inc(s["a_xl"], 1)

                def shift(n, b, early):
                    ve.wait_ge(s["a_lg"], n + 1)
                    if not early:
                        ve.wait_ge(s["a_ptp"], n - 1)
                    lg = psum[:, 2 * b:2 * b + 2, :].rearrange("p a (h n) -> p (a h) n", n=S)
                    nc.vector.tensor_reduce(mx[:, :], lg, AX.X, ALU.max)
                    ve.drain()
                    tt(pr[b].rearrange("p (h n) -> p h n", n=S), lg, bc(mx[:, :], S), ALU.subtract).then_inc(s["a_sub"], 1)

                def sums(n, b):
                    ve.wait_ge(s["a_ex"], n + 1)
                    nc.vector.tensor_reduce(sm[b][:, :], pr[b].rearrange("p (h n) -> p h n", n=S), AX.X, ALU.add)
                    ve.drain()
                    nc.vector.reciprocal(sm[b][:, :], sm[b][:, :]).then_inc(s["a_sm"], 1)

                def plow(n, first):
                    for h in range(2):
                        ve.wait_ge(s["a_ph"], n * 2 + (h + 1))
                        if h == 0 and not first:
                            ve.wait_ge(s["a_o"], n)
                        cols = slice(512 * h, 512 * h + 512)
                        last = tt(prl[:, cols], bank[4 + h], prh[:, cols].bitcast(F32), ALU.subtract)
                    last.then_inc(s["a_pl"], 1)

                def add(n):
                    ve.wait_ge(s["a_o"], n + 1)
                    tt(row(X, n), bank[7][:, 0:D], row(X, n), ALU.add).then_inc(s["a_xu"], 1)
                    ve.drain()
                    nc.vector.bn_stats(row(xstats, n), row(X, n))

                n0, n1 = G0[g], G0[g] + GT[g]
                e0 = 4 if n0 == 0 else 2
                def two_rows():
                    rows_in(n0, 0, n0 == 0)
                    rows_in(n0 + 1, 1, n0 == 0)

                if not rest:
                    return two_rows, lambda r: xlow(n0 + r, r, False)
                if g == 0:
                    ve.drain()
                    two_rows()
                    xlow(n0, 0, True)
                if g == 0:
                    for m in range(2, 4):
                        ve.wait_ge(s["av_h"], m + 1)
                        tt(pieces(Al, 0)[:, m, :], araw[:, m, :], pieces(Ah, 0)[:, m, :].bitcast(F32), ALU.subtract).then_inc(s["av_ld"], 1)
                for n in range(n0, n0 + e0):
                    if n - 2 >= n0:
                        plow(n - 2, n == 2)
                    if n > n0:
                        sums(n - 1, 1 - n % 2)
                    shift(n, n % 2, n < 2)
                    if not (g and n == n0):
                        xlow(n + 1, 1 - n % 2, n + 1 < 2)
                    rows_in(n + 2, n % 2, False)
                    if n - 2 >= n0:
                        add(n - 2)
                with ve.Fori((n0 + e0) // 2, n1 // 2 - 1) as h_:
                    n = h_ * 2
                    for r in range(2):
                        plow(n + (r - 2), False)
                        sums(n + (r - 1), 1 - r)
                        shift(n + r, r, False)
                        xlow(n + (r + 1), 1 - r, False)
                        rows_in(n + (r + 2), r, False)
                        add(n + (r - 2))
                for n in range(n1 - 2, n1 + 2):
                    plow(n - 2, False)
                    if n - 1 < n1:
                        sums(n - 1, 1 - n % 2)
                    if n < n1:
                        shift(n, n % 2, False)
                    if n + 1 < n1:
                        xlow(n + 1, 1 - n % 2, False)
                    add(n - 2)
                ve.drain()

            layer0()
            meet()
            attention(0)
            router(0)
            attention(1, begin=False)
            router(1)
            meet()
            experts()


_INS = ['x', 'ctx_1024', 'L0_xattn_conv_w', 'L0_xattn_conv_b', 'L0_ffn_routing_W', 'L0_ffn_expert_bias', 'L0_ffn_sW1',
        'L0_ffn_sb1', 'L0_ffn_sW2', 'L0_ffn_sb2', 'L0_ffn_rW1', 'L0_ffn_rb1', 'L0_ffn_rW2', 'L0_ffn_rb2',
        'L1_xattn_Wq', 'L1_xattn_bq', 'L1_xattn_Wk', 'L1_xattn_bk', 'L1_xattn_Wv', 'L1_xattn_bv', 'L1_xattn_Wo',
        'L1_xattn_bo', 'L1_ffn_Wr', 'L1_ffn_W1', 'L1_ffn_W2', 'L1_ffn_W3']


def kernel(**inputs):
    import numpy as _np
    import concourse.bacc as _bacc
    from concourse import mybir as _mybir
    from concourse.bass_utils import run_bass_kernel_spmd as _run

    nc = _bacc.Bacc("TRN2", target_bir_lowering=False, num_devices=1)
    arrays, args = {}, []
    for name in _INS:
        a = _np.ascontiguousarray(inputs[name])
        arrays[f"in_{name}_dram"] = a
        args.append(nc.dram_tensor(f"in_{name}_dram", a.shape, _mybir.dt.from_np(a.dtype), kind="ExternalInput").ap())
    args.append(nc.dram_tensor("out_0_dram", (NB, T, D), _mybir.dt.float32, kind="ExternalOutput").ap())
    build(nc, *args)
    r = _run(nc, [arrays], core_ids=[0])
    return r.results[0]["out_0_dram"]
```
